# Optimizing a Trainium2 kernel written in Bass

```python
import numpy as np
import jax
import jax.numpy as jnp

def _softmax(x, axis=-1):
    return jax.nn.softmax(x, axis=axis)

def _gelu(x):
    return jax.nn.gelu(x, approximate=True)

def _silu(x):
    return jax.nn.silu(x)

def _sigmoid(x):
    return jax.nn.sigmoid(x)

def _layernorm(x, axis=-1, eps=1e-05):
    m = jnp.mean(x, axis=axis, keepdims=True)
    v = jnp.var(x, axis=axis, keepdims=True)
    return (x - m) / jnp.sqrt(v + eps)

def _scatter_add(tgt, idx, src, axis=0):
    return tgt.at[idx].add(src)

def _segment_sum(src, seg, n):
    return jax.ops.segment_sum(src, seg, n)
kernel_name = 'mk_decoder_preln_d1_seqx_r2_c74272'

def setup_inputs(seed: int=0):
    np.random.seed(seed)
    _w = jnp.asarray

    def _rec_inputs():
        import jax
        import jax.numpy as jnp
        _rk = jax.random.key(seed)
        x = -0.0002928 + 1 * jax.random.normal(jax.random.fold_in(_rk, 1), (4, 1024, 512), jnp.float32)
        _lenS = 1024 - jax.random.randint(jax.random.fold_in(_rk, 7), (4,), 0, max(1, 1024 // 4) + 1, jnp.int32)
        _lenS2 = 1024 - jax.random.randint(jax.random.fold_in(_rk, 8), (4,), 0, max(1, 1024 // 4) + 1, jnp.int32)
        _ctx_1024P = jax.random.normal(jax.random.fold_in(_rk, 11), (4, 16, 512), jnp.float32)
        _ctx_1024c = jax.random.dirichlet(jax.random.fold_in(_rk, 511), 0.3 * jnp.ones((16,), jnp.float32), (4, 1024))
        _ctx_1024t = jnp.einsum('bsk,bkd->bsd', _ctx_1024c, _ctx_1024P)
        _ctx_1024t = _ctx_1024t * jax.lax.rsqrt(jnp.mean(jnp.square(_ctx_1024t)) + 1e-12) * 0.953939
        ctx_1024 = -1.39393e-06 + 0.999914 * (_ctx_1024t + 0.3 * jax.random.normal(jax.random.fold_in(_rk, 611), (4, 1024, 512), jnp.float32))
        _validS = jnp.arange(1024)[None, :] < _lenS[:, None]
        _validS2 = jnp.arange(1024)[None, :] < _lenS2[:, None]
        _causal = jnp.tril(jnp.ones((1024, 1024), dtype=bool))
        mask_BxS2_if1 = jnp.where(jnp.ones((4, 1024), dtype=bool), 1, 0).astype(jnp.int32)
        return (x, ctx_1024, mask_BxS2_if1)
    x, ctx_1024, mask_BxS2_if1 = _rec_inputs()

    def _L0_attn_setup():
        import jax, jax.numpy as jnp
        import numpy as np
        B, L, DIM = (4, 2048, 512)
        H, DQK, DV, DINNER, CHUNK = (16, 64, 64, 64, 64)
        BASE_LR, BASE_WD = (0.001, 0.9)
        key = jax.random.key(seed)
        ks = jax.random.split(key, 9)

        def s(k, shape, scale):
            return jax.random.normal(k, shape, jnp.float32) * scale
        return {'x': jax.random.normal(ks[0], (B, L, DIM), jnp.float32), 'Wq': s(ks[1], (H * DQK, DIM), DIM ** (-0.5)), 'Wk': s(ks[2], (H * DQK, DIM), DIM ** (-0.5)), 'Wv': s(ks[3], (H * DV, DIM), DIM ** (-0.5)), 'Wlr': s(ks[4], (2 * H, DIM), DIM ** (-0.5)), 'Wbeta': s(ks[5], (2 * H, DIM), DIM ** (-0.5)), 'Wo': s(ks[6], (DIM, H * DV), (H * DV) ** (-0.5)), 'W_in_init': s(ks[7], (1, DINNER, H, DQK), DQK ** (-0.5)), 'W_out_init': s(ks[8], (1, DINNER, H, DV), DINNER ** (-0.5))}
    _L0_attn_all = _L0_attn_setup()
    _L0_attn_in = {k: v for k, v in _L0_attn_all.items() if k in ('Wq', 'Wk', 'Wv', 'Wlr', 'Wbeta', 'Wo', 'W_in_init', 'W_out_init')}
    del _L0_attn_all

    def _L0_xattn_setup():
        import jax, jax.numpy as jnp
        import numpy as np
        D_MODEL = 512
        NUM_HEADS = 16
        D_K = D_MODEL // NUM_HEADS
        NEG_INF = -1000000000.0
        key = jax.random.key(seed)
        ks = jax.random.split(key, 12)
        B, S = (2, 1024)
        scale = 1.0 / np.sqrt(D_MODEL)
        inp = {'q': jax.random.normal(ks[0], (B, S, D_MODEL), jnp.float32), 'k': jax.random.normal(ks[1], (B, S, D_MODEL), jnp.float32), 'v': jax.random.normal(ks[2], (B, S, D_MODEL), jnp.float32), 'mask': jnp.ones((B, S), jnp.int32), 'W_q': jax.random.normal(ks[3], (D_MODEL, D_MODEL), jnp.float32) * scale, 'b_q': jnp.zeros((D_MODEL,), jnp.float32), 'W_k': jax.random.normal(ks[4], (D_MODEL, D_MODEL), jnp.float32) * scale, 'b_k': jnp.zeros((D_MODEL,), jnp.float32), 'W_v': jax.random.normal(ks[5], (D_MODEL, D_MODEL), jnp.float32) * scale, 'b_v': jnp.zeros((D_MODEL,), jnp.float32), 'W_o': jax.random.normal(ks[6], (D_MODEL, D_MODEL), jnp.float32) * scale, 'b_o': jnp.zeros((D_MODEL,), jnp.float32)}
        return inp
    _L0_xattn_all = _L0_xattn_setup()
    _L0_xattn_in = {k: v for k, v in _L0_xattn_all.items() if k in ('W_q', 'b_q', 'W_k', 'b_k', 'W_v', 'b_v', 'W_o', 'b_o')}
    del _L0_xattn_all

    def _L0_ffn_setup():
        import jax, jax.numpy as jnp
        import numpy as np
        B, S, H, F, E = (8, 1024, 512, 2048, 8)
        INIT_LAMBDA = 0.2
        key = jax.random.key(seed)
        ks = jax.random.split(key, 12)
        std = 0.02
        return {'hidden_states': jax.random.normal(ks[0], (B, S, H), jnp.float32), 'gate_w1': jax.random.normal(ks[1], (H, H), jnp.float32) * 0.01, 'gate_b1': jnp.zeros((H,), jnp.float32), 'gate_w2': jax.random.normal(ks[2], (E, H), jnp.float32) * 0.01, 'gate_b2': jnp.full((E,), INIT_LAMBDA, jnp.float32), 'W1': jax.random.normal(ks[3], (F, H), jnp.float32) * std, 'b1': jax.random.normal(ks[4], (F,), jnp.float32) * std, 'W2': jax.random.normal(ks[5], (H, F), jnp.float32) * std, 'b2': jax.random.normal(ks[6], (H,), jnp.float32) * std, 'TW1': jax.random.normal(ks[7], (E, F, H), jnp.float32) * std, 'Tb1': jax.random.normal(ks[8], (E, F), jnp.float32) * std, 'TW2': jax.random.normal(ks[9], (E, H, F), jnp.float32) * std, 'Tb2': jax.random.normal(ks[10], (E, H), jnp.float32) * std}
    _L0_ffn_all = _L0_ffn_setup()
    _L0_ffn_in = {k: v for k, v in _L0_ffn_all.items() if k in ('gate_w1', 'gate_b1', 'gate_w2', 'gate_b2', 'W1', 'b1', 'W2', 'b2', 'TW1', 'Tb1', 'TW2', 'Tb2')}
    del _L0_ffn_all
    return {'x': x, 'ctx_1024': ctx_1024, 'mask_BxS2_if1': mask_BxS2_if1, 'L0_attn_Wq': _L0_attn_in['Wq'], 'L0_attn_Wk': _L0_attn_in['Wk'], 'L0_attn_Wv': _L0_attn_in['Wv'], 'L0_attn_Wlr': _L0_attn_in['Wlr'], 'L0_attn_Wbeta': _L0_attn_in['Wbeta'], 'L0_attn_Wo': _L0_attn_in['Wo'], 'L0_attn_W_in_init': _L0_attn_in['W_in_init'], 'L0_attn_W_out_init': _L0_attn_in['W_out_init'], 'L0_xattn_W_q': _L0_xattn_in['W_q'], 'L0_xattn_b_q': _L0_xattn_in['b_q'], 'L0_xattn_W_k': _L0_xattn_in['W_k'], 'L0_xattn_b_k': _L0_xattn_in['b_k'], 'L0_xattn_W_v': _L0_xattn_in['W_v'], 'L0_xattn_b_v': _L0_xattn_in['b_v'], 'L0_xattn_W_o': _L0_xattn_in['W_o'], 'L0_xattn_b_o': _L0_xattn_in['b_o'], 'L0_ffn_gate_w1': _L0_ffn_in['gate_w1'], 'L0_ffn_gate_b1': _L0_ffn_in['gate_b1'], 'L0_ffn_gate_w2': _L0_ffn_in['gate_w2'], 'L0_ffn_gate_b2': _L0_ffn_in['gate_b2'], 'L0_ffn_W1': _L0_ffn_in['W1'], 'L0_ffn_b1': _L0_ffn_in['b1'], 'L0_ffn_W2': _L0_ffn_in['W2'], 'L0_ffn_b2': _L0_ffn_in['b2'], 'L0_ffn_TW1': _L0_ffn_in['TW1'], 'L0_ffn_Tb1': _L0_ffn_in['Tb1'], 'L0_ffn_TW2': _L0_ffn_in['TW2'], 'L0_ffn_Tb2': _L0_ffn_in['Tb2']}

def reference(x, ctx_1024, mask_BxS2_if1, L0_attn_Wq, L0_attn_Wk, L0_attn_Wv, L0_attn_Wlr, L0_attn_Wbeta, L0_attn_Wo, L0_attn_W_in_init, L0_attn_W_out_init, L0_xattn_W_q, L0_xattn_b_q, L0_xattn_W_k, L0_xattn_b_k, L0_xattn_W_v, L0_xattn_b_v, L0_xattn_W_o, L0_xattn_b_o, L0_ffn_gate_w1, L0_ffn_gate_b1, L0_ffn_gate_w2, L0_ffn_gate_b2, L0_ffn_W1, L0_ffn_b1, L0_ffn_W2, L0_ffn_b2, L0_ffn_TW1, L0_ffn_Tb1, L0_ffn_TW2, L0_ffn_Tb2):
    import jax
    import jax.numpy as jnp

    def _L0_attn_ref(x, Wq, Wk, Wv, Wlr, Wbeta, Wo, W_in_init, W_out_init):
        import jax, jax.numpy as jnp
        import numpy as np
        B, L, DIM = (4, 2048, 512)
        H, DQK, DV, DINNER, CHUNK = (16, 64, 64, 64, 64)
        BASE_LR, BASE_WD = (0.001, 0.9)
        b, l, _ = x.shape
        nc = l // CHUNK
        q = jax.nn.silu(x @ Wq.T).reshape(b, l, H, DQK)
        k = jax.nn.silu(x @ Wk.T).reshape(b, l, H, DQK)
        v = (x @ Wv.T).reshape(b, l, H, DV)
        lr = jax.nn.sigmoid(x @ Wlr.T) * BASE_LR
        wd = jax.nn.sigmoid(x @ Wbeta.T) * BASE_WD

        def chunked(t):
            return jnp.moveaxis(t.reshape(b, nc, CHUNK, *t.shape[2:]), 1, 0)
        qc, kc, vc = (chunked(q), chunked(k), chunked(v))
        lr_c = chunked(lr).mean(axis=2)
        wd_c = chunked(wd).mean(axis=2)
        lr_in, lr_out = (lr_c[..., :H], lr_c[..., H:])
        wd_in, wd_out = (wd_c[..., :H], wd_c[..., H:])
        W_in0 = jnp.broadcast_to(W_in_init, (b, DINNER, H, DQK))
        W_out0 = jnp.broadcast_to(W_out_init, (b, DINNER, H, DV))

        def step(carry, xs):
            W_in, W_out = carry
            qi, ki, vi, li, lo, wi, wo = xs
            p_q = jax.nn.softmax(jnp.einsum('bnhd,bDhd->bnhD', qi, W_in), axis=1)
            o = jnp.einsum('bnhD,bDhd->bnhd', p_q, W_out)
            p = jax.nn.softmax(jnp.einsum('bnhd,bDhd->bnhD', ki, W_in), axis=1)
            grad_out = jnp.einsum('bnhD,bnhd->bDhd', -p, vi)
            a = jnp.einsum('bDhd,bnhd->bnhD', W_out, vi)
            s = jnp.sum(p * a, axis=-1, keepdims=True)
            g_z = -(p * a - p * s)
            grad_in = jnp.einsum('bnhd,bnhD->bDhd', ki, g_z)
            W_in = wi[:, None, :, None] * W_in - li[:, None, :, None] * grad_in
            W_out = wo[:, None, :, None] * W_out - lo[:, None, :, None] * grad_out
            return ((W_in, W_out), o)
        _, outs = jax.lax.scan(step, (W_in0, W_out0), (qc, kc, vc, lr_in, lr_out, wd_in, wd_out))
        o = jnp.moveaxis(outs, 0, 1).reshape(b, l, H * DV)
        return o @ Wo.T

    def _L0_xattn_ref(q, k, v, mask, W_q, b_q, W_k, b_k, W_v, b_v, W_o, b_o):
        import jax, jax.numpy as jnp
        import numpy as np
        D_MODEL = 512
        NUM_HEADS = 16
        D_K = D_MODEL // NUM_HEADS
        NEG_INF = -1000000000.0
        B, S, _ = q.shape

        def proj(x, W, b):
            y = x @ W.T + b
            return y.reshape(B, -1, NUM_HEADS, D_K).transpose(0, 2, 1, 3)
        qh = proj(q, W_q, b_q)
        kh = proj(k, W_k, b_k)
        vh = proj(v, W_v, b_v)
        scores = jnp.einsum('bhqd,bhkd->bhqk', qh, kh) / jnp.sqrt(jnp.float32(D_K))
        m = mask[:, None, None, :]
        scores = jnp.where(m == 0, jnp.float32(NEG_INF), scores)
        attn = jax.nn.softmax(scores, axis=-1)
        context = jnp.einsum('bhqk,bhkd->bhqd', attn, vh)
        context = context.transpose(0, 2, 1, 3).reshape(B, S, D_MODEL)
        return context @ W_o.T + b_o

    def _L0_ffn_ref(hidden_states, gate_w1, gate_b1, gate_w2, gate_b2, W1, b1, W2, b2, TW1, Tb1, TW2, Tb2):
        import jax, jax.numpy as jnp
        import numpy as np
        B, S, H, F, E = (8, 1024, 512, 2048, 8)
        INIT_LAMBDA = 0.2
        x = hidden_states
        h = jax.nn.relu(jnp.einsum('bsh,oh->bso', x, gate_w1) + gate_b1)
        g = jnp.einsum('bso,eo->bse', h, gate_w2) + gate_b2
        g = g.mean(axis=1)
        mW1 = W1 + jnp.einsum('be,efh->bfh', g, TW1)
        mb1 = b1 + g @ Tb1
        mW2 = W2 + jnp.einsum('be,ehf->bhf', g, TW2)
        mb2 = b2 + g @ Tb2
        u = jax.nn.gelu(jnp.einsum('bsh,bfh->bsf', x, mW1) + mb1[:, None, :])
        out = jnp.einsum('bsf,bhf->bsh', u, mW2) + mb2[:, None, :]
        return out
    x = x + _L0_attn_ref(_layernorm(x, axis=-1), L0_attn_Wq, L0_attn_Wk, L0_attn_Wv, L0_attn_Wlr, L0_attn_Wbeta, L0_attn_Wo, L0_attn_W_in_init, L0_attn_W_out_init)
    x = x + _L0_xattn_ref(_layernorm(x, axis=-1), ctx_1024, ctx_1024, mask_BxS2_if1, L0_xattn_W_q, L0_xattn_b_q, L0_xattn_W_k, L0_xattn_b_k, L0_xattn_W_v, L0_xattn_b_v, L0_xattn_W_o, L0_xattn_b_o)
    x = x + _L0_ffn_ref(_layernorm(x, axis=-1), L0_ffn_gate_w1, L0_ffn_gate_b1, L0_ffn_gate_w2, L0_ffn_gate_b2, L0_ffn_W1, L0_ffn_b1, L0_ffn_W2, L0_ffn_b2, L0_ffn_TW1, L0_ffn_Tb1, L0_ffn_TW2, L0_ffn_Tb2)
    return x

_drawn_inputs = setup_inputs


def setup_inputs(seed=0):
    import zlib

    import numpy as np

    out = dict(_drawn_inputs(seed))
    spreads = {'L0_xattn_b_q': (0.0, 0.458),
     'L0_xattn_b_k': (0.0, 2.0),
     'L0_xattn_b_v': (0.0, 0.1),
     'L0_xattn_b_o': (0.0, 0.1),
     'L0_ffn_gate_b1': (0.0, 2.0),
     'L0_ffn_gate_b2': (0.20000000298023224, 0.6)}
    factors = {'L0_attn_Wq': 8.0,
     'L0_attn_Wk': 8.0,
     'L0_attn_Wv': 8.0,
     'L0_attn_Wlr': 8.0,
     'L0_attn_Wbeta': 8.0,
     'L0_attn_Wo': 8.0,
     'L0_attn_W_in_init': 8.0,
     'L0_attn_W_out_init': 8.0,
     'L0_ffn_gate_w1': 5.519,
     'L0_ffn_b1': 5.296,
     'L0_ffn_b2': 3.283,
     'L0_ffn_Tb1': 8.0,
     'L0_ffn_Tb2': 5.791}
    for name, (base, spread) in spreads.items():
        noise = np.random.default_rng([zlib.crc32(name.encode()), seed]).standard_normal(out[name].shape)
        drawn = base * np.exp(spread * noise) if base else spread * noise
        out[name] = jnp.asarray(drawn.astype(out[name].dtype))
    for name, factor in factors.items():
        out[name] = (out[name] * factor).astype(out[name].dtype)
    return out
```

```python
from contextlib import ExitStack

import concourse.bass as bass
from concourse import mybir

P = 128
F32 = mybir.dt.float32
F32R = mybir.dt.float32r
BF16 = mybir.dt.bfloat16
I32 = mybir.dt.int32
ALU = mybir.AluOpType
ACT = mybir.ActivationFunctionType
AX = mybir.AxisListType

EPS = 1e-5
BASE_LR = 0.001
BASE_WD = 0.9


def semaphores(nc, ex, prefix):
    held = []

    def sem(name):
        held.append(nc.alloc_semaphore(prefix + name))
        return held[-1]

    def give_back():
        nc.clear_and_free_semaphores(held)
        nc.all_engine_barrier()

    ex.callback(give_back)
    return sem


def scan_attention(nc, x, wq, wk, wv, wlb, wo, w0, x1):
    CH = 64
    NB, L, DIM = x.shape
    NCH = L // CH
    KT = DIM // P
    NJ = wq.shape[1] // P
    TOK = NB * CH
    NT = TOK // P
    H = 2 * NJ
    ex = ExitStack()
    with ex:
        sb = lambda name, shape, dt=F32: ex.enter_context(nc.sbuf_tensor(name, shape, dt))
        sem = semaphores(nc, ex, "")
        bank = [ex.enter_context(nc.psum_tensor(f"a_bank{i}", [P, 512], F32)) for i in range(8)]

        wq_s, wk_s, wv_s = (sb(n, [P, KT, NJ * P]) for n in ("a_wq", "a_wk", "a_wv"))
        wo_s = sb("a_wo", [P, NJ, DIM])
        wlb_s = sb("a_wlb", [P, KT, 4 * H])
        win_t, wout_t, wout = (sb(n, [P, NJ, NB, P]) for n in ("a_win_t", "a_wout_t", "a_wout"))
        winit = sb("a_winit", [P, 3, NJ, 64])
        ident = sb("a_ident", [P, P])
        meansel = sb("a_meansel", [P, 2, P])
        neghalf = sb("a_neghalf", [P, NT])
        xin, xn, xres = (sb(n, [P, NT, DIM]) for n in ("a_xin", "a_xn", "a_xres"))
        stats, mean, rstd = sb("a_stats", [P, NT, 6]), sb("a_mean", [P, NT]), sb("a_rstd", [P, NT])
        moments = sb("a_moments", [P, 5, NT])
        var_eps = sb("a_var_eps", [P, NT])
        xnt = sb("a_xnt", [P, KT, TOK])
        gates = sb("a_gates", [P, NT, 4 * H])
        coef_next, coef = (sb(n, [P, 4, NJ, NB]) for n in ("a_coef_next", "a_coef"))
        tanh_qk = sb("a_tanh_qk", [P, 2, 2, TOK])
        qk = sb("a_qk", [P, 2, 2, NB, CH])
        vt = sb("a_vt", [P, 4, TOK])
        kvtok = sb("a_kvtok", [P, 4, 2, NT, P])
        zs = sb("a_zs", [P, 2, 2 * NB, CH])
        ez, pr = (sb(n, [P, 2, 2, NB, CH]) for n in ("a_ez", "a_pr"))
        zmax, zsum, zinv = (sb(n, [P, 2, NB * 2]) for n in ("a_zmax", "a_zsum", "a_zinv"))
        pt = sb("a_pt", [P, 2, NT, 2, 64])
        pt_bd, gz_bd = (sb(n, [P, 2, NT, 2, 2, 64]) for n in ("a_pt_bd", "a_gz_bd"))
        pa, ps_ = (sb(n, [P, 2, NT, 2, 64]) for n in ("a_pa", "a_ps"))
        ssum = sb("a_ssum", [P, 2, NT * 2])
        decayed = sb("a_decayed", [P, 2, 2, NB, 64])
        step = sb("a_step", [P, 2, NB, 64])
        ot = sb("a_ot", [P, NJ, TOK])

        B_QK, B_VO, B_Z, B_KV, B_PT, B_A, B_G, B_X = range(8)
        ps_qk = bank[B_QK][:, :].rearrange("p (t n) -> p t n", t=2)
        ps_v, ps_o = bank[B_VO][:, 0:TOK], bank[B_VO][:, TOK:2 * TOK]
        ps_z = bank[B_Z][:, :].rearrange("p (b n) -> p b n", n=CH)
        ps_kv = bank[B_KV][:, :].rearrange("p (t u f) -> p t u f", t=2, u=NT)
        ps_wt = bank[B_KV][:, :].rearrange("p (b f) -> p b f", b=NB)
        ps_pt = bank[B_PT][:, 0:NT * P].rearrange("p (u g f) -> p u g f", u=NT, g=2)
        ps_a = bank[B_A][:, 0:NT * P].rearrange("p (u g f) -> p u g f", u=NT, g=2)
        ps_g = bank[B_G][:, :].rearrange("p (m b f) -> p m b f", m=2, b=NB)
        ps_x = bank[B_X]

        wlb_in, wq_in, wk_in, wv_in, wo_in = (sem(f"a_{n}_in") for n in ("wlb", "wq", "wk", "wv", "wo"))
        consts_set = sem("a_consts_set")
        states_clear, states_set = sem("a_states_clear"), sem("a_states_set")
        winit_in = sem("a_winit_in")
        x_in = sem("a_x_in")
        xres_in = sem("a_xres_in")
        x1_out = sem("a_x1_out")
        stats_set = sem("a_stats_set")
        ln_chain = sem("a_ln_chain")
        rstd_set = sem("a_rstd_set")
        xn_set = sem("a_xn_set")
        xt_mm, xt_evac = sem("a_xt_mm"), sem("a_xt_evac")
        gate_mm, gate_set = sem("a_gate_mm"), sem("a_gate_set")
        mean_mm, mean_evac = sem("a_mean_mm"), sem("a_mean_evac")
        y_mm, y_evac = sem("a_y_mm"), sem("a_y_evac")
        coef_set = sem("a_coef_set")
        qk_mm, v_mm, z_mm, kv_mm = sem("a_qk_mm"), sem("a_v_mm"), sem("a_z_mm"), sem("a_kv_mm")
        o_mm, a_mm, pt_mm, g_mm, wt_mm = (sem(f"a_{n}") for n in ("o_mm", "a_mm", "pt_mm", "g_mm", "wt_mm"))
        tanh_set, v_evac, kv_evac, e_set = (sem(f"a_{n}") for n in ("tanh_set", "v_evac", "kv_evac", "e_set"))
        pt_evac, o_evac, wt_evac = (sem(f"a_{n}") for n in ("pt_evac", "o_evac", "wt_evac"))
        qk_set, zmax_set, zs_set, zsum_set, zinv_set = (
            sem(f"a_{n}") for n in ("qk_set", "zmax_set", "zs_set", "zsum_set", "zinv_set"))
        pa_set, ssum_set = sem("a_pa_set"), sem("a_ssum_set")
        step_set = sem("a_step_set")
        w_set = sem("a_w_set")
        pr_set, ps_set, gz_set = (sem(f"a_{n}") for n in ("pr_set", "ps_set", "gz_set"))
        decayed_set = sem("a_decayed_set")

        block = ex.enter_context(nc.Block())
        halves = ((0, slice(0, 64)), (1, slice(64, 128)))

        def wait(eng, s, value):
            if not isinstance(value, int) or value > 0:
                eng.wait_ge(s, value)

        LEARNING = (NCH - 1) * NJ

        KV_SLOTS, TOKEN_KV_SLOTS = LEARNING + 3, LEARNING + 1

        def before(s, top):
            return not isinstance(s, int) or s < top

        def clip(value, top):
            return min(value, top) if isinstance(value, int) else value

        def over_slots(eng, slot):
            for j in range(NJ):
                slot(0, j)
            with eng.Fori(1, NCH - 1) as c:
                for j in range(NJ):
                    slot(c, j)
            for j in range(NJ):
                slot(NCH - 1, j)

        def exists(c, j):
            return not isinstance(c, int) or 0 <= c * NJ + j < NCH * NJ

        def learns(c, j):
            return not isinstance(c, int) or 0 <= c * NJ + j < LEARNING

        @block.sync
        def _(sp):

            def rows(of, c, b):
                return of[b, bass.ds(c * CH, CH), :]

            def load_xin(c):
                wait(sp, xn_set, c)
                for b in range(NB):
                    sp.dma_start(xin[64 * (b % 2):64 * (b % 2) + 64, b // 2, :], rows(x, c, b)).then_inc(x_in, 16)

            def residual(c):
                wait(sp, x1_out, 64 * c)
                for b in range(NB):
                    sp.dma_start(xres[64 * (b % 2):64 * (b % 2) + 64, b // 2, :], rows(x, c, b)
                                 ).then_inc(xres_in, 16)
                sp.wait_ge(y_evac, 2 * c + 2)
                for b in range(NB):
                    sp.dma_start(rows(x1, c, b), xres[64 * (b % 2):64 * (b % 2) + 64, b // 2, :]
                                 ).then_inc(x1_out, 16)

            load_xin(0)
            sp.dma_start(winit[:, :, :, :], w0.rearrange("m p j b -> p m j b")).then_inc(winit_in, 16)
            for s_, w, loaded in ((wlb_s, wlb, wlb_in), (wq_s, wq, wq_in), (wk_s, wk, wk_in), (wv_s, wv, wv_in),
                                  (wo_s, wo, wo_in)):
                sp.dma_start(s_[:, :, :], w.rearrange("(t p) n -> p t n", p=P)).then_inc(loaded, 16)
            load_xin(1)
            residual(0)
            with sp.Fori(2, NCH) as c:
                load_xin(c)
                residual(c - 1)
            residual(NCH - 1)
            sp.wait_ge(x1_out, 64 * NCH)

        @block.gpsimd
        def _(pool):
            def norm_scale(c):
                pool.wait_ge(ln_chain, 3 * c + 3)
                wait(pool, xn_set, c)
                pool.tensor_tensor(rstd[:, :], var_eps[:, :], neghalf[:, :], ALU.pow).then_inc(rstd_set, 1)

            def decay(c, s, jj, r):
                wait(pool, w_set, 4 * (s - 1))
                pool.wait_ge(states_set, 6)
                pool.wait_ge(coef_set, c + 1)
                wait(pool, pr_set, s + 1)
                for g, half in halves:
                    if g == 1:
                        pool.wait_ge(decayed_set, 4 * s + 2)
                    for m, w in ((0, win_t), (1, wout_t)):
                        pool.tensor_tensor(
                            decayed[half, r, m, :, :], w[half, jj, :, 64 * g:64 * g + 64],
                            coef[half, 2 + m, jj, :].unsqueeze(2).broadcast_to([64, NB, 64]),
                            ALU.mult).then_inc(decayed_set, 1)

            def score_gradient(s, r):
                pool.wait_ge(ssum_set, s + 1)
                wait(pool, gz_set, 2 * s)
                wait(pool, decayed_set, 4 * s)
                pool.tensor_tensor(ps_[:, r, :, :, :], pt[:, r, :, :, :],
                                   ssum[:, r, :].rearrange("p (u g) -> p u g", u=NT).unsqueeze(3)
                                   .broadcast_to([P, NT, 2, 64]), ALU.mult).then_inc(ps_set, 1)
                pool.wait_ge(ps_set, s + 1)
                wait(pool, g_mm, s - 1)
                for g, half in halves:
                    if g == 1:
                        pool.wait_ge(gz_set, 2 * s + 1)
                    pool.tensor_tensor(gz_bd[half, r, :, :, g, :], ps_[half, r, :, :, :],
                                       pa[half, r, :, :, :], ALU.subtract).then_inc(gz_set, 1)

            def probabilities(s, r):
                pool.wait_ge(zinv_set, s + 1)
                wait(pool, o_mm, s - 1)
                wait(pool, pt_mm, clip(s - 1, LEARNING))
                wait(pool, gz_set, 2 * clip(s, LEARNING))
                pool.tensor_tensor(pr[:, r, :, :, :], ez[:, r, :, :, :],
                                   zinv[:, r, :].rearrange("p (t b) -> p t b", t=2).unsqueeze(3)
                                   .broadcast_to([P, 2, NB, CH]), ALU.mult).then_inc(pr_set, 1)

            def slot(c, j):
                if learns(c, j - 1):
                    decay(c if j else c - 1, c * NJ + j - 1, (j - 1) % NJ, (j - 1) % 2)
                if learns(c, j):
                    score_gradient(c * NJ + j, j % 2)
                if exists(c, j + 1):
                    probabilities(c * NJ + j + 1, (j + 1) % 2)
                if j == 2 and exists(c, NJ):
                    norm_scale(c + 1)

            pool.memset(ident[:, :], 0.0).then_inc(consts_set, 1)
            pool.memset(neghalf[:, :], -0.5).then_inc(consts_set, 1)
            pool.memset(meansel[:, :, :], 0.0).then_inc(consts_set, 1)
            pool.wait_ge(consts_set, 3)
            pool.affine_select(out=ident[:, :], in_=ident[:, :], compare_op=ALU.not_equal, fill=1.0,
                               base=0, pattern=[[-1, P]], channel_multiplier=1).then_inc(consts_set, 1)
            norm_scale(0)
            pool.memset(pt_bd[:, :, :, :, :, :], 0.0).then_inc(consts_set, 1)
            pool.memset(gz_bd[:, :, :, :, :, :], 0.0).then_inc(consts_set, 1)
            for h, half in halves:
                pool.wait_ge(consts_set, 6 + h)
                pool.memset(meansel[half, h, :], 1.0 / CH).then_inc(consts_set, 1)
            pool.wait_ge(consts_set, 8)
            probabilities(0, 0)
            over_slots(pool, slot)

        @block.vector
        def _(dve):
            def norm(c):
                dve.wait_ge(x_in, 64 * c + 64)
                for u in range(NT):
                    i = dve.bn_stats(stats[:, u, :], xin[:, u, :])
                i.then_inc(stats_set, 1)
                dve.wait_ge(stats_set, c + 1)
                dve.tensor_tensor(moments[:, 0, :], stats[:, :, 1], stats[:, :, 4], ALU.add)
                dve.tensor_tensor(moments[:, 1, :], stats[:, :, 1], stats[:, :, 4], ALU.subtract)
                dve.tensor_tensor(moments[:, 2, :], stats[:, :, 2], stats[:, :, 5], ALU.add).then_inc(ln_chain, 1)
                dve.wait_ge(ln_chain, 3 * c + 1)
                dve.tensor_scalar(mean[:, :], moments[:, 0, :], 0.5, None, ALU.mult)
                dve.scalar_tensor_tensor(out=moments[:, 3, :], in0=moments[:, 1, :], scalar=0.25,
                                         in1=moments[:, 1, :], op0=ALU.mult, op1=ALU.mult)
                dve.tensor_scalar(moments[:, 4, :], moments[:, 2, :], 1.0 / DIM, EPS, ALU.mult, ALU.add
                                  ).then_inc(ln_chain, 1)
                dve.wait_ge(ln_chain, 3 * c + 2)
                dve.tensor_tensor(var_eps[:, :], moments[:, 3, :], moments[:, 4, :], ALU.add).then_inc(ln_chain, 1)

            def normed(c):
                dve.wait_ge(rstd_set, c + 1)
                wait(dve, xt_mm, 2 * c)
                for u in range(NT):
                    i = dve.tensor_scalar(xn[:, u, :], xin[:, u, :], mean[:, u:u + 1], rstd[:, u:u + 1],
                                          ALU.subtract, ALU.mult)
                i.then_inc(xn_set, 1)

            def silu(s, r):
                dve.wait_ge(tanh_set, s + 1)
                wait(dve, z_mm, s - 1)
                wait(dve, kv_mm, clip(s - 1, TOKEN_KV_SLOTS))
                dve.scalar_tensor_tensor(
                    out=qk[:, r, :, :, :].rearrange("p t b n -> p (t b n)"),
                    in0=tanh_qk[:, r, :, :].rearrange("p t n -> p (t n)"), scalar=1.0,
                    in1=bank[B_QK][:, :], op0=ALU.add, op1=ALU.mult).then_inc(qk_set, 1)

            def scores(s, r):
                dve.wait_ge(z_mm, s + 1)
                wait(dve, zs_set, s - 1)
                dve.tensor_reduce(zmax[:, r, :], ps_z, AX.X, ALU.max).then_inc(zmax_set, 1)
                dve.wait_ge(zmax_set, s + 1)
                wait(dve, e_set, s - 1)
                dve.tensor_tensor(zs[:, r, :, :], ps_z, zmax[:, r, :].unsqueeze(2).broadcast_to([P, 2 * NB, CH]),
                                  ALU.subtract).then_inc(zs_set, 1)

            def sums(s, r):
                dve.wait_ge(e_set, s + 1)
                wait(dve, pr_set, s - 1)
                dve.tensor_reduce(zsum[:, r, :], ez[:, r, :, :, :].rearrange("p t b n -> p (t b) n"),
                                  AX.X, ALU.add).then_inc(zsum_set, 1)
                dve.wait_ge(zsum_set, s + 1)
                dve.reciprocal(zinv[:, r, :], zsum[:, r, :]).then_inc(zinv_set, 1)

            def coefficients(c):
                dve.wait_ge(mean_mm, c + 1)
                wait(dve, coef_set, c)
                for g, half in halves:
                    src = ps_x[half, 0:NB * 4 * H].rearrange("p (b m j g) -> p g m j b", b=NB, m=4, g=2)
                    for m, c0 in enumerate((0.5 * BASE_LR, BASE_LR, BASE_WD, BASE_WD)):
                        i = dve.tensor_scalar(coef_next[half, m, :, :], src[:, g, m, :, :], 0.5 * c0, 0.5 * c0,
                                              ALU.mult, ALU.add)
                i.then_inc(mean_evac, 1)

            def inner_products(s, r):
                dve.wait_ge(a_mm, s + 1)
                dve.wait_ge(pt_evac, 3 * s + 3)
                wait(dve, gz_set, 2 * (s - 1))
                dve.tensor_tensor(pa[:, r, :, :, :], ps_a, pt[:, r, :, :, :], ALU.mult).then_inc(pa_set, 1)
                dve.wait_ge(pa_set, s + 1)
                dve.tensor_reduce(ssum[:, r, :], pa[:, r, :, :, :].rearrange("p u g f -> p (u g) f"),
                                  AX.X, ALU.add).then_inc(ssum_set, 1)

            def next_coefficients(c):
                wait(dve, decayed_set, 4 * NJ * c)
                dve.wait_ge(mean_evac, c + 1)
                dve.tensor_copy(coef[:, :, :, :], coef_next[:, :, :, :]).then_inc(coef_set, 1)
                dve.wait_ge(coef_set, c + 1)

            def update(s, jj, r):
                dve.wait_ge(g_mm, s + 1)
                wait(dve, w_set, 4 * s)
                for m in range(2):
                    dve.tensor_tensor(step[:, m, :, :], ps_g[:, m, :, :],
                                      coef[:, m, jj, :].unsqueeze(2).broadcast_to([P, NB, 64]), ALU.mult
                                      ).then_inc(step_set, 1)
                dve.wait_ge(step_set, 2 * s + 2)
                dve.wait_ge(decayed_set, 4 * s + 4)
                for m, w, op in ((0, win_t, ALU.subtract), (1, wout_t, ALU.add)):
                    for g, half in halves:
                        dve.tensor_tensor(w[half, jj, :, 64 * g:64 * g + 64], decayed[half, r, m, :, :],
                                          step[half, m, :, :], op).then_inc(w_set, 1)

            def attended(c, u):
                dve.wait_ge(y_mm, 2 * c + 1 + u)
                dve.wait_ge(xres_in, 64 * c + 64)
                dve.tensor_tensor(xres[:, u, :], ps_x[:, :], xres[:, u, :], ALU.add).then_inc(y_evac, 1)

            def slot(c, j):
                if exists(c, j + 1):
                    scores(c * NJ + j + 1, (j + 1) % 2)
                if j == 0 and exists(c, -1):
                    attended(c - 1, 0)
                if learns(c, j):
                    inner_products(c * NJ + j, j % 2)
                if j == 1 and learns(c, 0):
                    next_coefficients(c)
                if learns(c, j - 1):
                    update(c * NJ + j - 1, (j - 1) % NJ, (j - 1) % 2)
                if exists(c, j + 1):
                    sums(c * NJ + j + 1, (j + 1) % 2)
                if j == 0 and exists(c, -1):
                    attended(c - 1, 1)
                if j == 1 and exists(c, NJ):
                    norm(c + 1)
                if j == 3 and exists(c, NJ):
                    normed(c + 1)
                if j == 7 and exists(c, NJ):
                    coefficients(c + 1)
                if exists(c, j + 3):
                    silu(c * NJ + j + 3, (j + 3) % 2)

            norm(0)
            normed(0)
            for w in (win_t, wout_t, wout):
                dve.memset(w[:, :, :, :], 0.0).then_inc(states_clear, 1)
            dve.wait_ge(states_clear, 3)
            dve.wait_ge(winit_in, 16)
            for m, w in ((0, win_t), (1, wout_t), (2, wout)):
                for g, half in halves:
                    dve.tensor_copy(w[half, :, :, 64 * g:64 * g + 64],
                                    winit[half, m, :, :].unsqueeze(2).broadcast_to([64, NJ, NB, 64])
                                    ).then_inc(states_set, 1)
            coefficients(0)
            for s in range(3):
                silu(s, s % 2)
                if s == 0:
                    scores(0, 0)
                    sums(0, 0)
            over_slots(dve, slot)
            attended(NCH - 1, 0)
            attended(NCH - 1, 1)

        @block.scalar
        def _(act):
            def x_transposed(c, u):
                act.wait_ge(xt_mm, 2 * c + u + 1)
                act.activation(xnt[:, :, u * P:u * P + P], ps_x[:, :].rearrange("p (t n) -> p t n", t=KT),
                               ACT.Copy).then_inc(xt_evac, 1)

            def gate_tanh(c):
                act.wait_ge(gate_mm, c + 1)
                act.activation(gates[:, :, :], ps_x[:, 0:NT * 4 * H].rearrange("p (u n) -> p u n", u=NT),
                               ACT.Tanh, scale=0.5).then_inc(gate_set, 1)

            def qk_tanh(s, r):
                act.wait_ge(qk_mm, s + 1)
                wait(act, qk_set, s - 1)
                act.activation(tanh_qk[:, r, :, :], ps_qk, ACT.Tanh, scale=0.5).then_inc(tanh_set, 1)

            def v_copy(s, r4):
                act.wait_ge(v_mm, s + 1)
                wait(act, a_mm, clip(s - 3, LEARNING))
                act.activation(vt[:, r4, :], ps_v, ACT.Copy).then_inc(v_evac, 1)

            def kv_copy(s, r4):
                act.wait_ge(kv_mm, s + 1)
                wait(act, g_mm, clip(s - 3, LEARNING))
                act.activation(kvtok[:, r4, :, :, :], ps_kv, ACT.Copy).then_inc(kv_evac, 1)

            def exps(s, r):
                act.wait_ge(zs_set, s + 1)
                wait(act, pr_set, s - 1)
                wait(act, zsum_set, s - 1)
                act.activation(ez[:, r, :, :, :].rearrange("p t b n -> p (t b) n"), zs[:, r, :, :], ACT.Exp,
                               scale=0.5).then_inc(e_set, 1)

            def pt_copy(s, r):
                act.wait_ge(pt_mm, s + 1)
                wait(act, ps_set, s - 1)
                wait(act, pa_set, s - 1)
                act.activation(pt[:, r, :, :, :], ps_pt, ACT.Copy).then_inc(pt_evac, 1)
                wait(act, g_mm, s - 1)
                for g, half in halves:
                    act.activation(pt_bd[half, r, :, :, g, :], ps_pt[half], ACT.Copy).then_inc(pt_evac, 1)

            def o_copy(c, s, j):
                act.wait_ge(o_mm, s + 1)
                wait(act, y_mm, 2 * c)
                act.activation(ot[:, j, :], ps_o, ACT.Copy).then_inc(o_evac, 1)

            def wout_copy(s, jj):
                act.wait_ge(wt_mm, s + 1)
                act.activation(wout[:, jj, :, :], ps_wt, ACT.Copy).then_inc(wt_evac, 1)

            def slot(c, j):
                s = c * NJ + j
                if exists(c, j + 1):
                    if before(s + 1, TOKEN_KV_SLOTS):
                        kv_copy(s + 1, (j + 1) % 4)
                    exps(s + 1, (j + 1) % 2)
                if j == 5 and exists(c, NJ):
                    x_transposed(c + 1, 0)
                if learns(c, j):
                    pt_copy(s, j % 2)
                o_copy(c, s, j)
                if learns(c, j - 2):
                    wout_copy(s - 2, (j - 2) % NJ)
                if j == 5 and exists(c, NJ):
                    x_transposed(c + 1, 1)
                if j == 6 and exists(c, NJ):
                    gate_tanh(c + 1)
                if exists(c, j + 3):
                    qk_tanh(s + 3, (j + 3) % 2)
                    if before(s + 3, KV_SLOTS):
                        v_copy(s + 3, (j + 3) % 4)

            act.wait_ge(consts_set, 8)
            x_transposed(0, 0)
            x_transposed(0, 1)
            gate_tanh(0)
            for s in range(3):
                qk_tanh(s, s % 2)
                v_copy(s, s)
                if s == 0:
                    kv_copy(0, 0)
                    exps(0, 0)
            over_slots(act, slot)

        @block.tensor
        def _(pe):
            def x_transposes(c, u):
                pe.wait_ge(xn_set, c + 1)
                if u == 0:
                    wait(pe, mean_evac, c)
                    wait(pe, y_evac, 2 * (c - 1))
                wait(pe, xt_evac, 2 * c + u)
                for t in range(KT):
                    i = pe.transpose(ps_x[:, t * P:t * P + P], xn[:, u, t * P:t * P + P], ident[:, :])
                i.then_inc(xt_mm, 1)

            def gate_scores(c):
                pe.wait_ge(xt_evac, 2 * c + 2)
                for u in range(NT):
                    for t in range(KT):
                        i = pe.matmul(ps_x[:, u * 4 * H:(u + 1) * 4 * H], xnt[:, t, u * P:u * P + P], wlb_s[:, t, :],
                                      start=t == 0, stop=t == KT - 1)
                i.then_inc(gate_mm, 1)

            def gate_means(c):
                pe.wait_ge(gate_set, c + 1)
                for b in range(NB):
                    i = pe.matmul(ps_x[:, b * 4 * H:(b + 1) * 4 * H], meansel[:, b % 2, :], gates[:, b // 2, :],
                                  start=True, stop=True)
                i.then_inc(mean_mm, 1)

            def project(s, j):
                pe.wait_ge(xt_evac, 2)
                wait(pe, qk_set, s)
                for n, (w, loaded) in enumerate(((wq_s, wq_in), (wk_s, wk_in))):
                    if n and not before(s, KV_SLOTS):
                        continue
                    if isinstance(s, int) and s == 0:
                        pe.wait_ge(loaded, 16)
                    for t in range(KT):
                        i = pe.matmul(ps_qk[:, n, :], w[:, t, j * P:j * P + P], xnt[:, t, :],
                                      start=t == 0, stop=t == KT - 1)
                i.then_inc(qk_mm, 1)
                if not before(s, KV_SLOTS):
                    return
                wait(pe, v_evac, s)
                wait(pe, o_evac, s - 2)
                if isinstance(s, int) and s == 0:
                    pe.wait_ge(wv_in, 16)
                for t in range(KT):
                    i = pe.matmul(ps_v, wv_s[:, t, j * P:j * P + P], xnt[:, t, :], start=t == 0, stop=t == KT - 1)
                i.then_inc(v_mm, 1)

            def scores(s, j, r, r4):
                pe.wait_ge(qk_set, s + 1)
                wait(pe, zs_set, s)
                wait(pe, w_set, 4 * (s - NJ + 1))
                for b in range(NB):
                    i = pe.matmul(ps_z.rearrange("p (t b) n -> p t b n", t=2)[:, :, b, :], win_t[:, j, b, :],
                                  qk[:, r, :, b, :], start=True, stop=True)
                i.then_inc(z_mm, 1)
                if not before(s, TOKEN_KV_SLOTS):
                    return
                pe.wait_ge(v_evac, s + 1)
                wait(pe, kv_evac, s)
                wait(pe, wt_evac, clip(s - 3, LEARNING))
                for u in range(NT):
                    pe.transpose(ps_kv[:, 0, u, :], qk[:, r, 1, 2 * u:2 * u + 2, :].rearrange("p b n -> p (b n)"), ident[:, :])
                for u in range(NT):
                    i = pe.transpose(ps_kv[:, 1, u, :], vt[:, r4, u * P:u * P + P], ident[:, :])
                i.then_inc(kv_mm, 1)

            def outputs(c, s, j, r):
                pe.wait_ge(pr_set, s + 1)
                pe.wait_ge(v_evac, clip(s + 3, KV_SLOTS))
                wait(pe, o_evac, s)
                wait(pe, wt_evac, s - NJ + 1)
                for b in range(NB):
                    for g in range(2):
                        i = pe.matmul(ps_o[64 * g:64 * g + 64, b * CH:(b + 1) * CH],
                                      wout[:, j, b, 64 * g:64 * g + 64], pr[:, r, 0, b, :], start=True, stop=True)
                i.then_inc(o_mm, 1)

            def gradients_of_p(s, j, r, r4):
                wait(pe, pt_evac, 3 * s)
                for u in range(NT):
                    i = pe.transpose(ps_pt[:, u, :, :].rearrange("p g f -> p (g f)"),
                                     pr[:, r, 1, 2 * u:2 * u + 2, :].rearrange("p b n -> p (b n)"), ident[:, :])
                i.then_inc(pt_mm, 1)
                wait(pe, pa_set, s)
                for b in range(NB):
                    h, u = b % 2, b // 2
                    i = pe.matmul(bank[B_A][64 * h:64 * h + 64, u * P:u * P + P], vt[:, r4, b * CH:(b + 1) * CH],
                                  wout_t[:, j, b, :], start=True, stop=True)
                i.then_inc(a_mm, 1)

            def gradients(s, r, r4):
                pe.wait_ge(kv_evac, s + 1)
                pe.wait_ge(gz_set, 2 * s + 2)
                wait(pe, step_set, 2 * s)
                for m, by_batch in ((0, gz_bd), (1, pt_bd)):
                    for u in range(NT):
                        for g in range(2):
                            i = pe.matmul(bank[B_G][64 * g:64 * g + 64, m * 256 + u * P:m * 256 + u * P + P],
                                          kvtok[:, r4, m, u, 64 * g:64 * g + 64],
                                          by_batch[:, r, u, g, :, :].rearrange("p b f -> p (b f)"),
                                          start=True, stop=True)
                i.then_inc(g_mm, 1)

            def wout_transposes(s, jj):
                pe.wait_ge(w_set, 4 * s + 4)
                pe.wait_ge(kv_evac, clip(s + 4, TOKEN_KV_SLOTS))
                wait(pe, wt_evac, s)
                for b in range(NB):
                    i = pe.transpose(ps_wt[:, b, :], wout_t[:, jj, b, :], ident[:, :])
                i.then_inc(wt_mm, 1)

            def attention(c, u):
                pe.wait_ge(o_evac, NJ * (c + 1))
                pe.wait_ge(mean_evac, clip(c + 2, NCH))
                wait(pe, y_evac, 2 * c + u)
                if isinstance(c, int) and c == 0:
                    pe.wait_ge(wo_in, 16)
                for j in range(NJ):
                    i = pe.matmul(ps_x[:, :], ot[:, j, u * P:u * P + P], wo_s[:, j, :], start=j == 0, stop=j == NJ - 1)
                i.then_inc(y_mm, 1)

            def slot(c, j):
                s = c * NJ + j
                if exists(c, j + 1):
                    scores(s + 1, (j + 1) % NJ, (j + 1) % 2, (j + 1) % 4)
                if j == 5 and exists(c, NJ):
                    x_transposes(c + 1, 0)
                if j == 0 and exists(c, -1):
                    attention(c - 1, 0)
                outputs(c, s, j, j % 2)
                if learns(c, j):
                    gradients_of_p(s, j, j % 2, j % 4)
                if learns(c, j - 1):
                    gradients(s - 1, (j - 1) % 2, (j - 1) % 4)
                if j == 0 and exists(c, -1):
                    attention(c - 1, 1)
                if learns(c, j - 2):
                    wout_transposes(s - 2, (j - 2) % NJ)
                if exists(c, NJ):
                    if j == 5:
                        x_transposes(c + 1, 1)
                    if j == 6:
                        gate_scores(c + 1)
                    if j == 7:
                        gate_means(c + 1)
                if exists(c, j + 3):
                    if j == 5:
                        pe.wait_ge(xt_evac, 2 * c + 4)
                    project(s + 3, (j + 3) % NJ)

            pe.wait_ge(consts_set, 4)
            x_transposes(0, 0)
            x_transposes(0, 1)
            pe.wait_ge(wlb_in, 16)
            gate_scores(0)
            pe.wait_ge(consts_set, 8)
            gate_means(0)
            for s in range(3):
                project(s, s)
                if s == 0:
                    pe.wait_ge(states_set, 6)
                    scores(0, 0, 0, 0)
            over_slots(pe, slot)
            attention(NCH - 1, 0)
            attention(NCH - 1, 1)


def moments_of(dve, c, xin, tiles, width, stats, moments, mean, var_eps, stats_set, ln_chain):
    for u in range(tiles):
        i = dve.bn_stats(stats[:, u, :], xin[:, u, :])
    i.then_inc(stats_set, 1)
    dve.wait_ge(stats_set, c + 1)
    dve.tensor_tensor(moments[:, 0, :], stats[:, :, 1], stats[:, :, 4], ALU.add)
    dve.tensor_tensor(moments[:, 1, :], stats[:, :, 1], stats[:, :, 4], ALU.subtract)
    dve.tensor_tensor(moments[:, 2, :], stats[:, :, 2], stats[:, :, 5], ALU.add).then_inc(ln_chain, 1)
    dve.wait_ge(ln_chain, 3 * c + 1)
    dve.tensor_scalar(mean[:, :], moments[:, 0, :], 0.5, None, ALU.mult)
    dve.scalar_tensor_tensor(out=moments[:, 3, :], in0=moments[:, 1, :], scalar=0.25, in1=moments[:, 1, :],
                             op0=ALU.mult, op1=ALU.mult)
    dve.tensor_scalar(moments[:, 4, :], moments[:, 2, :], 1.0 / width, EPS, ALU.mult, ALU.add).then_inc(ln_chain, 1)
    dve.wait_ge(ln_chain, 3 * c + 2)
    dve.tensor_tensor(var_eps[:, :], moments[:, 3, :], moments[:, 4, :], ALU.add).then_inc(ln_chain, 1)


def wait(eng, s, value):
    if not isinstance(value, int) or value > 0:
        eng.wait_ge(s, value)


def cross_projections(nc, x1, ctx_t, mask, wq, wk, wv, bq, bk, bv, q_hi, q_lo, k_hi, k_lo, v_out):
    NB, S, DIM = x1.shape
    GT = 512
    NG = NB * S // GT
    GPB = S // GT
    KT = DIM // P
    TT = GT // P
    ex = ExitStack()
    with ex:
        sb = lambda name, shape, dt=F32: ex.enter_context(nc.sbuf_tensor("p_" + name, shape, dt))
        sem = semaphores(nc, ex, "p_")
        bank = [ex.enter_context(nc.psum_tensor(f"p_bank{i}", [P, 512], F32)) for i in range(8)]
        stage = sb("stage", [P, KT, DIM])
        w_hi = [sb(f"w_hi{n}", [P, KT, DIM], F32R) for n in range(3)]
        w_lo = [sb(f"w_lo{n}", [P, KT, DIM], F32R) for n in range(3)]
        bq_s, bk_s = sb("bq", [P, KT]), sb("bk", [P, KT])
        bv_s = sb("bv", [P, DIM])
        ident = sb("ident", [P, P])
        neghalf = sb("neghalf", [P, TT])
        xin, xn = sb("xin", [P, TT, DIM]), sb("xn", [P, TT, DIM])
        stats, moments = sb("stats", [P, TT, 6]), sb("moments", [P, 5, TT])
        mean, var_eps, rstd = sb("mean", [P, TT]), sb("var_eps", [P, TT]), sb("rstd", [P, TT])
        xnt_hi, xnt_lo = (sb(n, [P, 2, KT, GT], F32R) for n in ("xnt_hi", "xnt_lo"))
        ctx_in = sb("ctx_in", [P, KT, GT])
        ctx_hi, ctx_lo = (sb(n, [P, 2, KT, GT], F32R) for n in ("ctx_hi", "ctx_lo"))
        mask_i, mask_f = sb("mask_i", [P, GT], I32), sb("mask_f", [P, 2, GT])
        qk_f = sb("qk_f", [P, 4, GT])
        qk_hi, qk_lo = (sb(n, [P, 4, GT], F32R) for n in ("qk_hi", "qk_lo"))
        v_s = sb("v_s", [P, 4, DIM])

        consts_in, w_in, w_split, w_hi_set = sem("consts_in"), sem("w_in"), sem("w_split"), sem("w_hi_set")
        consts_set = sem("consts_set")
        x_in, c_in, m_in = sem("x_in"), sem("c_in"), sem("m_in")
        stats_set, ln_chain, rstd_set, xn_set = sem("stats_set"), sem("ln_chain"), sem("rstd_set"), sem("xn_set")
        c_hi_set, c_lo_set, mask_set = sem("c_hi_set"), sem("c_lo_set"), sem("mask_set")
        xt_mm = sem("xt_mm")
        xt_hi_set, xt_lo_set = sem("xt_hi_set"), sem("xt_lo_set")
        out_mm = sem("out_mm")
        q_evac, k_evac, v_evac = sem("q_evac"), sem("k_evac"), sem("v_evac")
        hi_set, lo_set = sem("hi_set"), sem("lo_set")
        qk_out = [sem(f"qk_out{r}") for r in range(4)]
        v_outs = [sem(f"v_out{r}") for r in range(4)]
        wait_taken = sem("wait_taken")
        block = ex.enter_context(nc.Block())

        def over_groups(eng, group):
            for h in range(GPB):
                group(0, h)
            with eng.Fori(1, NB - 1) as b:
                for h in range(GPB):
                    group(b, h)
            for h in range(GPB):
                group(NB - 1, h)

        def following(b, h):
            if h + 1 < GPB:
                return b, h + 1
            return (b + 1, 0) if not isinstance(b, int) or b + 1 < NB else None

        @block.sync
        def _(sp):
            sp.dma_start(bq_s[:, :], bq).then_inc(consts_in, 16)
            sp.dma_start(bk_s[:, :], bk).then_inc(consts_in, 16)
            sp.dma_start(bv_s[:, :], bv.unsqueeze(0).broadcast_to([P, DIM])).then_inc(consts_in, 16)

            def load(b, h):
                g = b * GPB + h
                wait(sp, xn_set, g)
                sp.dma_start(xin[:, :, :], x1[b, h * GT:(h + 1) * GT, :].rearrange("(u p) d -> p u d", p=P)
                             ).then_inc(x_in, 16)
                wait(sp, c_lo_set, g)
                sp.dma_start(ctx_in[:, :, :], ctx_t[b, :, h * GT:(h + 1) * GT].rearrange("(t p) n -> p t n", p=P)
                             ).then_inc(c_in, 16)
                wait(sp, mask_set, g)
                sp.dma_start(mask_i[:, :], mask[b, h * GT:(h + 1) * GT].unsqueeze(0).broadcast_to([P, GT])
                             ).then_inc(m_in, 16)

            def stores(b, h):
                g = b * GPB + h
                for u in range(8):
                    n, t = divmod(u, 4)
                    hi, lo = ((q_hi, q_lo), (k_hi, k_lo))[n]
                    sp.wait_ge(lo_set, 8 * g + u + 1)
                    if u == 0:
                        sp.sem_inc(wait_taken, 1)
                    for part, of in ((hi, qk_hi), (lo, qk_lo)):
                        sp.dma_start(part[b, t * P:(t + 1) * P, h * GT:(h + 1) * GT], of[:, u % 4, :].bitcast(F32)
                                     ).then_inc(qk_out[u % 4], 16)
                for u in range(TT):
                    sp.wait_ge(v_evac, 4 * g + u + 1)
                    sp.dma_start(v_out[b, h * GT + u * P:h * GT + (u + 1) * P, :], v_s[:, u, :]
                                 ).then_inc(v_outs[u], 16)

            load(0, 0)
            for n, w in enumerate((wq, wk, wv)):
                wait(sp, w_split, n)
                sp.dma_start(stage[:, :, :], w.rearrange("(t p) n -> p t n", p=P)).then_inc(w_in, 16)

            def group(b, h):
                if following(b, h):
                    load(*following(b, h))
                stores(b, h)

            over_groups(sp, group)
            for r in range(4):
                sp.wait_ge(qk_out[r], 32 * 2 * NG)
                sp.wait_ge(v_outs[r], 16 * NG)

        @block.gpsimd
        def _(pool):
            pool.memset(ident[:, :], 0.0).then_inc(consts_set, 1)
            pool.memset(neghalf[:, :], -0.5).then_inc(consts_set, 1)
            pool.wait_ge(consts_set, 2)
            pool.affine_select(out=ident[:, :], in_=ident[:, :], compare_op=ALU.not_equal, fill=1.0,
                               base=0, pattern=[[-1, P]], channel_multiplier=1).then_inc(consts_set, 1)

            def norm_scale(g):
                pool.wait_ge(ln_chain, 3 * g + 3)
                wait(pool, xn_set, g)
                pool.tensor_tensor(rstd[:, :], var_eps[:, :], neghalf[:, :], ALU.pow).then_inc(rstd_set, 1)

            def group(b, h):
                g = b * GPB + h
                if following(b, h):
                    norm_scale(g + 1)
                for u in range(8):
                    n = 8 * g + u
                    wait(pool, qk_out[u % 4], 32 * (2 * g + u // 4))
                    pool.wait_ge(hi_set, n + 1)
                    pool.tensor_tensor(qk_lo[:, u % 4, :], qk_f[:, u % 4, :], qk_hi[:, u % 4, :].bitcast(F32),
                                       ALU.subtract).then_inc(lo_set, 1)

            norm_scale(0)
            over_groups(pool, group)

        @block.vector
        def _(dve):
            def prepare(g, b, h, r):
                dve.wait_ge(x_in, 16 * g + 16)
                moments_of(dve, g, xin, TT, DIM, stats, moments, mean, var_eps, stats_set, ln_chain)
                dve.wait_ge(c_in, 16 * g + 16)
                wait(dve, out_mm, 12 * (g - 1))
                dve.tensor_copy(ctx_hi[:, r, :, :], ctx_in[:, :, :]).then_inc(c_hi_set, 1)
                dve.wait_ge(c_hi_set, g + 1)
                dve.tensor_tensor(ctx_lo[:, r, :, :], ctx_in[:, :, :], ctx_hi[:, r, :, :].bitcast(F32), ALU.subtract
                                  ).then_inc(c_lo_set, 1)
                dve.wait_ge(m_in, 16 * g + 16)
                dve.tensor_scalar(mask_f[:, r, :], mask_i[:, :], 0.0, None, ALU.not_equal).then_inc(mask_set, 1)
                dve.wait_ge(rstd_set, g + 1)
                wait(dve, xt_mm, 4 * g)
                for u in range(TT):
                    i = dve.tensor_scalar(xn[:, u, :], xin[:, u, :], mean[:, u:u + 1], rstd[:, u:u + 1],
                                          ALU.subtract, ALU.mult)
                i.then_inc(xn_set, 1)

            def transposed_lo(g, r):
                for u in range(TT):
                    dve.wait_ge(xt_hi_set, 4 * g + u + 1)
                    dve.tensor_tensor(xnt_lo[:, r, :, u * P:(u + 1) * P],
                                      bank[u % 2][:, :].rearrange("p (t n) -> p t n", t=KT),
                                      xnt_hi[:, r, :, u * P:(u + 1) * P].bitcast(F32), ALU.subtract
                                      ).then_inc(xt_lo_set, 1)

            prepare(0, 0, 0, 0)
            dve.wait_ge(consts_in, 48)
            for n in range(3):
                dve.wait_ge(w_in, 16 * n + 16)
                dve.tensor_copy(w_hi[n][:, :, :], stage[:, :, :]).then_inc(w_hi_set, 1)
                dve.wait_ge(w_hi_set, n + 1)
                dve.tensor_tensor(w_lo[n][:, :, :], stage[:, :, :], w_hi[n][:, :, :].bitcast(F32), ALU.subtract
                                  ).then_inc(w_split, 1)
                if n == 0:
                    transposed_lo(0, 0)

            def group(b, h):
                g, r = b * GPB + h, h % 2
                if following(b, h):
                    prepare(g + 1, *following(b, h), (h + 1) % 2)
                for t in range(4):
                    dve.wait_ge(out_mm, 12 * g + 5 + t)
                    dve.wait_ge(mask_set, g + 1)
                    wait(dve, lo_set, 8 * g + t + 1)
                    dve.scalar_tensor_tensor(out=qk_f[:, t, :], in0=bank[2 + (4 + t) % 6][:, :],
                                             scalar=bk_s[:, t:t + 1], in1=mask_f[:, r, :], op0=ALU.add,
                                             op1=ALU.mult).then_inc(k_evac, 1)
                if following(b, h):
                    transposed_lo(g + 1, (h + 1) % 2)
                for u in range(TT):
                    dve.wait_ge(out_mm, 12 * g + 9 + u)
                    wait(dve, v_outs[u], 16 * g)
                    dve.tensor_tensor(v_s[:, u, :], bank[2 + (8 + u) % 6][:, :], bv_s[:, :], ALU.add
                                      ).then_inc(v_evac, 1)

            over_groups(dve, group)

        @block.scalar
        def _(act):
            def transposed_hi(g, r):
                for u in range(TT):
                    act.wait_ge(xt_mm, 4 * g + u + 1)
                    wait(act, out_mm, 12 * (g - 1))
                    act.activation(xnt_hi[:, r, :, u * P:(u + 1) * P],
                                   bank[u % 2][:, :].rearrange("p (t n) -> p t n", t=KT), ACT.Copy
                                   ).then_inc(xt_hi_set, 1)

            def first_part(g, u):
                wait(act, qk_out[u % 4], 32 * (2 * g + u // 4))
                act.activation(qk_hi[:, u % 4, :], qk_f[:, u % 4, :], ACT.Copy).then_inc(hi_set, 1)

            transposed_hi(0, 0)
            act.wait_ge(consts_in, 48)

            def group(b, h):
                g = b * GPB + h
                for t in range(4):
                    act.wait_ge(out_mm, 12 * g + 1 + t)
                    wait(act, lo_set, 8 * g - 3 + t)
                    act.activation(qk_f[:, t, :], bank[2 + t][:, :], ACT.Identity, bias=bq_s[:, t:t + 1]
                                   ).then_inc(q_evac, 1)
                    act.wait_ge(q_evac, 4 * g + t + 1)
                    first_part(g, t)
                for t in range(4):
                    act.wait_ge(k_evac, 4 * g + t + 1)
                    first_part(g, 4 + t)
                if following(b, h):
                    transposed_hi(g + 1, (h + 1) % 2)

            over_groups(act, group)

        @block.tensor
        def _(pe):
            def transposes(g):
                for u in range(TT):
                    pe.wait_ge(xn_set, g + 1)
                    wait(pe, xt_lo_set, 4 * g + u - 1)
                    for t in range(KT):
                        i = pe.transpose(bank[u % 2][:, t * P:(t + 1) * P], xn[:, u, t * P:(t + 1) * P], ident[:, :])
                    i.then_inc(xt_mm, 1)

            def product(out, left, right):
                for t in range(KT):
                    for n, (a, b) in enumerate(((0, 0), (0, 1), (1, 0))):
                        i = pe.matmul(out, left(a, t), right(b, t), start=t == 0 and n == 0, stop=t == KT - 1 and n == 2)
                return i

            def group(b, h):
                g, r = b * GPB + h, h % 2
                pe.wait_ge(xt_lo_set, 4 * g + 4)
                pe.wait_ge(c_lo_set, g + 1)
                for i in range(12):
                    if i == 8 and following(b, h):
                        transposes(g + 1)
                    if i < 2:
                        wait(pe, k_evac, 4 * (g - 1) + i + 3)
                    elif i < 6:
                        wait(pe, v_evac, 4 * (g - 1) + i - 1)
                    elif i < 10:
                        pe.wait_ge(q_evac, 4 * g + i - 5)
                    else:
                        pe.wait_ge(k_evac, 4 * g + i - 9)
                    n, t = divmod(i, 4)
                    if t == 0:
                        pe.wait_ge(w_split, n + 1)
                    w = (w_hi[n], w_lo[n])
                    if n < 2:
                        act_ = ((xnt_hi, xnt_lo), (ctx_hi, ctx_lo))[n]
                        last = product(bank[2 + i % 6][:, :], lambda a, k: w[a][:, k, t * P:(t + 1) * P],
                                       lambda a, k: act_[a][:, r, k, :])
                    else:
                        last = product(bank[2 + i % 6][:, :],
                                       lambda a, k: (ctx_hi, ctx_lo)[a][:, r, k, t * P:(t + 1) * P],
                                       lambda a, k: w[a][:, k, :])
                    last.then_inc(out_mm, 1)

            pe.wait_ge(consts_set, 3)
            transposes(0)
            over_groups(pe, group)


def cross_attention(nc, q_hi, q_lo, k_hi, k_lo, v, mask, m_rows, ctx_out):
    NB, DIM, S = q_hi.shape
    DK = 32
    HT = P // DK
    NTILE = DIM // P
    NSLOT = NB * NTILE
    KB = S // P
    NSTEP = 2 * KB
    SCALE = DK ** -0.5
    MASK_ROW, MAX_ROW, ROWS = 3 * DK, 3 * DK + 2, 3 * DK + 4
    PER_STEP = (2, 3, 2, 3, 2, 3, 2, 3, 2, 3, 2, 3, 2)
    MAX_STEP = len(PER_STEP)
    UNITS = HT * KB
    PARTS = 4
    assert sum(PER_STEP) == UNITS and NTILE % 2 == 0
    masked = -1e9 / SCALE
    unit = 2.0 ** (33 - 12)
    masked_hi = round(masked / unit) * unit
    masked_lo = round((masked - masked_hi) / 512.0) * 512.0
    ex = ExitStack()
    with ex:
        sb = lambda name, shape, dt=F32: ex.enter_context(nc.sbuf_tensor("c_" + name, shape, dt))
        sem = semaphores(nc, ex, "c_")
        psum = lambda name, shape: ex.enter_context(nc.psum_tensor("c_" + name, shape, F32))
        ps_s = [psum(f"ps_s{i}", [P, 512]) for i in range(2)]
        ps_max = [psum(f"ps_max{i}", [P, 2, 512]) for i in range(2)]
        ps_ctx, ps_sum = psum("ps_ctx", [P, 512]), psum("ps_sum", [P, 512])
        qs = [sb(f"qs{i}", [P, HT, S], F32R) for i in range(NTILE)]
        ks = [sb(f"ks{i}", [P, HT, S], F32R) for i in range(NTILE)]
        vs = sb("vs", [P, NTILE, KB, P])
        pt = sb("pt", [P, 2, HT, 512])
        inverse = sb("inverse", [P, 2, 512])
        ones = sb("ones", [P, DK])
        ident = sb("ident", [P, P])
        mask_i, mask_f = sb("mask_i", [P, S], I32), sb("mask_f", [P, S])
        mval, neg_mval = sb("mval", [P, 1]), sb("neg_mval", [P, 1])
        neg_max = sb("neg_max", [P, UNITS])
        max_parts = sb("max_parts", [P, P // UNITS, UNITS])
        max_t = sb("max_t", [2 * UNITS, P])
        sum_s, raw = sb("sum_s", [P, 2, 512]), sb("raw", [P, 2, 512])
        ctx_s = sb("ctx_s", [P, 2, 512])

        consts_set, rows_set = sem("consts_set"), sem("rows_set")
        stack_in = [sem(f"stack_in{i}") for i in range(2)]
        v_in = [sem(f"v_in{i}") for i in range(2)]
        m_in = sem("m_in")
        mask_set = sem("mask_set")
        mask_rows = sem("mask_rows")
        s_mm = sem("s_mm")
        exp_set = sem("exp_set")
        pv_mm = sem("pv_mm")
        c_mm, c_max = sem("c_mm"), sem("c_max")
        hi_set, parts_set = sem("hi_set"), sem("parts_set")
        mt_mm, mt_evac = sem("mt_mm"), sem("mt_evac")
        m_stored, m_rows_in = sem("m_stored"), sem("m_rows_in")
        sum_set, raw_set = sem("sum_set"), sem("raw_set")
        inverse_set = sem("inverse_set")
        norm_set = sem("norm_set")
        ctx_stored = [sem(f"ctx_stored{i}") for i in range(2)]
        parts_clear, wait_taken = sem("parts_clear"), sem("wait_taken")
        block = ex.enter_context(nc.Block())
        mrows = slice(MASK_ROW, MASK_ROW + 2)

        def over_slots(eng, slot):
            for t in range(NTILE):
                slot(0, t)
            with eng.Fori(1, NB - 1) as b:
                for t in range(NTILE):
                    slot(b, t)
            for t in range(NTILE):
                slot(NB - 1, t)

        def following(b, t):
            if t + 1 < NTILE:
                return b, t + 1
            return (b + 1, 0) if not isinstance(b, int) or b + 1 < NB else None

        def after_next(b, t):
            nxt = following(b, t)
            return following(*nxt) if nxt else None

        @block.sync
        def _(sp):
            def load_stack(b, t):
                T = NTILE * b + t
                wait(sp, s_mm, HT * NSTEP * (T - NTILE + 1))
                if not isinstance(T, int):
                    sp.sem_inc(wait_taken, 1)
                rows = lambda of: of[b, t * P:(t + 1) * P, :].rearrange("(h r) n -> r h n", h=HT)
                for i, (q, k) in enumerate(((q_hi, k_hi), (q_lo, k_hi), (q_hi, k_lo))):
                    sp.dma_start(qs[t][i * DK:(i + 1) * DK, :, :].bitcast(F32), rows(q)).then_inc(stack_in[t % 2], 16)
                    sp.dma_start(ks[t][i * DK:(i + 1) * DK, :, :].bitcast(F32), rows(k)).then_inc(stack_in[t % 2], 16)
                wait(sp, pv_mm, NSTEP * (T - NTILE + 1))
                if not isinstance(T, int):
                    sp.sem_inc(wait_taken, 1)
                sp.dma_start(vs[:, t, :, :], v[b, :, t * P:(t + 1) * P].rearrange("(i p) d -> p i d", p=P)
                             ).then_inc(v_in[t % 2], 16)

            def load_mask(b):
                sp.dma_start(mask_i[mrows, :], mask[b, :].unsqueeze(0).broadcast_to([2, S])).then_inc(m_in, 16)

            def maximum_rows(T, t):
                sp.wait_ge(mt_evac, T + 1)
                sp.dma_start(m_rows.rearrange("a h (t n) -> (a h t) n", n=P), max_t[:, :]).then_inc(m_stored, 16)
                sp.wait_ge(m_stored, 16 * T + 16)
                sp.dma_start(qs[t][MAX_ROW:ROWS, :, :].bitcast(F32), m_rows).then_inc(m_rows_in, 16)

            def store(b, t, half):
                sp.wait_ge(norm_set, 2 * (NTILE * b + t) + half + 1)
                if not isinstance(b, int):
                    sp.sem_inc(wait_taken, 1)
                sp.dma_start(ctx_out[b, t * P:(t + 1) * P, half * 512:(half + 1) * 512], ctx_s[:, half, :]
                             ).then_inc(ctx_stored[half], 16)

            load_mask(0)
            load_stack(0, 0)
            load_stack(0, 1)
            sp.wait_ge(rows_set, 2 * NTILE)
            maximum_rows(0, 0)

            def slot(b, t):
                T, nxt = NTILE * b + t, following(b, t)
                if nxt:
                    if t == 1 and (not isinstance(b, int) or b + 1 < NB):
                        sp.wait_ge(mask_set, b + 1)
                        load_mask(b + 1)
                    if after_next(b, t):
                        load_stack(*after_next(b, t))
                store(b, t, 0)
                if nxt:
                    maximum_rows(T + 1, (t + 1) % NTILE)
                store(b, t, 1)

            over_slots(sp, slot)
            for half in range(2):
                sp.wait_ge(ctx_stored[half], 16 * NSLOT)

        @block.gpsimd
        def _(pool):
            pool.memset(ident[:, :], 0.0).then_inc(consts_set, 1)
            pool.memset(ones[:, :], 1.0).then_inc(consts_set, 1)
            pool.memset(mval[:, :], masked_lo).then_inc(consts_set, 1)
            pool.memset(neg_mval[:, :], -masked_lo).then_inc(consts_set, 1)
            pool.wait_ge(consts_set, 4)
            pool.affine_select(out=ident[:, :], in_=ident[:, :], compare_op=ALU.not_equal, fill=1.0,
                               base=0, pattern=[[-1, P]], channel_multiplier=1).then_inc(consts_set, 1)
            for n, (of, value) in enumerate(((mval, masked_hi), (neg_mval, -masked_hi))):
                pool.wait_ge(consts_set, 5 + n)
                pool.affine_select(out=of[:, :], in_=of[:, :], compare_op=ALU.not_equal, fill=value,
                                   base=-MASK_ROW, pattern=[[0, 1]], channel_multiplier=1).then_inc(consts_set, 1)
            pool.wait_ge(consts_set, 7)
            for s_ in zip(qs, ks):
                for of in s_:
                    pool.memset(of[MASK_ROW:ROWS, :, :].bitcast(F32), 1.0).then_inc(rows_set, 1)

            def slot(b, t):
                T = NTILE * b + t
                for half in range(2):
                    pool.wait_ge(raw_set, 2 * T + half + 1)
                    pool.wait_ge(inverse_set, PARTS * (2 * T + half + 1))
                    wait(pool, ctx_stored[half], 16 * T)
                    pool.tensor_tensor(ctx_s[:, half, :], raw[:, half, :], inverse[:, half, :], ALU.mult
                                       ).then_inc(norm_set, 1)

            over_slots(pool, slot)

        @block.vector
        def _(dve):
            def set_mask(b):
                dve.wait_ge(m_in, 16 * b + 16)
                wait(dve, mask_rows, NTILE * HT * b)
                dve.tensor_scalar(mask_f[mrows, :], mask_i[mrows, :], 0.0, None, ALU.not_equal).then_inc(mask_set, 1)

            def set_mask_rows(b, t):
                T = NTILE * b + t
                dve.wait_ge(mask_set, b + 1)
                wait(dve, s_mm, HT * NSTEP * (T - NTILE + 1))
                for h in range(HT):
                    dve.tensor_scalar(ks[t][mrows, h, :], mask_f[mrows, :], neg_mval[mrows, :], mval[mrows, :],
                                      ALU.mult, ALU.add).then_inc(mask_rows, 1)

            def maxima(T, units):
                for u in units:
                    dve.wait_ge(c_mm, UNITS * T + u + 1)
                    if u == 0:
                        wait(dve, parts_set, T)
                    dve.tensor_reduce(neg_max[:, u:u + 1], ps_max[u % 2][:, :, :].rearrange("p t n -> p (t n)"),
                                      AX.X, ALU.max, negate=True).then_inc(c_max, 1)

            def parts_of_maxima(T):
                dve.wait_ge(c_max, UNITS * T + UNITS)
                wait(dve, mt_mm, T)
                dve.tensor_copy(max_parts[:, 0, :].bitcast(F32R), neg_max[:, :]).then_inc(hi_set, 1)
                dve.wait_ge(hi_set, T + 1)
                dve.tensor_tensor(max_parts[:, 1, :].bitcast(F32R), neg_max[:, :], max_parts[:, 0, :], ALU.subtract
                                  ).then_inc(parts_set, 1)

            def maxima_by_rows(T):
                dve.wait_ge(mt_mm, T + 1)
                wait(dve, m_stored, 16 * T)
                dve.tensor_copy(max_t[:, :], ps_max[0][0:2 * UNITS, 0, 0:P]).then_inc(mt_evac, 1)

            def summed(T, half):
                dve.wait_ge(pv_mm, NSTEP * T + KB * (half + 1))
                wait(dve, norm_set, 2 * T + half - 1)
                dve.tensor_copy(sum_s[:, half, :], ps_sum[:, :]).then_inc(sum_set, 1)

            def inverses(T, half, part):
                dve.wait_ge(sum_set, 2 * T + half + 1)
                wait(dve, norm_set, 2 * T + half - 1)
                n = 512 // PARTS
                dve.reciprocal(inverse[:, half, part * n:(part + 1) * n], sum_s[:, half, part * n:(part + 1) * n]
                               ).then_inc(inverse_set, 1)

            dve.memset(max_parts[:, 2:, :], 0.0).then_inc(parts_clear, 1)
            dve.wait_ge(rows_set, 2)
            set_mask(0)
            set_mask_rows(0, 0)
            maxima(0, range(UNITS))
            parts_of_maxima(0)
            maxima_by_rows(0)
            dve.wait_ge(rows_set, 2 * NTILE)
            set_mask_rows(0, 1)

            def slot(b, t):
                T, nxt = NTILE * b + t, following(b, t)
                later = after_next(b, t)
                u = 0
                for i in range(NSTEP):
                    if nxt and i < MAX_STEP:
                        n = PER_STEP[i]
                        maxima(T + 1, range(u, u + n))
                        u += n
                        if i == MAX_STEP - 1:
                            parts_of_maxima(T + 1)
                    if nxt and i == MAX_STEP:
                        maxima_by_rows(T + 1)
                    if i < PARTS and (not isinstance(T, int) or T):
                        inverses(T - 1, 1, i)
                    if KB <= i < KB + PARTS:
                        inverses(T, 0, i - KB)
                    if i % KB == KB - 1:
                        summed(T, i // KB)
                    if i == MAX_STEP and later:
                        if later[1] == 0:
                            set_mask(later[0])
                        set_mask_rows(*later)

            over_slots(dve, slot)
            for part in range(PARTS):
                inverses(NSLOT - 1, 1, part)

        @block.scalar
        def _(act):
            def weighted(T, half):
                act.wait_ge(pv_mm, NSTEP * T + KB * (half + 1))
                wait(act, norm_set, 2 * T + half - 1)
                act.activation(raw[:, half, :], ps_ctx[:, :], ACT.Copy).then_inc(raw_set, 1)

            def slot(b, t):
                T = NTILE * b + t
                for i in range(NSTEP):
                    for h in range(HT):
                        act.wait_ge(s_mm, HT * (NSTEP * T + i) + h + 1)
                        wait(act, pv_mm, NSTEP * T + i - 1)
                        act.activation(pt[:, i % 2, h, :], ps_s[h % 2][:, :], ACT.Exp, scale=SCALE).then_inc(exp_set, 1)
                        if h == HT - 1 and i % KB == 0 and (not isinstance(T, int) or T or i):
                            weighted(T if i else T - 1, (i // KB + 1) % 2)

            over_slots(act, slot)
            weighted(NSLOT - 1, 1)

        @block.tensor
        def _(pe):
            def scores(T, t, i, heads):
                half, kb = i // KB, i % KB
                if i == 0 and heads[0] == 0:
                    pe.wait_ge(m_rows_in, 16 * T + 16)
                for h in heads:
                    wait(pe, exp_set, HT * (NSTEP * T + i) + h - 1)
                    pe.matmul(ps_s[h % 2][:, :], ks[t][0:ROWS, h, kb * P:(kb + 1) * P],
                              qs[t][0:ROWS, h, half * 512:(half + 1) * 512], start=True, stop=True).then_inc(s_mm, 1)

            def score_rows(b, t, units):
                T = NTILE * b + t
                for u in units:
                    h, qb = divmod(u, KB)
                    if u == 0:
                        pe.wait_ge(stack_in[t % 2], 96 * (NTILE // 2 * b + t // 2) + 96)
                        wait(pe, mt_evac, T)
                    wait(pe, c_max, UNITS * T + u - 1)
                    for half in range(2):
                        i = pe.matmul(ps_max[u % 2][:, half, :], qs[t][0:MAX_ROW, h, qb * P:(qb + 1) * P],
                                      ks[t][0:MAX_ROW, h, half * 512:(half + 1) * 512], start=True, stop=True)
                    i.then_inc(c_mm, 1)

            def maxima_transposed(T):
                pe.wait_ge(parts_set, T + 1)
                pe.transpose(ps_max[0][:, 0, 0:P], max_parts[:, :, :].rearrange("p a u -> p (a u)"),
                             ident[:, :]).then_inc(mt_mm, 1)

            def values(b, T, t, i):
                kb = i % KB
                if i == 0:
                    pe.wait_ge(v_in[t % 2], 16 * (NTILE // 2 * b + t // 2) + 16)
                if kb == 0:
                    wait(pe, raw_set, 2 * T + i // KB)
                    wait(pe, sum_set, 2 * T + i // KB)
                for h in range(HT):
                    pe.wait_ge(exp_set, HT * (NSTEP * T + i) + h + 1)
                    pe.matmul(ps_ctx[h * DK:(h + 1) * DK, :], vs[:, t, kb, h * DK:(h + 1) * DK],
                              pt[:, i % 2, h, :], start=kb == 0, stop=kb == KB - 1)

            def sums(i):
                kb = i % KB
                for h in range(HT):
                    last = pe.matmul(ps_sum[h * DK:(h + 1) * DK, :], ones[:, :], pt[:, i % 2, h, :],
                                     start=kb == 0, stop=kb == KB - 1)
                last.then_inc(pv_mm, 1)

            pe.wait_ge(consts_set, 7)
            pe.wait_ge(rows_set, 2)
            pe.wait_ge(parts_clear, 1)
            pe.wait_ge(mask_rows, HT)
            score_rows(0, 0, range(UNITS))
            maxima_transposed(0)
            scores(0, 0, 0, range(HT // 2))
            scores(0, 0, 0, range(HT // 2, HT))

            def slot(b, t):
                T, nxt = NTILE * b + t, following(b, t)
                u = 0
                for i in range(NSTEP):
                    if i + 1 < NSTEP:
                        ahead = (T, t, i + 1)
                    else:
                        ahead = (T + 1, (t + 1) % NTILE, 0) if nxt else None
                    if ahead:
                        scores(*ahead, range(HT // 2))
                    if nxt and i == 0:
                        pe.wait_ge(mask_rows, HT * (T + 2))
                    units = range(u, u + PER_STEP[i]) if nxt and i < MAX_STEP else range(0)
                    u += len(units)
                    score_rows(*(nxt or (b, t)), units[:1])
                    values(b, T, t, i)
                    if nxt and i == MAX_STEP:
                        maxima_transposed(T + 1)
                    if ahead:
                        scores(*ahead, range(HT // 2, HT))
                    score_rows(*(nxt or (b, t)), units[1:])
                    sums(i)

            over_slots(pe, slot)


def output_projection_and_gate(nc, ctx, x1, wo, bo, gw1, gb1, x2, xn_hi, xn_lo, h_sums):
    NB, S, DIM = x1.shape
    GT = 512
    NG = NB * S // GT
    GPB = S // GT
    KT = DIM // P
    TT = GT // P
    ex = ExitStack()
    with ex:
        sb = lambda name, shape, dt=F32: ex.enter_context(nc.sbuf_tensor("o_" + name, shape, dt))
        sem = semaphores(nc, ex, "o_")
        bank = [ex.enter_context(nc.psum_tensor(f"o_bank{i}", [P, 512], F32)) for i in range(8)]
        stage = sb("stage", [P, KT, DIM])
        w_hi = [sb(f"w_hi{n}", [P, KT, DIM], F32R) for n in range(2)]
        w_lo = [sb(f"w_lo{n}", [P, KT, DIM], F32R) for n in range(2)]
        bo_s, gb1_s = sb("bo", [P, DIM]), sb("gb1", [P, KT])
        ident, neghalf = sb("ident", [P, P]), sb("neghalf", [P, TT])
        ctx_in = sb("ctx_in", [P, KT, GT])
        ctx_hi, ctx_lo = (sb(n, [P, KT, GT], F32R) for n in ("ctx_hi", "ctx_lo"))
        x1_in, x1_b = sb("x1_in", [P, TT, DIM]), sb("x1_b", [P, TT, DIM])
        x2_s, xn = sb("x2_s", [P, TT, DIM]), sb("xn", [P, TT, DIM])
        stats, moments = sb("stats", [P, TT, 6]), sb("moments", [P, 5, TT])
        mean, var_eps, rstd = sb("mean", [P, TT]), sb("var_eps", [P, TT]), sb("rstd", [P, TT])
        xnt_hi, xnt_lo = (sb(n, [P, 2, KT, GT], F32R) for n in ("xnt_hi", "xnt_lo"))
        relu = sb("relu", [P, 2, GT])
        hs = sb("hs", [P, NB, GPB, KT])

        consts_in, w_in, w_split, w_hi_set = sem("consts_in"), sem("w_in"), sem("w_split"), sem("w_hi_set")
        consts_set = sem("consts_set")
        c_in, x_in = sem("c_in"), sem("x_in")
        c_hi_set, c_lo_set = sem("c_hi_set"), sem("c_lo_set")
        biased = sem("biased")
        o_mm, x2_set = sem("o_mm"), sem("x2_set")
        x2_stored = sem("x2_stored")
        stats_set, ln_chain, rstd_set, xn_set = sem("stats_set"), sem("ln_chain"), sem("rstd_set"), sem("xn_set")
        xt_mm, xt_hi_set, xt_lo_set = sem("xt_mm"), sem("xt_hi_set"), sem("xt_lo_set")
        xn_stored = [sem(f"xn_stored{r}") for r in range(2)]
        gate_mm, relu_set = sem("gate_mm"), sem("relu_set")
        hs_stored = sem("hs_stored")
        wait_taken = sem("wait_taken")
        block = ex.enter_context(nc.Block())

        def over_groups(eng, group):
            for h in range(GPB):
                group(0, h)
            with eng.Fori(1, NB - 1) as b:
                for h in range(GPB):
                    group(b, h)
            for h in range(GPB):
                group(NB - 1, h)

        def following(b, h):
            if h + 1 < GPB:
                return b, h + 1
            return (b + 1, 0) if not isinstance(b, int) or b + 1 < NB else None

        def after_next(b, h):
            nxt = following(b, h)
            return following(*nxt) if nxt else None

        @block.sync
        def _(sp):
            sp.dma_start(bo_s[:, :], bo.unsqueeze(0).broadcast_to([P, DIM])).then_inc(consts_in, 16)
            sp.dma_start(gb1_s[:, :], gb1).then_inc(consts_in, 16)

            def load_context(b, h):
                g = b * GPB + h
                wait(sp, c_lo_set, g)
                if not isinstance(b, int):
                    sp.sem_inc(wait_taken, 1)
                sp.dma_start(ctx_in[:, :, :], ctx[b, :, h * GT:(h + 1) * GT].rearrange("(t p) n -> p t n", p=P)
                             ).then_inc(c_in, 16)

            def load_x1(b, h):
                g = b * GPB + h
                wait(sp, biased, g)
                if not isinstance(b, int):
                    sp.sem_inc(wait_taken, 1)
                sp.dma_start(x1_in[:, :, :], x1[b, h * GT:(h + 1) * GT, :].rearrange("(u p) d -> p u d", p=P)
                             ).then_inc(x_in, 16)

            def stores(b, h):
                g = b * GPB + h
                sp.wait_ge(x2_set, 4 * g + 4)
                if not isinstance(b, int):
                    sp.sem_inc(wait_taken, 1)
                sp.dma_start(x2[b, h * GT:(h + 1) * GT, :].rearrange("(u p) d -> p u d", p=P), x2_s[:, :, :]
                             ).then_inc(x2_stored, 16)
                sp.wait_ge(xt_lo_set, 4 * g + 4)
                if not isinstance(b, int):
                    sp.sem_inc(wait_taken, 1)
                for part, of in ((xn_hi, xnt_hi), (xn_lo, xnt_lo)):
                    sp.dma_start(part[b, :, h * GT:(h + 1) * GT].rearrange("(t p) n -> p t n", p=P),
                                 of[:, h, :, :].bitcast(F32)).then_inc(xn_stored[h], 16)

            load_context(0, 0)
            for n, w in enumerate((wo, gw1)):
                if n:
                    load_x1(0, 0)
                    sp.wait_ge(w_split, n)
                sp.dma_start(stage[:, :, :], w.rearrange("(t p) n -> p t n", p=P)).then_inc(w_in, 16)

            load_context(*following(0, 0))

            def group(b, h):
                if after_next(b, h):
                    load_context(*after_next(b, h))
                if following(b, h):
                    load_x1(*following(b, h))
                stores(b, h)

            over_groups(sp, group)
            sp.wait_ge(relu_set, 4 * NG)
            sp.dma_start(h_sums, hs[:, :, :, :]).then_inc(hs_stored, 16)
            sp.wait_ge(hs_stored, 16)
            sp.wait_ge(x2_stored, 16 * NG)
            for r in range(2):
                sp.wait_ge(xn_stored[r], 32 * NB)

        @block.gpsimd
        def _(pool):
            pool.memset(ident[:, :], 0.0).then_inc(consts_set, 1)
            pool.memset(neghalf[:, :], -0.5).then_inc(consts_set, 1)
            pool.wait_ge(consts_set, 2)
            pool.affine_select(out=ident[:, :], in_=ident[:, :], compare_op=ALU.not_equal, fill=1.0,
                               base=0, pattern=[[-1, P]], channel_multiplier=1).then_inc(consts_set, 1)
            pool.wait_ge(consts_in, 32)

            def add_bias(g):
                pool.wait_ge(x_in, 16 * g + 16)
                wait(pool, x2_set, 4 * g)
                pool.tensor_tensor(x1_b[:, :, :], x1_in[:, :, :],
                                   bo_s[:, :].unsqueeze(1).broadcast_to([P, TT, DIM]), ALU.add).then_inc(biased, 1)

            def norm_scale(g):
                pool.wait_ge(ln_chain, 3 * g + 3)
                wait(pool, xn_set, g)
                pool.tensor_tensor(rstd[:, :], var_eps[:, :], neghalf[:, :], ALU.pow).then_inc(rstd_set, 1)

            add_bias(0)
            norm_scale(0)

            def group(b, h):
                if following(b, h):
                    add_bias(b * GPB + h + 1)
                    norm_scale(b * GPB + h + 1)

            over_groups(pool, group)

        @block.vector
        def _(dve):
            def split_context(g):
                dve.wait_ge(c_hi_set, g + 1)
                wait(dve, o_mm, 4 * g)
                dve.tensor_tensor(ctx_lo[:, :, :], ctx_in[:, :, :], ctx_hi[:, :, :].bitcast(F32), ALU.subtract
                                  ).then_inc(c_lo_set, 1)

            def residual_and_norm(g):
                wait(dve, x2_stored, 16 * g)
                dve.wait_ge(biased, g + 1)
                for u in range(TT):
                    dve.wait_ge(o_mm, 4 * g + u + 1)
                    dve.tensor_tensor(x2_s[:, u, :], bank[u][:, :], x1_b[:, u, :], ALU.add).then_inc(x2_set, 1)
                dve.wait_ge(x2_set, 4 * g + 4)
                moments_of(dve, g, x2_s, TT, DIM, stats, moments, mean, var_eps, stats_set, ln_chain)
                dve.wait_ge(rstd_set, g + 1)
                wait(dve, xt_mm, 4 * g)
                for u in range(TT):
                    i = dve.tensor_scalar(xn[:, u, :], x2_s[:, u, :], mean[:, u:u + 1], rstd[:, u:u + 1],
                                          ALU.subtract, ALU.mult)
                i.then_inc(xn_set, 1)

            def transposed_lo(g, r):
                for u in range(TT):
                    dve.wait_ge(xt_hi_set, 4 * g + u + 1)
                    dve.tensor_tensor(xnt_lo[:, r, :, u * P:(u + 1) * P],
                                      bank[6 + u % 2][:, :].rearrange("p (t n) -> p t n", t=KT),
                                      xnt_hi[:, r, :, u * P:(u + 1) * P].bitcast(F32), ALU.subtract
                                      ).then_inc(xt_lo_set, 1)

            for n in range(2):
                if n:
                    split_context(0)
                dve.wait_ge(w_in, 16 * n + 16)
                dve.tensor_copy(w_hi[n][:, :, :], stage[:, :, :]).then_inc(w_hi_set, 1)
                dve.wait_ge(w_hi_set, n + 1)
                dve.tensor_tensor(w_lo[n][:, :, :], stage[:, :, :], w_hi[n][:, :, :].bitcast(F32), ALU.subtract
                                  ).then_inc(w_split, 1)
            residual_and_norm(0)
            split_context(1)
            transposed_lo(0, 0)

            def group(b, h):
                g = b * GPB + h
                if following(b, h):
                    residual_and_norm(g + 1)
                    if after_next(b, h):
                        split_context(g + 2)
                    transposed_lo(g + 1, (h + 1) % 2)

            over_groups(dve, group)

        @block.scalar
        def _(act):
            def context_hi(g):
                act.wait_ge(c_in, 16 * g + 16)
                wait(act, o_mm, 4 * g)
                act.activation(ctx_hi[:, :, :], ctx_in[:, :, :], ACT.Copy).then_inc(c_hi_set, 1)

            def transposed_hi(b, g, r):
                for u in range(TT):
                    act.wait_ge(xt_mm, 4 * g + u + 1)
                    wait(act, xn_stored[r], 32 * b)
                    act.activation(xnt_hi[:, r, :, u * P:(u + 1) * P],
                                   bank[6 + u % 2][:, :].rearrange("p (t n) -> p t n", t=KT), ACT.Copy
                                   ).then_inc(xt_hi_set, 1)

            context_hi(0)
            context_hi(1)
            transposed_hi(0, 0, 0)
            act.wait_ge(consts_in, 32)

            def group(b, h):
                g = b * GPB + h
                nxt = following(b, h)
                if after_next(b, h):
                    context_hi(g + 2)
                for t in range(KT):
                    act.wait_ge(gate_mm, 4 * g + t + 1)
                    wait(act, relu_set, 4 * g + t - 1)
                    act.activation(relu[:, t % 2, :], bank[4 + t % 2][:, :], ACT.Relu, bias=gb1_s[:, t:t + 1],
                                   accum_out=hs[:, b, h, t:t + 1]).then_inc(relu_set, 1)
                if nxt:
                    transposed_hi(nxt[0], g + 1, nxt[1])

            over_groups(act, group)

        @block.tensor
        def _(pe):
            def product(out, left, right):
                for t in range(KT):
                    for n, (a, b) in enumerate(((0, 0), (0, 1), (1, 0))):
                        i = pe.matmul(out, left(a, t), right(b, t), start=t == 0 and n == 0, stop=t == KT - 1 and n == 2)
                return i

            def project(g):
                pe.wait_ge(c_lo_set, g + 1)
                for u in range(TT):
                    wait(pe, x2_set, 4 * (g - 1) + u + 1)
                    product(bank[u][:, :], lambda a, k: (ctx_hi, ctx_lo)[a][:, k, u * P:(u + 1) * P],
                            lambda a, k: (w_hi, w_lo)[a][0][:, k, :]).then_inc(o_mm, 1)

            def transposes(g):
                pe.wait_ge(xn_set, g + 1)
                for u in range(TT):
                    wait(pe, xt_lo_set, 4 * g + u - 1)
                    for t in range(KT):
                        i = pe.transpose(bank[6 + u % 2][:, t * P:(t + 1) * P], xn[:, u, t * P:(t + 1) * P],
                                         ident[:, :])
                    i.then_inc(xt_mm, 1)

            def gate(g, r):
                pe.wait_ge(xt_lo_set, 4 * g + 4)
                for t in range(KT):
                    wait(pe, relu_set, 4 * g + t - 1)
                    product(bank[4 + t % 2][:, :], lambda a, k: (w_hi, w_lo)[a][1][:, k, t * P:(t + 1) * P],
                            lambda a, k: (xnt_hi, xnt_lo)[a][:, r, k, :]).then_inc(gate_mm, 1)

            pe.wait_ge(consts_set, 3)
            pe.wait_ge(w_split, 1)
            project(0)
            pe.wait_ge(w_split, 2)
            transposes(0)

            def group(b, h):
                g = b * GPB + h
                if following(b, h):
                    project(g + 1)
                gate(g, h)
                if following(b, h):
                    transposes(g + 1)

            over_groups(pe, group)


def modulate_weights(nc, h_sums, gw2, gb2, tw, base, b1, tb1, b2, tb2, mw, mb1, mb2):
    NBLK, E, _, N = tw.shape
    NB, GPB, KT = h_sums.shape[1:]
    FT = b1.shape[1]
    R = P // E
    U = P // R
    PAIRS = U // 2
    RING = 3
    ex = ExitStack()
    with ex:
        sb = lambda name, shape, dt=F32: ex.enter_context(nc.sbuf_tensor("m_" + name, shape, dt))
        sem = semaphores(nc, ex, "m_")
        bank = [ex.enter_context(nc.psum_tensor(f"m_bank{i}", [P, 512], F32)) for i in range(8)]
        hs, hsum, hmean = sb("hs", [P, NB, GPB, KT]), sb("hsum", [P, KT, NB]), sb("hmean", [P, KT, NB])
        gw2_s, gb2_s = sb("gw2", [P, KT, E]), sb("gb2", [E, 1])
        b1_s, tb1_s, b2_s, tb2_s = sb("b1", [P, FT]), sb("tb1", [E, FT * P]), sb("b2", [P, N]), sb("tb2", [E, N])
        ident, expand = sb("ident", [P, P]), sb("expand", [E, P])
        same_row = sb("same_row", [P, R])
        g_s, g_wide, g_col = sb("g", [E, NB]), sb("g_wide", [E, NB, P]), sb("g_col", [P, NB])
        gates = sb("gates", [P, NB, R])
        pick = sb("pick", [P, PAIRS, 2, NB, R])
        mb1_s, mb2_s = sb("mb1", [P, NB, FT]), sb("mb2", [P, NB, N])
        tw_in = sb("tw_in", [P, RING, U, N])
        base_in = sb("base_in", [P, RING, N])
        made = sb("made", [P, 2, PAIRS, N])

        consts_in, consts_set = sem("consts_in"), sem("consts_set")
        g_mm, g_set = sem("g_mm"), sem("g_set")
        picks_set = sem("picks_set")
        bias_mm, bias_set, bias_stored = sem("bias_mm"), sem("bias_set"), sem("bias_stored")
        tw_loaded = [sem(f"tw_loaded{r}") for r in range(RING)]
        made_mm = sem("made_mm")
        act_copied, dve_copied = sem("act_copied"), sem("dve_copied")
        stored = [sem(f"stored{r}") for r in range(2)]
        wait_taken, wait_taken_act = sem("wait_taken"), sem("wait_taken_act")
        block = ex.enter_context(nc.Block())
        HALF = PAIRS // 2
        CONSTS = 7

        @block.sync
        def _(sp):
            sp.dma_start(hs[:, :, :, :], h_sums).then_inc(consts_in, 16)
            sp.dma_start(gw2_s[:, :, :], gw2.rearrange("(t p) e -> p t e", p=P)).then_inc(consts_in, 16)
            sp.dma_start(gb2_s[:, :], gb2).then_inc(consts_in, 16)
            sp.dma_start(b1_s[:, :], b1).then_inc(consts_in, 16)
            sp.dma_start(tb1_s[:, :], tb1).then_inc(consts_in, 16)
            sp.dma_start(b2_s[:, :], b2.unsqueeze(0).broadcast_to([P, N])).then_inc(consts_in, 16)
            sp.dma_start(tb2_s[:, :], tb2).then_inc(consts_in, 16)

            def load(c, r):
                wait(sp, made_mm, PAIRS * (c - RING + 1))
                if not isinstance(c, int):
                    sp.sem_inc(wait_taken, 1)
                sp.dma_start(tw_in[:, r, :, :], tw[c, :, :, :].rearrange("e (r u) n -> (e r) u n", u=U)
                             ).then_inc(tw_loaded[r], 16)
                sp.dma_start(base_in[:, r, :], base[c, :, :]).then_inc(tw_loaded[r], 16)

            for c in range(RING):
                load(c, c)
            with sp.Fori(1, NBLK // RING) as t:
                for r in range(RING):
                    load(t * RING + r, r)
            for c in range(NBLK // RING * RING, NBLK):
                load(c, c % RING)
            sp.wait_ge(bias_set, 1 + NB)
            sp.dma_start(mb1, mb1_s[:, :, :]).then_inc(bias_stored, 16)
            sp.dma_start(mb2.rearrange("b p n -> p b n"), mb2_s[:, :, :]).then_inc(bias_stored, 16)
            sp.wait_ge(bias_stored, 32)
            for r in range(2):
                sp.wait_ge(stored[r], 32 * (NBLK // 2))

        @block.gpsimd
        def _(pool):
            pool.memset(ident[:, :], 0.0).then_inc(consts_set, 1)
            pool.memset(expand[:, :], 1.0).then_inc(consts_set, 1)
            pool.wait_ge(consts_set, 2)
            pool.affine_select(out=ident[:, :], in_=ident[:, :], compare_op=ALU.not_equal, fill=1.0,
                               base=0, pattern=[[-1, P]], channel_multiplier=1).then_inc(consts_set, 1)
            pool.affine_select(out=expand[:, :], in_=expand[:, :], compare_op=ALU.is_ge, fill=0.0,
                               base=0, pattern=[[1, P]], channel_multiplier=-R).then_inc(consts_set, 1)
            pool.wait_ge(consts_set, 4)
            pool.affine_select(out=expand[:, :], in_=expand[:, :], compare_op=ALU.is_ge, fill=0.0,
                               base=R - 1, pattern=[[-1, P]], channel_multiplier=R).then_inc(consts_set, 1)

        @block.vector
        def _(dve):
            dve.wait_ge(consts_set, 5)
            dve.tensor_reduce(same_row[:, :], ident[:, :].rearrange("p (e r) -> p r e", r=R), AX.X, ALU.add
                              ).then_inc(g_set, 1)
            dve.wait_ge(consts_in, 16 * CONSTS)
            dve.tensor_reduce(hsum[:, :, :], hs[:, :, :, :].rearrange("p b h t -> p t b h"), AX.X, ALU.add
                              ).then_inc(g_set, 1)
            dve.wait_ge(g_set, 2)
            dve.tensor_scalar(hmean[:, :, :], hsum[:, :, :], 1.0 / (GPB * 512), None, ALU.mult).then_inc(g_set, 1)
            for j in range(PAIRS):
                for a in range(2):
                    i = dve.tensor_copy(pick[:, j, a, :, :],
                                        ident[:, :].rearrange("p (r u) -> p u r", u=U)[:, 2 * j + a, :]
                                        .unsqueeze(1).broadcast_to([P, NB, R]))
            i.then_inc(picks_set, 1)
            dve.wait_ge(g_mm, 1)
            dve.tensor_scalar(g_s[:, :], bank[0][:E, :NB], gb2_s[:, :], None, ALU.add).then_inc(g_set, 1)
            dve.wait_ge(g_set, 4)
            dve.tensor_copy(g_wide[:, :, :], g_s[:, :].unsqueeze(2).broadcast_to([E, NB, P])).then_inc(g_set, 1)
            dve.wait_ge(g_mm, 2)
            dve.tensor_copy(g_col[:, :], bank[1][:, :NB]).then_inc(g_set, 1)
            dve.wait_ge(g_set, 6)
            dve.tensor_tensor(gates[:, :, :], same_row[:, :].unsqueeze(1).broadcast_to([P, NB, R]),
                              g_col[:, :].unsqueeze(2).broadcast_to([P, NB, R]), ALU.mult).then_inc(g_set, 1)
            dve.wait_ge(bias_mm, 1)
            dve.tensor_tensor(mb1_s[:, :, :], bank[2][:, :NB * FT].rearrange("p (f b) -> p b f", b=NB),
                              b1_s[:, :].unsqueeze(1).broadcast_to([P, NB, FT]), ALU.add).then_inc(bias_set, 1)
            for b in range(NB):
                dve.wait_ge(bias_mm, 2 + b)
                dve.tensor_tensor(mb2_s[:, b, :], bank[3 + b][:, :], b2_s[:, :], ALU.add).then_inc(bias_set, 1)

            def copies(c, k, r):
                wait(dve, stored[r], 32 * k)
                for j in range(1, PAIRS, 2):
                    dve.wait_ge(made_mm, PAIRS * c + j + 1)
                    dve.tensor_copy(made[:, r, j, :], bank[PAIRS * r + j][:, :]).then_inc(dve_copied, 1)

            for r in range(2):
                copies(r, 0, r)
            with dve.Fori(1, NBLK // 2) as t:
                for r in range(2):
                    copies(t * 2 + r, t, r)

        @block.scalar
        def _(act):
            def copies(c, k, r):
                wait(act, stored[r], 32 * k)
                for j in range(0, PAIRS, 2):
                    act.wait_ge(made_mm, PAIRS * c + j + 1)
                    act.activation(made[:, r, j, :], bank[PAIRS * r + j][:, :], ACT.Copy).then_inc(act_copied, 1)
                act.wait_ge(dve_copied, HALF * c + HALF)
                if not isinstance(c, int):
                    act.sem_inc(wait_taken_act, 1)
                act.wait_ge(act_copied, HALF * c + HALF)
                if not isinstance(c, int):
                    act.sem_inc(wait_taken_act, 1)
                for a in range(2):
                    act.dma_start(mw[c, :, :, :].rearrange("b (r j a) n -> a (b r) j n", a=2, j=PAIRS)[a],
                                  made[a * NB * R:(a + 1) * NB * R, r, :, :]).then_inc(stored[r], 16)

            for r in range(2):
                copies(r, 0, r)
            with act.Fori(1, NBLK // 2) as t:
                for r in range(2):
                    copies(t * 2 + r, t, r)

        @block.tensor
        def _(pe):
            pe.wait_ge(g_set, 3)
            for t in range(KT):
                i = pe.matmul(bank[0][:E, :NB], gw2_s[:, t, :], hmean[:, t, :], start=t == 0, stop=t == KT - 1)
            i.then_inc(g_mm, 1)
            pe.wait_ge(g_set, 4)
            pe.matmul(bank[1][:, :NB], expand[:, :], g_s[:, :], start=True, stop=True).then_inc(g_mm, 1)
            for f in range(FT):
                i = pe.matmul(bank[2][:, f * NB:(f + 1) * NB], tb1_s[:, f * P:(f + 1) * P], g_s[:, :],
                              start=True, stop=True)
            i.then_inc(bias_mm, 1)
            pe.wait_ge(g_set, 5)
            for b in range(NB):
                pe.matmul(bank[3 + b][:, :], g_wide[:, b, :], tb2_s[:, :], start=True, stop=True).then_inc(bias_mm, 1)
            pe.wait_ge(g_set, 7)
            pe.wait_ge(bias_set, 1 + NB)
            pe.wait_ge(picks_set, 1)

            def products(c, k, rt, r):
                pe.wait_ge(tw_loaded[rt], 32 * k + 32)
                for j in range(PAIRS):
                    if j % 2:
                        wait(pe, dve_copied, HALF * (c - 2) + j // 2 + 1)
                    else:
                        wait(pe, act_copied, HALF * (c - 2) + j // 2 + 1)
                    out = bank[PAIRS * r + j]
                    pe.matmul(out[:, :], pick[:, j, :, :, :].rearrange("p a b r -> p (a b r)"), base_in[:, rt, :],
                              start=True, stop=False)
                    for a in range(2):
                        rows = slice(a * NB * R, (a + 1) * NB * R)
                        i = pe.matmul(out[rows, :], gates[:, :, :].rearrange("p b r -> p (b r)"),
                                      tw_in[:, rt, 2 * j + a, :], start=False, stop=True)
                    i.then_inc(made_mm, 1)

            BODY = 2 * RING
            for c in range(BODY):
                products(c, c // RING, c % RING, c % 2)
            with pe.Fori(1, NBLK // BODY) as t:
                for c in range(BODY):
                    products(t * BODY + c, t * 2 + c // RING, c % RING, c % 2)
            for c in range(NBLK // BODY * BODY, NBLK):
                products(c, c // RING, c % RING, c % 2)


def feed_forward(nc, xn_hi, xn_lo, x2, mw, mb1, mb2, out):
    NB, DIM, S = xn_hi.shape
    NBLK = mw.shape[0]
    GT = 512
    GPB = S // GT
    KT = DIM // P
    TT = GT // P
    FT = NBLK // 2
    FG = FT // KT
    STEPS = GPB * FT
    ex = ExitStack()
    with ex:
        sb = lambda name, shape, dt=F32: ex.enter_context(nc.sbuf_tensor("f_" + name, shape, dt))
        sem = semaphores(nc, ex, "f_")
        bank = [ex.enter_context(nc.psum_tensor(f"f_bank{i}", [P, 512], F32)) for i in range(8)]
        w_hi, w_lo = sb("w_hi", [P, NBLK, 512], F32R), sb("w_lo", [P, NBLK, 512], F32R)
        stage = sb("stage", [P, 2, 2, 512])
        x_hi, x_lo = sb("x_hi", [P, GPB, KT, GT], F32R), sb("x_lo", [P, GPB, KT, GT], F32R)
        mb1_s, mb2_s = sb("mb1", [P, NB, FT]), sb("mb2", [P, NB, DIM])
        u, u_hi, u_lo = sb("u", [P, 2, GT]), sb("u_hi", [P, 2, GT], F32R), sb("u_lo", [P, 2, GT], F32R)
        x2_s, out_s = sb("x2_s", [P, TT, DIM]), sb("out_s", [P, TT, DIM])

        mb1_in, mb2_in = sem("mb1_in"), sem("mb2_in")
        staged = [sem(f"staged{r}") for r in range(2)]
        w_hi_set, w_set = sem("w_hi_set"), sem("w_set")
        x_in = [sem(f"x_in{h}") for h in range(GPB)]
        x2_in = sem("x2_in")
        x2_biased = sem("x2_biased")
        u_mm, u_set, u_hi_set, u_lo_set = sem("u_mm"), sem("u_set"), sem("u_hi_set"), sem("u_lo_set")
        o_mm = sem("o_mm")
        out_set = sem("out_set")
        out_stored = sem("out_stored")
        wait_taken, wait_taken_act, wait_taken_pool = sem("wait_taken"), sem("wait_taken_act"), sem("wait_taken_pool")
        block = ex.enter_context(nc.Block())

        def over_batches(eng, batch):
            batch(0)
            with eng.Fori(1, NB - 1) as b:
                batch(b)
            batch(NB - 1)

        def more(b):
            return not isinstance(b, int) or b + 1 < NB

        @block.sync
        def _(sp):
            def taken(b):
                if not isinstance(b, int):
                    sp.sem_inc(wait_taken, 1)

            def load_unit(b, fg, k):
                wait(sp, w_set, FT * b + KT * fg + k - 1)
                taken(b)
                first = 2 * (KT * fg + k)
                sp.dma_start(stage[:, k % 2, :, :], mw[first:first + 2, b, :, :].rearrange("a p n -> p a n")
                             ).then_inc(staged[k % 2], 16)

            def load_x(b, h):
                wait(sp, u_mm, STEPS * (b - 1) + FT * (h + 1))
                taken(b)
                for part, to in ((xn_hi, x_hi), (xn_lo, x_lo)):
                    sp.dma_start(to[:, h, :, :].bitcast(F32),
                                 part[b, :, h * GT:(h + 1) * GT].rearrange("(t p) n -> p t n", p=P)
                                 ).then_inc(x_in[h], 16)

            def load_x2(b, h):
                wait(sp, out_set, TT * (GPB * b + h))
                taken(b)
                sp.dma_start(x2_s[:, :, :], x2[b, h * GT:(h + 1) * GT, :].rearrange("(u p) d -> p u d", p=P)
                             ).then_inc(x2_in, 16)

            def store(b, h):
                sp.wait_ge(out_set, TT * (GPB * b + h) + TT)
                taken(b)
                sp.dma_start(out[b, h * GT:(h + 1) * GT, :].rearrange("(u p) d -> p u d", p=P), out_s[:, :, :]
                             ).then_inc(out_stored, 16)

            for fg in range(FG - 1):
                for k in range(KT):
                    load_unit(0, fg, k)
                    if (fg, k) == (0, 1):
                        load_x(0, 0)
                        sp.dma_start(mb1_s[:, :, :], mb1).then_inc(mb1_in, 16)
                    if (fg, k) == (0, 3):
                        sp.dma_start(mb2_s[:, :, :], mb2.rearrange("b p n -> p b n")).then_inc(mb2_in, 16)

            def batch(b):
                for k in range(KT):
                    load_unit(b, FG - 1, k)
                for h in range(GPB):
                    if h + 1 < GPB:
                        load_x(b, h + 1)
                    load_x2(b, h)
                    if h + 1 == GPB and more(b):
                        load_x(b + 1, 0)
                        for fg in range(FG - 1):
                            for k in range(KT):
                                load_unit(b + 1, fg, k)
                    store(b, h)

            over_batches(sp, batch)
            sp.wait_ge(out_stored, 16 * NB * GPB)

        @block.gpsimd
        def _(pool):
            pool.wait_ge(mb2_in, 16)

            def batch(b):
                for h in range(GPB):
                    pool.wait_ge(x2_in, 16 * (GPB * b + h) + 16)
                    pool.sem_inc(wait_taken_pool, 1)
                    pool.tensor_tensor(x2_s[:, :, :], x2_s[:, :, :],
                                       mb2_s[:, b, :].unsqueeze(1).broadcast_to([P, TT, DIM]), ALU.add
                                       ).then_inc(x2_biased, 1)

            over_batches(pool, batch)

        @block.vector
        def _(dve):
            def split_unit(b, fg, k):
                n = FT * b + KT * fg + k
                dve.wait_ge(staged[k % 2], 16 * (FT // 2 * b + KT // 2 * fg + k // 2) + 16)
                wait(dve, o_mm, TT * (STEPS * b - FT + KT * fg + KT))
                part = slice(2 * (KT * fg + k), 2 * (KT * fg + k) + 2)
                dve.tensor_copy(w_hi[:, part, :], stage[:, k % 2, :, :]).then_inc(w_hi_set, 1)
                dve.wait_ge(w_hi_set, n + 1)
                dve.tensor_tensor(w_lo[:, part, :], stage[:, k % 2, :, :], w_hi[:, part, :].bitcast(F32),
                                  ALU.subtract).then_inc(w_set, 1)

            def split_hidden(b, c):
                s = STEPS * b + c
                dve.wait_ge(u_hi_set, s + 1)
                dve.tensor_tensor(u_lo[:, c % 2, :], u[:, c % 2, :], u_hi[:, c % 2, :].bitcast(F32), ALU.subtract
                                  ).then_inc(u_lo_set, 1)

            def finish(b, h):
                g = GPB * b + h
                dve.wait_ge(x2_biased, g + 1)
                wait(dve, out_stored, 16 * g)
                for t in range(TT):
                    dve.wait_ge(o_mm, TT * (FT * g + FT - 1) + t + 1)
                    dve.tensor_tensor(out_s[:, t, :], bank[t][:, :], x2_s[:, t, :], ALU.add).then_inc(out_set, 1)

            for k in range(KT):
                split_unit(0, 0, k)

            def batch(b):
                for c in range(STEPS):
                    h, ft = divmod(c, FT)
                    split_hidden(b, c)
                    if ft == 0 and h:
                        finish(b, h - 1)
                    elif ft == 0 and (not isinstance(b, int) or b):
                        finish(b - 1, GPB - 1)
                    if h == 0 and isinstance(b, int) and b == 0:
                        if ft < FT - KT:
                            split_unit(0, 1 + ft // KT, ft % KT)
                    elif h == 0 and ft < KT:
                        split_unit(b, FG - 1, ft)
                    if h == GPB - 1 and ft >= KT and more(b):
                        split_unit(b + 1, ft // KT - 1, ft % KT)

            over_batches(dve, batch)
            finish(NB - 1, GPB - 1)

        @block.scalar
        def _(act):
            act.wait_ge(mb1_in, 16)

            def batch(b):
                for c in range(STEPS):
                    s, ft = STEPS * b + c, c % FT
                    act.wait_ge(u_mm, s + 1)
                    wait(act, u_lo_set, s - 1)
                    act.sem_inc(wait_taken_act, 1)
                    act.activation(u[:, c % 2, :], bank[4 + c % 4][:, :], ACT.Gelu_apprx_tanh,
                                   bias=mb1_s[:, b, ft:ft + 1]).then_inc(u_set, 1)
                    act.wait_ge(u_set, s + 1)
                    wait(act, o_mm, TT * (s - 1))
                    act.activation(u_hi[:, c % 2, :], u[:, c % 2, :], ACT.Copy).then_inc(u_hi_set, 1)

            over_batches(act, batch)

        @block.tensor
        def _(pe):
            PARTS = ((0, 0), (0, 1), (1, 0))

            def hidden(b, c):
                s = STEPS * b + c
                h, ft = divmod(c, FT)
                if ft == 0:
                    pe.wait_ge(x_in[h], 32 * b + 32)
                if h == 0 and ft % KT == 0:
                    pe.wait_ge(w_set, FT * b + ft + KT)
                wait(pe, u_set, s - 3)
                for k in range(KT):
                    for n, (wp, xp) in enumerate(PARTS):
                        i = pe.matmul(bank[4 + c % 4][:, :],
                                      (w_hi, w_lo)[wp][:, 2 * (ft // KT * KT + k), ft % KT * P:(ft % KT + 1) * P],
                                      (x_hi, x_lo)[xp][:, h, k, :], start=k == 0 and n == 0, stop=k == KT - 1 and n == 2)
                i.then_inc(u_mm, 1)

            def output(b, c):
                s = STEPS * b + c
                ft = c % FT
                pe.wait_ge(u_lo_set, s + 1)
                for t in range(TT):
                    if ft == 0:
                        wait(pe, out_set, TT * (GPB * b + c // FT - 1) + t + 1)
                    for n, (up, wp) in enumerate(PARTS):
                        i = pe.matmul(bank[t][:, :], (u_hi, u_lo)[up][:, c % 2, t * P:(t + 1) * P],
                                      (w_hi, w_lo)[wp][:, 2 * ft + 1, :], start=ft == 0 and n == 0,
                                      stop=ft == FT - 1 and n == 2)
                    i.then_inc(o_mm, 1)

            hidden(0, 0)

            def batch(b):
                for c in range(STEPS):
                    if c + 1 < STEPS:
                        hidden(b, c + 1)
                    elif more(b):
                        hidden(b + 1, 0)
                    output(b, c)

            over_batches(pe, batch)


def decoder_layer(nc, x, ctx_t, mask, wq, wk, wv, wlb, wo, w0, xwq, xwk, xwv, bq, bk, bv, xwo, bo, gw1, gb1, gw2, gb2,
                  tw, base, b1, tb1, b2, tb2, out):
    NB, S, DIM = x.shape
    dram = lambda name, *shape: nc.dram_tensor(name, shape, F32).ap()
    x1 = dram("x1", NB, S, DIM)
    scan_attention(nc, x, wq, wk, wv, wlb, wo, w0, x1)
    q_hi, q_lo, k_hi, k_lo = (dram(n, NB, DIM, S) for n in ("q_hi", "q_lo", "k_hi", "k_lo"))
    v = dram("v", NB, S, DIM)
    cross_projections(nc, x1, ctx_t, mask, xwq, xwk, xwv, bq, bk, bv, q_hi, q_lo, k_hi, k_lo, v)
    attended = dram("attended", NB, DIM, S)
    cross_attention(nc, q_hi, q_lo, k_hi, k_lo, v, mask, dram("m_rows", 2, 4, S), attended)
    x2 = dram("x2", NB, S, DIM)
    xn_hi, xn_lo, h_sums = dram("xn_hi", NB, DIM, S), dram("xn_lo", NB, DIM, S), dram("h_sums", P, NB, 2, DIM // P)
    output_projection_and_gate(nc, attended, x1, xwo, bo, gw1, gb1, x2, xn_hi, xn_lo, h_sums)
    mw, mb1, mb2 = dram("mw", tw.shape[0], NB, P, DIM), dram("mb1", P, NB, b1.shape[1]), dram("mb2", NB, P, DIM)
    modulate_weights(nc, h_sums, gw2, gb2, tw, base, b1, tb1, b2, tb2, mw, mb1, mb2)
    feed_forward(nc, xn_hi, xn_lo, x2, mw, mb1, mb2, out)


def _layouts(i):
    import numpy as np

    a = {k: np.asarray(v) for k, v in i.items()}
    t = lambda name: a[name].T
    columns = lambda name: a[name].reshape(-1, P).T

    def by_blocks(w1, w2):
        e, f, h = w1.shape
        parts, units = f // 512, h // P
        b1 = w1.reshape(e, parts, 512, units, P).transpose(1, 3, 0, 4, 2)
        b2 = w2.reshape(e, h, parts, units, P).transpose(2, 3, 0, 4, 1)
        return np.stack([b1, b2], 2).reshape(parts * units * 2, e, P, 512)

    w_in, w_out = a["L0_attn_W_in_init"][0], a["L0_attn_W_out_init"][0]
    heads, d = w_in.shape[1], w_in.shape[0]
    w0 = np.stack([w_in.transpose(1, 2, 0), w_out.transpose(1, 2, 0), w_out.transpose(1, 0, 2)])
    return {
        "x": a["x"], "ctx_t": a["ctx_1024"].transpose(0, 2, 1), "mask": a["mask_BxS2_if1"],
        "wq": t("L0_attn_Wq"), "wk": t("L0_attn_Wk"), "wv": t("L0_attn_Wv"),
        "wlb": np.concatenate([a["L0_attn_Wlr"], a["L0_attn_Wbeta"]], 0).T, "wo": t("L0_attn_Wo"),
        "w0": w0.reshape(3, heads // 2, 2, d, d).transpose(0, 2, 3, 1, 4).reshape(3, 2 * d, heads // 2, d),
        "xwq": t("L0_xattn_W_q"), "xwk": t("L0_xattn_W_k"), "xwv": t("L0_xattn_W_v"),
        "bq": columns("L0_xattn_b_q"), "bk": columns("L0_xattn_b_k"), "bv": a["L0_xattn_b_v"],
        "xwo": t("L0_xattn_W_o"), "bo": a["L0_xattn_b_o"],
        "gw1": t("L0_ffn_gate_w1"), "gb1": columns("L0_ffn_gate_b1"),
        "gw2": t("L0_ffn_gate_w2"), "gb2": a["L0_ffn_gate_b2"].reshape(-1, 1),
        "tw": by_blocks(a["L0_ffn_TW1"], a["L0_ffn_TW2"]),
        "base": by_blocks(a["L0_ffn_W1"][None], a["L0_ffn_W2"][None])[:, 0],
        "b1": columns("L0_ffn_b1"), "tb1": a["L0_ffn_Tb1"], "b2": a["L0_ffn_b2"], "tb2": a["L0_ffn_Tb2"],
    }


def kernel(**inputs):
    import numpy as _np
    import concourse.bacc as _bacc
    from concourse import mybir as _mybir
    from concourse.bass_utils import run_bass_kernel_spmd as _run

    nc = _bacc.Bacc("TRN2", target_bir_lowering=False, num_devices=1)
    arrays, args = {}, []
    for name, a in _layouts(inputs).items():
        a = _np.ascontiguousarray(a)
        arrays[f"in_{name}"] = a
        args.append(nc.dram_tensor(f"in_{name}", a.shape, _mybir.dt.from_np(a.dtype), kind="ExternalInput").ap())
    shape = inputs["x"].shape
    args.append(nc.dram_tensor("out", shape, F32, kind="ExternalOutput").ap())
    decoder_layer(nc, *args)
    r = _run(nc, [arrays], core_ids=[0])
    return r.results[0]["out"]
```

```python
from contextlib import ExitStack

import concourse.bass as bass
from concourse import mybir

P = 128
F32 = mybir.dt.float32
F32R = mybir.dt.float32r
I32 = mybir.dt.int32
ALU = mybir.AluOpType
ACT = mybir.ActivationFunctionType
AX = mybir.AxisListType

EPS = 1e-5
CH = 64
BASE_LR = 0.001
BASE_WD = 0.9


def semaphores(nc, ex, prefix):
    held = []

    def sem(name):
        held.append(nc.alloc_semaphore(prefix + name))
        return held[-1]

    def give_back():
        nc.clear_and_free_semaphores(held)
        nc.all_engine_barrier()

    ex.callback(give_back)
    return sem


def wait(eng, s, value):
    if not isinstance(value, int) or value > 0:
        eng.wait_ge(s, value)


def scan_attention(nc, x, wq, wk, wv, wlb, w0, o_t):
    NB, L, DIM = x.shape
    NCH = L // CH
    KT = DIM // P
    NJ = wq.shape[1] // P
    TOK = NB * CH
    NT = TOK // P
    H = 2 * NJ
    ex = ExitStack()
    with ex:
        sb = lambda name, shape, dt=F32: ex.enter_context(nc.sbuf_tensor(name, shape, dt))
        sem = semaphores(nc, ex, "")
        bank = [ex.enter_context(nc.psum_tensor(f"a_bank{i}", [P, 512], F32)) for i in range(8)]

        (wq_hi, wq_lo), (wk_hi, wk_lo), (wv_hi, wv_lo) = (
            [sb(f"a_{n}_{part}", [P, KT, NJ * P], F32R) for part in ("hi", "lo")] for n in ("wq", "wk", "wv"))
        wlb_hi, wlb_lo = (sb(n, [P, KT, 4 * H], F32R) for n in ("a_wlb_hi", "a_wlb_lo"))
        win_t, wout_t, wout = (sb(n, [P, NJ, NB, P]) for n in ("a_win_t", "a_wout_t", "a_wout"))
        staged = [w[:, :, :, :].rearrange("p j b n -> p (j b n)").rearrange("p (t n) -> p t n", t=KT)
                  for w in (win_t, wout_t, wout)]
        ident = sb("a_ident", [P, P])
        meansel = sb("a_meansel", [P, 2, P])
        neghalf = sb("a_neghalf", [P, NT])
        xin = sb("a_xin", [P, NT, DIM])
        stats, mean, rstd = sb("a_stats", [P, NT, 6]), sb("a_mean", [P, NT]), sb("a_rstd", [P, NT])
        moments = sb("a_moments", [P, 5, NT])
        var_eps = sb("a_var_eps", [P, NT])
        xnt_hi, xnt_lo = (sb(n, [P, KT, TOK], F32R) for n in ("a_xnt_hi", "a_xnt_lo"))
        gates = sb("a_gates", [P, NT, 4 * H])
        coef_next, coef = (sb(n, [P, 4, NJ, NB]) for n in ("a_coef_next", "a_coef"))
        qk = sb("a_qk", [P, 2, 2, NB, CH])
        tanh_qk = qk[:, :, :, :, :].rearrange("p r t b n -> p r t (b n)")
        vt = sb("a_vt", [P, 4, TOK])
        kvtok = sb("a_kvtok", [P, 4, 2, NT, P])
        winit = (kvtok[:, :, :, :, :].rearrange("p r t u n -> p (r t u n)")[:, 0:3 * NJ * 64]
                 .rearrange("p (m j b) -> p m j b", m=3, j=NJ))
        zs = sb("a_zs", [P, 2, 2 * NB, CH])
        ez = zs[:, :, :, :].rearrange("p r (t b) n -> p r t b n", t=2)
        pr = sb("a_pr", [P, 2, 2, NB, CH])
        zmax, zsum, zinv = (sb(n, [P, 2, NB * 2]) for n in ("a_zmax", "a_zsum", "a_zinv"))
        pt = sb("a_pt", [P, 2, NT, 2, 64])
        wlb_s = pt[:, :, :, :, :].rearrange("p r u g f -> p (r u g f)")[:, 0:KT * 4 * H].rearrange("p (t n) -> p t n", t=KT)
        pt_bd, gz_bd = (sb(n, [P, 2, NT, 2, 2, 64]) for n in ("a_pt_bd", "a_gz_bd"))
        pa, ps_ = (sb(n, [P, 2, NT, 2, 64]) for n in ("a_pa", "a_ps"))
        ssum = sb("a_ssum", [P, 2, NT * 2])
        decayed = sb("a_decayed", [P, 2, 2, NB, 64])
        step = sb("a_step", [P, 2, NB, 64])
        ot = sb("a_ot", [P, 2, TOK])

        B_QK, B_VO, B_Z, B_KV, B_PT, B_A, B_G, B_X = range(8)
        ps_qk = bank[B_QK][:, :].rearrange("p (t n) -> p t n", t=2)
        ps_v, ps_o = bank[B_VO][:, 0:TOK], bank[B_VO][:, TOK:2 * TOK]
        ps_z = bank[B_Z][:, :].rearrange("p (b n) -> p b n", n=CH)
        ps_kv = bank[B_KV][:, :].rearrange("p (t u f) -> p t u f", t=2, u=NT)
        ps_wt = bank[B_KV][:, :].rearrange("p (b f) -> p b f", b=NB)
        ps_pt = bank[B_PT][:, 0:NT * P].rearrange("p (u g f) -> p u g f", u=NT, g=2)
        ps_a = bank[B_A][:, 0:NT * P].rearrange("p (u g f) -> p u g f", u=NT, g=2)
        ps_g = bank[B_G][:, :].rearrange("p (m b f) -> p m b f", m=2, b=NB)
        ps_x = bank[B_X]

        wlb_in, wq_in, wk_in, wv_in = (sem(f"a_{n}_in") for n in ("wlb", "wq", "wk", "wv"))
        w_hi_set, w_lo_set = sem("a_w_hi_set"), sem("a_w_lo_set")
        consts_set = sem("a_consts_set")
        states_clear, states_set = sem("a_states_clear"), sem("a_states_set")
        winit_in = sem("a_winit_in")
        x_in = sem("a_x_in")
        o_stored = [sem(f"a_o_stored{r}") for r in range(2)]
        wait_taken = sem("a_wait_taken")
        stats_set = sem("a_stats_set")
        ln_chain = sem("a_ln_chain")
        rstd_set = sem("a_rstd_set")
        xn_set = sem("a_xn_set")
        xt_mm, xt_hi_set, xt_lo_set = sem("a_xt_mm"), sem("a_xt_hi_set"), sem("a_xt_lo_set")
        gate_mm, gate_set = sem("a_gate_mm"), sem("a_gate_set")
        mean_mm, mean_evac = sem("a_mean_mm"), sem("a_mean_evac")
        coef_set = sem("a_coef_set")
        qk_mm, v_mm, z_mm, kv_mm = sem("a_qk_mm"), sem("a_v_mm"), sem("a_z_mm"), sem("a_kv_mm")
        o_mm, a_mm, pt_mm, g_mm, wt_mm = (sem(f"a_{n}") for n in ("o_mm", "a_mm", "pt_mm", "g_mm", "wt_mm"))
        tanh_set, v_evac, kv_evac, e_set = (sem(f"a_{n}") for n in ("tanh_set", "v_evac", "kv_evac", "e_set"))
        pt_evac, o_evac, wt_evac = (sem(f"a_{n}") for n in ("pt_evac", "o_evac", "wt_evac"))
        qk_set, zmax_set, zs_set, zsum_set, zinv_set = (
            sem(f"a_{n}") for n in ("qk_set", "zmax_set", "zs_set", "zsum_set", "zinv_set"))
        pa_set, ssum_set = sem("a_pa_set"), sem("a_ssum_set")
        step_set = sem("a_step_set")
        w_set = sem("a_w_set")
        pr_set, ps_set, gz_set = (sem(f"a_{n}") for n in ("pr_set", "ps_set", "gz_set"))
        decayed_set = sem("a_decayed_set")

        block = ex.enter_context(nc.Block())
        halves = ((0, slice(0, 64)), (1, slice(64, 128)))

        LEARNING = (NCH - 1) * NJ

        KV_SLOTS, TOKEN_KV_SLOTS = LEARNING + 3, LEARNING + 1

        def before(s, top):
            return not isinstance(s, int) or s < top

        def clip(value, top):
            return min(value, top) if isinstance(value, int) else value

        def over_slots(eng, slot):
            for j in range(NJ):
                slot(0, j)
            with eng.Fori(1, NCH - 1) as c:
                for j in range(NJ):
                    slot(c, j)
            for j in range(NJ):
                slot(NCH - 1, j)

        def exists(c, j):
            return not isinstance(c, int) or 0 <= c * NJ + j < NCH * NJ

        def learns(c, j):
            return not isinstance(c, int) or 0 <= c * NJ + j < LEARNING

        @block.sync
        def _(sp):

            def load_xin(c):
                wait(sp, xt_mm, 2 * c)
                for b in range(NB):
                    sp.dma_start(xin[64 * (b % 2):64 * (b % 2) + 64, b // 2, :], x[b, bass.ds(c * CH, CH), :]
                                 ).then_inc(x_in, 16)

            def store(c, j):
                sp.wait_ge(o_evac, c * NJ + j + 1)
                sp.sem_inc(wait_taken, 1)
                sp.dma_start(o_t[j, :, c, :], ot[:, j % 2, :]).then_inc(o_stored[j % 2], 16)

            load_xin(0)
            sp.dma_start(winit[:, :, :, :], w0.rearrange("m p j b -> p m j b")).then_inc(winit_in, 16)
            sp.dma_start(wlb_s[:, :, :], wlb.rearrange("(t p) n -> p t n", p=P)).then_inc(wlb_in, 16)
            for to, w, loaded in zip(staged, (wq, wk, wv), (wq_in, wk_in, wv_in)):
                sp.dma_start(to, w.rearrange("(t p) n -> p t n", p=P)).then_inc(loaded, 16)

            def chunk(c):
                if exists(c, NJ):
                    load_xin(c + 1)
                for j in range(NJ):
                    store(c, j)

            chunk(0)
            with sp.Fori(1, NCH - 1) as c:
                chunk(c)
            chunk(NCH - 1)
            for r in range(2):
                sp.wait_ge(o_stored[r], 16 * NCH * NJ // 2)

        @block.gpsimd
        def _(pool):
            def norm_scale(c):
                pool.wait_ge(ln_chain, 3 * c + 3)
                wait(pool, xn_set, c)
                pool.tensor_tensor(rstd[:, :], var_eps[:, :], neghalf[:, :], ALU.pow).then_inc(rstd_set, 1)

            def decay(c, s, jj, r):
                wait(pool, w_set, 4 * (s - 1))
                pool.wait_ge(states_set, 6)
                pool.wait_ge(coef_set, c + 1)
                wait(pool, pr_set, s + 1)
                for g, half in halves:
                    if g == 1:
                        pool.wait_ge(decayed_set, 4 * s + 2)
                    for m, w in ((0, win_t), (1, wout_t)):
                        pool.tensor_tensor(
                            decayed[half, r, m, :, :], w[half, jj, :, 64 * g:64 * g + 64],
                            coef[half, 2 + m, jj, :].unsqueeze(2).broadcast_to([64, NB, 64]),
                            ALU.mult).then_inc(decayed_set, 1)

            def score_gradient(s, r):
                pool.wait_ge(ssum_set, s + 1)
                wait(pool, gz_set, 2 * s)
                wait(pool, decayed_set, 4 * s)
                pool.tensor_tensor(ps_[:, r, :, :, :], pt[:, r, :, :, :],
                                   ssum[:, r, :].rearrange("p (u g) -> p u g", u=NT).unsqueeze(3)
                                   .broadcast_to([P, NT, 2, 64]), ALU.mult).then_inc(ps_set, 1)
                pool.wait_ge(ps_set, s + 1)
                wait(pool, g_mm, s - 1)
                for g, half in halves:
                    if g == 1:
                        pool.wait_ge(gz_set, 2 * s + 1)
                    pool.tensor_tensor(gz_bd[half, r, :, :, g, :], ps_[half, r, :, :, :],
                                       pa[half, r, :, :, :], ALU.subtract).then_inc(gz_set, 1)

            def probabilities(s, r):
                pool.wait_ge(zinv_set, s + 1)
                wait(pool, o_mm, s - 1)
                wait(pool, pt_mm, clip(s - 1, LEARNING))
                wait(pool, gz_set, 2 * clip(s, LEARNING))
                pool.tensor_tensor(pr[:, r, :, :, :], ez[:, r, :, :, :],
                                   zinv[:, r, :].rearrange("p (t b) -> p t b", t=2).unsqueeze(3)
                                   .broadcast_to([P, 2, NB, CH]), ALU.mult).then_inc(pr_set, 1)

            def slot(c, j):
                if learns(c, j - 1):
                    decay(c if j else c - 1, c * NJ + j - 1, (j - 1) % NJ, (j - 1) % 2)
                if learns(c, j):
                    score_gradient(c * NJ + j, j % 2)
                if exists(c, j + 1):
                    probabilities(c * NJ + j + 1, (j + 1) % 2)
                if j == 2 and exists(c, NJ):
                    norm_scale(c + 1)

            pool.memset(ident[:, :], 0.0).then_inc(consts_set, 1)
            pool.memset(neghalf[:, :], -0.5).then_inc(consts_set, 1)
            pool.memset(meansel[:, :, :], 0.0).then_inc(consts_set, 1)
            pool.wait_ge(consts_set, 3)
            pool.affine_select(out=ident[:, :], in_=ident[:, :], compare_op=ALU.not_equal, fill=1.0,
                               base=0, pattern=[[-1, P]], channel_multiplier=1).then_inc(consts_set, 1)
            norm_scale(0)
            pool.memset(pt_bd[:, :, :, :, :, :], 0.0).then_inc(consts_set, 1)
            pool.memset(gz_bd[:, :, :, :, :, :], 0.0).then_inc(consts_set, 1)
            for h, half in halves:
                pool.wait_ge(consts_set, 6 + h)
                pool.memset(meansel[half, h, :], 1.0 / CH).then_inc(consts_set, 1)
            pool.wait_ge(consts_set, 8)
            probabilities(0, 0)
            over_slots(pool, slot)

        @block.vector
        def _(dve):
            def norm(c, u):
                dve.wait_ge(x_in, 64 * c + 64)
                dve.bn_stats(stats[:, u, :], xin[:, u, :]).then_inc(stats_set, 1)

            def moments_of_chunk(c):
                dve.wait_ge(stats_set, NT * c + NT)
                dve.tensor_tensor(moments[:, 0, :], stats[:, :, 1], stats[:, :, 4], ALU.add)
                dve.tensor_tensor(moments[:, 1, :], stats[:, :, 1], stats[:, :, 4], ALU.subtract)
                dve.tensor_tensor(moments[:, 2, :], stats[:, :, 2], stats[:, :, 5], ALU.add).then_inc(ln_chain, 1)
                dve.wait_ge(ln_chain, 3 * c + 1)
                dve.tensor_scalar(mean[:, :], moments[:, 0, :], 0.5, None, ALU.mult)
                dve.scalar_tensor_tensor(out=moments[:, 3, :], in0=moments[:, 1, :], scalar=0.25,
                                         in1=moments[:, 1, :], op0=ALU.mult, op1=ALU.mult)
                dve.tensor_scalar(moments[:, 4, :], moments[:, 2, :], 1.0 / DIM, EPS, ALU.mult, ALU.add
                                  ).then_inc(ln_chain, 1)
                dve.wait_ge(ln_chain, 3 * c + 2)
                dve.tensor_tensor(var_eps[:, :], moments[:, 3, :], moments[:, 4, :], ALU.add).then_inc(ln_chain, 1)

            def normed(c):
                dve.wait_ge(rstd_set, c + 1)
                for u in range(NT):
                    i = dve.tensor_scalar(xin[:, u, :], xin[:, u, :], mean[:, u:u + 1], rstd[:, u:u + 1],
                                          ALU.subtract, ALU.mult)
                i.then_inc(xn_set, 1)

            def silu(s, r):
                dve.wait_ge(tanh_set, s + 1)
                dve.scalar_tensor_tensor(
                    out=qk[:, r, :, :, :].rearrange("p t b n -> p (t b n)"),
                    in0=tanh_qk[:, r, :, :].rearrange("p t n -> p (t n)"), scalar=1.0,
                    in1=bank[B_QK][:, :], op0=ALU.add, op1=ALU.mult).then_inc(qk_set, 1)

            def scores(s, r):
                dve.wait_ge(z_mm, s + 1)
                wait(dve, zs_set, s - 1)
                dve.tensor_reduce(zmax[:, r, :], ps_z, AX.X, ALU.max).then_inc(zmax_set, 1)
                dve.wait_ge(zmax_set, s + 1)
                wait(dve, zsum_set, s - 1)
                wait(dve, pr_set, s - 1)
                dve.tensor_tensor(zs[:, r, :, :], ps_z, zmax[:, r, :].unsqueeze(2).broadcast_to([P, 2 * NB, CH]),
                                  ALU.subtract).then_inc(zs_set, 1)

            def sums(s, r):
                dve.wait_ge(e_set, s + 1)
                wait(dve, pr_set, s - 1)
                dve.tensor_reduce(zsum[:, r, :], ez[:, r, :, :, :].rearrange("p t b n -> p (t b) n"),
                                  AX.X, ALU.add).then_inc(zsum_set, 1)
                dve.wait_ge(zsum_set, s + 1)
                dve.reciprocal(zinv[:, r, :], zsum[:, r, :]).then_inc(zinv_set, 1)

            def coefficients(c):
                dve.wait_ge(mean_mm, c + 1)
                wait(dve, coef_set, c)
                for g, half in halves:
                    src = ps_x[half, 0:NB * 4 * H].rearrange("p (b m j g) -> p g m j b", b=NB, m=4, g=2)
                    for m, c0 in enumerate((0.5 * BASE_LR, BASE_LR, BASE_WD, BASE_WD)):
                        i = dve.tensor_scalar(coef_next[half, m, :, :], src[:, g, m, :, :], 0.5 * c0, 0.5 * c0,
                                              ALU.mult, ALU.add)
                i.then_inc(mean_evac, 1)

            def inner_products(s, r):
                dve.wait_ge(a_mm, s + 1)
                dve.wait_ge(pt_evac, 3 * s + 3)
                wait(dve, gz_set, 2 * (s - 1))
                dve.tensor_tensor(pa[:, r, :, :, :], ps_a, pt[:, r, :, :, :], ALU.mult).then_inc(pa_set, 1)
                dve.wait_ge(pa_set, s + 1)
                dve.tensor_reduce(ssum[:, r, :], pa[:, r, :, :, :].rearrange("p u g f -> p (u g) f"),
                                  AX.X, ALU.add).then_inc(ssum_set, 1)

            def next_coefficients(c):
                wait(dve, decayed_set, 4 * NJ * c)
                dve.wait_ge(mean_evac, c + 1)
                dve.tensor_copy(coef[:, :, :, :], coef_next[:, :, :, :]).then_inc(coef_set, 1)
                dve.wait_ge(coef_set, c + 1)

            def update(s, jj, r):
                dve.wait_ge(g_mm, s + 1)
                wait(dve, w_set, 4 * s)
                for m in range(2):
                    dve.tensor_tensor(step[:, m, :, :], ps_g[:, m, :, :],
                                      coef[:, m, jj, :].unsqueeze(2).broadcast_to([P, NB, 64]), ALU.mult
                                      ).then_inc(step_set, 1)
                dve.wait_ge(step_set, 2 * s + 2)
                dve.wait_ge(decayed_set, 4 * s + 4)
                for m, w, op in ((0, win_t, ALU.subtract), (1, wout_t, ALU.add)):
                    for g, half in halves:
                        dve.tensor_tensor(w[half, jj, :, 64 * g:64 * g + 64], decayed[half, r, m, :, :],
                                          step[half, m, :, :], op).then_inc(w_set, 1)

            def x_transposed_lo(c, u):
                dve.wait_ge(xt_hi_set, 2 * c + u + 1)
                dve.tensor_tensor(xnt_lo[:, :, u * P:u * P + P], ps_x[:, :].rearrange("p (t n) -> p t n", t=KT),
                                  xnt_hi[:, :, u * P:u * P + P].bitcast(F32), ALU.subtract).then_inc(xt_lo_set, 1)

            def weights_lo(n, of, hi, lo):
                dve.wait_ge(w_hi_set, n + 1)
                dve.tensor_tensor(lo[:, :, :], of, hi[:, :, :].bitcast(F32), ALU.subtract).then_inc(w_lo_set, 1)

            def slot(c, j):
                if exists(c, j + 1):
                    scores(c * NJ + j + 1, (j + 1) % 2)
                if j == 5 and exists(c, NJ):
                    x_transposed_lo(c + 1, 0)
                if learns(c, j):
                    inner_products(c * NJ + j, j % 2)
                if j == 5 and exists(c, NJ):
                    x_transposed_lo(c + 1, 1)
                if learns(c, j - 1):
                    update(c * NJ + j - 1, (j - 1) % NJ, (j - 1) % 2)
                if exists(c, j + 1):
                    sums(c * NJ + j + 1, (j + 1) % 2)
                if j == 0 and learns(c, 0):
                    next_coefficients(c)
                if j == 7 and exists(c, NJ):
                    coefficients(c + 1)
                if exists(c, j + 3):
                    silu(c * NJ + j + 3, (j + 3) % 2)
                if j < NT and exists(c, NJ):
                    norm(c + 1, j)
                if j == 1 and exists(c, NJ):
                    moments_of_chunk(c + 1)
                if j == 3 and exists(c, NJ):
                    normed(c + 1)

            for u in range(NT):
                norm(0, u)
            moments_of_chunk(0)
            normed(0)
            x_transposed_lo(0, 0)
            x_transposed_lo(0, 1)
            weights_lo(0, wlb_s[:, :, :], wlb_hi, wlb_lo)
            for n, (hi, lo) in enumerate(((wq_hi, wq_lo), (wk_hi, wk_lo), (wv_hi, wv_lo))):
                weights_lo(n + 1, staged[n], hi, lo)
                if n == 2:
                    coefficients(0)
                    silu(0, 0)
                w = (win_t, wout_t, wout)[n]
                dve.wait_ge(w_lo_set, n + 2)
                dve.memset(w[:, :, :, :], 0.0).then_inc(states_clear, 1)
                dve.wait_ge(states_clear, n + 1)
                dve.wait_ge(winit_in, 16)
                for g, half in halves:
                    dve.tensor_copy(w[half, :, :, 64 * g:64 * g + 64],
                                    winit[half, n, :, :].unsqueeze(2).broadcast_to([64, NJ, NB, 64])
                                    ).then_inc(states_set, 1)
            for s in range(3):
                if s:
                    silu(s, s % 2)
                if s == 0:
                    scores(0, 0)
                    sums(0, 0)
            over_slots(dve, slot)

        @block.scalar
        def _(act):
            def x_transposed(c, u):
                act.wait_ge(xt_mm, 2 * c + u + 1)
                act.activation(xnt_hi[:, :, u * P:u * P + P], ps_x[:, :].rearrange("p (t n) -> p t n", t=KT),
                               ACT.Copy).then_inc(xt_hi_set, 1)

            def gate_tanh(c):
                act.wait_ge(gate_mm, c + 1)
                act.activation(gates[:, :, :], ps_x[:, 0:NT * 4 * H].rearrange("p (u n) -> p u n", u=NT),
                               ACT.Tanh, scale=0.5).then_inc(gate_set, 1)

            def qk_tanh(s, r):
                act.wait_ge(qk_mm, s + 1)
                wait(act, z_mm, s - 1)
                wait(act, kv_mm, clip(s - 1, TOKEN_KV_SLOTS))
                act.activation(tanh_qk[:, r, :, :], ps_qk, ACT.Tanh, scale=0.5).then_inc(tanh_set, 1)

            def v_copy(s, r4):
                act.wait_ge(v_mm, s + 1)
                wait(act, a_mm, clip(s - 3, LEARNING))
                act.activation(vt[:, r4, :], ps_v, ACT.Copy).then_inc(v_evac, 1)

            def kv_copy(s, r4):
                act.wait_ge(kv_mm, s + 1)
                wait(act, g_mm, clip(s - 3, LEARNING))
                act.activation(kvtok[:, r4, :, :, :], ps_kv, ACT.Copy).then_inc(kv_evac, 1)

            def exps(s, r):
                act.wait_ge(zs_set, s + 1)
                act.activation(ez[:, r, :, :, :].rearrange("p t b n -> p (t b) n"), zs[:, r, :, :], ACT.Exp,
                               scale=0.5).then_inc(e_set, 1)

            def pt_copy(s, r):
                act.wait_ge(pt_mm, s + 1)
                wait(act, ps_set, s - 1)
                wait(act, pa_set, s - 1)
                act.activation(pt[:, r, :, :, :], ps_pt, ACT.Copy).then_inc(pt_evac, 1)
                wait(act, g_mm, s - 1)
                for g, half in halves:
                    act.activation(pt_bd[half, r, :, :, g, :], ps_pt[half], ACT.Copy).then_inc(pt_evac, 1)

            def o_copy(c, s, j):
                act.wait_ge(o_mm, s + 1)
                wait(act, o_stored[j % 2], 16 * (NJ // 2 * c + j // 2))
                act.activation(ot[:, j % 2, :], ps_o, ACT.Copy).then_inc(o_evac, 1)

            def wout_copy(s, jj):
                act.wait_ge(wt_mm, s + 1)
                act.activation(wout[:, jj, :, :], ps_wt, ACT.Copy).then_inc(wt_evac, 1)

            def slot(c, j):
                s = c * NJ + j
                if exists(c, j + 1):
                    if before(s + 1, TOKEN_KV_SLOTS):
                        kv_copy(s + 1, (j + 1) % 4)
                    exps(s + 1, (j + 1) % 2)
                if j == 5 and exists(c, NJ):
                    x_transposed(c + 1, 0)
                if learns(c, j):
                    pt_copy(s, j % 2)
                if j == 5 and exists(c, NJ):
                    x_transposed(c + 1, 1)
                o_copy(c, s, j)
                if learns(c, j - 2):
                    wout_copy(s - 2, (j - 2) % NJ)
                if j == 6 and exists(c, NJ):
                    gate_tanh(c + 1)
                if exists(c, j + 3):
                    qk_tanh(s + 3, (j + 3) % 2)
                    if before(s + 3, KV_SLOTS):
                        v_copy(s + 3, (j + 3) % 4)

            x_transposed(0, 0)
            x_transposed(0, 1)
            for of, loaded, hi in ((wlb_s[:, :, :], wlb_in, wlb_hi), (staged[0], wq_in, wq_hi),
                                   (staged[1], wk_in, wk_hi), (staged[2], wv_in, wv_hi)):
                act.wait_ge(loaded, 16)
                act.activation(hi[:, :, :], of, ACT.Copy).then_inc(w_hi_set, 1)
            act.wait_ge(consts_set, 8)
            gate_tanh(0)
            for s in range(3):
                qk_tanh(s, s % 2)
                v_copy(s, s)
                if s == 0:
                    kv_copy(0, 0)
                    exps(0, 0)
            over_slots(act, slot)

        @block.tensor
        def _(pe):
            def product(out, left, right):
                for t in range(KT):
                    for n, (a, b) in enumerate(((0, 0), (0, 1), (1, 0))):
                        i = pe.matmul(out, left(a, t), right(b, t), start=t == 0 and n == 0, stop=t == KT - 1 and n == 2)
                return i

            def x_transposes(c, u):
                pe.wait_ge(xn_set, c + 1)
                if u == 0:
                    wait(pe, mean_evac, c)
                wait(pe, xt_lo_set, 2 * c + u)
                for t in range(KT):
                    i = pe.transpose(ps_x[:, t * P:t * P + P], xin[:, u, t * P:t * P + P], ident[:, :])
                i.then_inc(xt_mm, 1)

            def gate_scores(c):
                pe.wait_ge(xt_lo_set, 2 * c + 2)
                for u in range(NT):
                    i = product(ps_x[:, u * 4 * H:(u + 1) * 4 * H],
                                lambda a, t: (xnt_hi, xnt_lo)[a][:, t, u * P:u * P + P],
                                lambda b, t: (wlb_hi, wlb_lo)[b][:, t, :])
                i.then_inc(gate_mm, 1)

            def gate_means(c):
                pe.wait_ge(gate_set, c + 1)
                for b in range(NB):
                    i = pe.matmul(ps_x[:, b * 4 * H:(b + 1) * 4 * H], meansel[:, b % 2, :], gates[:, b // 2, :],
                                  start=True, stop=True)
                i.then_inc(mean_mm, 1)

            def project(s, j):
                pe.wait_ge(xt_lo_set, 2)
                wait(pe, qk_set, s)
                for n, w in enumerate(((wq_hi, wq_lo), (wk_hi, wk_lo))):
                    if n and not before(s, KV_SLOTS):
                        continue
                    if isinstance(s, int) and s == 0:
                        pe.wait_ge(w_lo_set, n + 2)
                    i = product(ps_qk[:, n, :], lambda a, t: w[a][:, t, j * P:j * P + P],
                                lambda b, t: (xnt_hi, xnt_lo)[b][:, t, :])
                i.then_inc(qk_mm, 1)
                if not before(s, KV_SLOTS):
                    return
                wait(pe, v_evac, s)
                wait(pe, o_evac, s - 2)
                if isinstance(s, int) and s == 0:
                    pe.wait_ge(w_lo_set, 4)
                product(ps_v, lambda a, t: (wv_hi, wv_lo)[a][:, t, j * P:j * P + P],
                        lambda b, t: (xnt_hi, xnt_lo)[b][:, t, :]).then_inc(v_mm, 1)

            def scores(s, j, r, r4):
                pe.wait_ge(qk_set, s + 1)
                wait(pe, zs_set, s)
                wait(pe, w_set, 4 * (s - NJ + 1))
                for b in range(NB):
                    i = pe.matmul(ps_z.rearrange("p (t b) n -> p t b n", t=2)[:, :, b, :], win_t[:, j, b, :],
                                  qk[:, r, :, b, :], start=True, stop=True)
                i.then_inc(z_mm, 1)
                if not before(s, TOKEN_KV_SLOTS):
                    return
                pe.wait_ge(v_evac, s + 1)
                wait(pe, kv_evac, s)
                wait(pe, wt_evac, clip(s - 3, LEARNING))
                for u in range(NT):
                    pe.transpose(ps_kv[:, 0, u, :], qk[:, r, 1, 2 * u:2 * u + 2, :].rearrange("p b n -> p (b n)"), ident[:, :])
                for u in range(NT):
                    i = pe.transpose(ps_kv[:, 1, u, :], vt[:, r4, u * P:u * P + P], ident[:, :])
                i.then_inc(kv_mm, 1)

            def outputs(c, s, j, r):
                pe.wait_ge(pr_set, s + 1)
                pe.wait_ge(v_evac, clip(s + 3, KV_SLOTS))
                wait(pe, o_evac, s)
                wait(pe, wt_evac, s - NJ + 1)
                for b in range(NB):
                    for g in range(2):
                        i = pe.matmul(ps_o[64 * g:64 * g + 64, b * CH:(b + 1) * CH],
                                      wout[:, j, b, 64 * g:64 * g + 64], pr[:, r, 0, b, :], start=True, stop=True)
                i.then_inc(o_mm, 1)

            def gradients_of_p(s, j, r, r4):
                wait(pe, pt_evac, 3 * s)
                for u in range(NT):
                    i = pe.transpose(ps_pt[:, u, :, :].rearrange("p g f -> p (g f)"),
                                     pr[:, r, 1, 2 * u:2 * u + 2, :].rearrange("p b n -> p (b n)"), ident[:, :])
                i.then_inc(pt_mm, 1)
                wait(pe, pa_set, s)
                for b in range(NB):
                    h, u = b % 2, b // 2
                    i = pe.matmul(bank[B_A][64 * h:64 * h + 64, u * P:u * P + P], vt[:, r4, b * CH:(b + 1) * CH],
                                  wout_t[:, j, b, :], start=True, stop=True)
                i.then_inc(a_mm, 1)

            def gradients(s, r, r4):
                pe.wait_ge(kv_evac, s + 1)
                pe.wait_ge(gz_set, 2 * s + 2)
                wait(pe, step_set, 2 * s)
                for m, by_batch in ((0, gz_bd), (1, pt_bd)):
                    for u in range(NT):
                        for g in range(2):
                            i = pe.matmul(bank[B_G][64 * g:64 * g + 64, m * 256 + u * P:m * 256 + u * P + P],
                                          kvtok[:, r4, m, u, 64 * g:64 * g + 64],
                                          by_batch[:, r, u, g, :, :].rearrange("p b f -> p (b f)"),
                                          start=True, stop=True)
                i.then_inc(g_mm, 1)

            def wout_transposes(s, jj):
                pe.wait_ge(w_set, 4 * s + 4)
                pe.wait_ge(kv_evac, clip(s + 4, TOKEN_KV_SLOTS))
                wait(pe, wt_evac, s)
                for b in range(NB):
                    i = pe.transpose(ps_wt[:, b, :], wout_t[:, jj, b, :], ident[:, :])
                i.then_inc(wt_mm, 1)

            def slot(c, j):
                s = c * NJ + j
                if exists(c, j + 1):
                    scores(s + 1, (j + 1) % NJ, (j + 1) % 2, (j + 1) % 4)
                if j == 5 and exists(c, NJ):
                    x_transposes(c + 1, 0)
                outputs(c, s, j, j % 2)
                if learns(c, j):
                    gradients_of_p(s, j, j % 2, j % 4)
                if j == 5 and exists(c, NJ):
                    x_transposes(c + 1, 1)
                if learns(c, j - 1):
                    gradients(s - 1, (j - 1) % 2, (j - 1) % 4)
                if learns(c, j - 2):
                    wout_transposes(s - 2, (j - 2) % NJ)
                if exists(c, NJ):
                    if j == 6:
                        gate_scores(c + 1)
                    if j == 7:
                        gate_means(c + 1)
                if exists(c, j + 3):
                    if j == 5:
                        pe.wait_ge(xt_lo_set, 2 * c + 4)
                    project(s + 3, (j + 3) % NJ)

            pe.wait_ge(consts_set, 4)
            x_transposes(0, 0)
            x_transposes(0, 1)
            pe.wait_ge(w_lo_set, 1)
            gate_scores(0)
            pe.wait_ge(consts_set, 8)
            gate_means(0)
            for s in range(3):
                project(s, s)
                if s == 0:
                    pe.wait_ge(states_set, 2)
                    scores(0, 0, 0, 0)
            pe.wait_ge(states_set, 6)
            over_slots(pe, slot)


def moments_of(dve, c, xin, tiles, width, stats, moments, mean, var_eps, stats_set, ln_chain):
    for u in range(tiles):
        i = dve.bn_stats(stats[:, u, :], xin[:, u, :])
    i.then_inc(stats_set, 1)
    dve.wait_ge(stats_set, c + 1)
    dve.tensor_tensor(moments[:, 0, :], stats[:, :, 1], stats[:, :, 4], ALU.add)
    dve.tensor_tensor(moments[:, 1, :], stats[:, :, 1], stats[:, :, 4], ALU.subtract)
    dve.tensor_tensor(moments[:, 2, :], stats[:, :, 2], stats[:, :, 5], ALU.add).then_inc(ln_chain, 1)
    dve.wait_ge(ln_chain, 3 * c + 1)
    dve.tensor_scalar(mean[:, :], moments[:, 0, :], 0.5, None, ALU.mult)
    dve.scalar_tensor_tensor(out=moments[:, 3, :], in0=moments[:, 1, :], scalar=0.25, in1=moments[:, 1, :],
                             op0=ALU.mult, op1=ALU.mult)
    dve.tensor_scalar(moments[:, 4, :], moments[:, 2, :], 1.0 / width, EPS, ALU.mult, ALU.add).then_inc(ln_chain, 1)
    dve.wait_ge(ln_chain, 3 * c + 2)
    dve.tensor_tensor(var_eps[:, :], moments[:, 3, :], moments[:, 4, :], ALU.add).then_inc(ln_chain, 1)


def cross_projections(nc, x1, ctx_t, mask, wq, wk, wv, bq, bk, bv, q_hi, q_lo, k_hi, k_lo, v_out):
    NB, S, DIM = x1.shape
    GT = 512
    NG = NB * S // GT
    GPB = S // GT
    KT = DIM // P
    TT = GT // P
    ex = ExitStack()
    with ex:
        sb = lambda name, shape, dt=F32: ex.enter_context(nc.sbuf_tensor("p_" + name, shape, dt))
        sem = semaphores(nc, ex, "p_")
        bank = [ex.enter_context(nc.psum_tensor(f"p_bank{i}", [P, 512], F32)) for i in range(8)]
        stage = sb("stage", [P, KT, DIM])
        w_hi = [sb(f"w_hi{n}", [P, KT, DIM], F32R) for n in range(3)]
        w_lo = [sb(f"w_lo{n}", [P, KT, DIM], F32R) for n in range(3)]
        bq_s, bk_s = sb("bq", [P, KT]), sb("bk", [P, KT])
        bv_s = sb("bv", [P, DIM])
        ident = sb("ident", [P, P])
        neghalf = sb("neghalf", [P, TT])
        xin, xn = sb("xin", [P, TT, DIM]), sb("xn", [P, TT, DIM])
        stats, moments = sb("stats", [P, TT, 6]), sb("moments", [P, 5, TT])
        mean, var_eps, rstd = sb("mean", [P, TT]), sb("var_eps", [P, TT]), sb("rstd", [P, TT])
        xnt_hi, xnt_lo = (sb(n, [P, 2, KT, GT], F32R) for n in ("xnt_hi", "xnt_lo"))
        ctx_in = sb("ctx_in", [P, KT, GT])
        ctx_hi, ctx_lo = (sb(n, [P, 2, KT, GT], F32R) for n in ("ctx_hi", "ctx_lo"))
        mask_i, mask_f = sb("mask_i", [P, GT], I32), sb("mask_f", [P, 2, GT])
        qk_f = sb("qk_f", [P, 4, GT])
        qk_hi, qk_lo = (sb(n, [P, 4, GT], F32R) for n in ("qk_hi", "qk_lo"))
        v_s = sb("v_s", [P, 4, DIM])

        consts_in, w_in, w_split, w_hi_set = sem("consts_in"), sem("w_in"), sem("w_split"), sem("w_hi_set")
        consts_set = sem("consts_set")
        x_in, c_in, m_in = sem("x_in"), sem("c_in"), sem("m_in")
        stats_set, ln_chain, rstd_set, xn_set = sem("stats_set"), sem("ln_chain"), sem("rstd_set"), sem("xn_set")
        c_hi_set, c_lo_set, mask_set = sem("c_hi_set"), sem("c_lo_set"), sem("mask_set")
        xt_mm = sem("xt_mm")
        xt_hi_set, xt_lo_set = sem("xt_hi_set"), sem("xt_lo_set")
        out_mm = sem("out_mm")
        q_evac, k_evac, v_evac = sem("q_evac"), sem("k_evac"), sem("v_evac")
        hi_set, lo_set = sem("hi_set"), sem("lo_set")
        qk_out = [sem(f"qk_out{r}") for r in range(4)]
        v_outs = [sem(f"v_out{r}") for r in range(4)]
        wait_taken = sem("wait_taken")
        block = ex.enter_context(nc.Block())

        def over_groups(eng, group):
            for h in range(GPB):
                group(0, h)
            with eng.Fori(1, NB - 1) as b:
                for h in range(GPB):
                    group(b, h)
            for h in range(GPB):
                group(NB - 1, h)

        def following(b, h):
            if h + 1 < GPB:
                return b, h + 1
            return (b + 1, 0) if not isinstance(b, int) or b + 1 < NB else None

        @block.sync
        def _(sp):
            sp.dma_start(bq_s[:, :], bq).then_inc(consts_in, 16)
            sp.dma_start(bk_s[:, :], bk).then_inc(consts_in, 16)
            sp.dma_start(bv_s[:, :], bv.unsqueeze(0).broadcast_to([P, DIM])).then_inc(consts_in, 16)

            def load(b, h):
                g = b * GPB + h
                wait(sp, xn_set, g)
                sp.dma_start(xin[:, :, :], x1[b, h * GT:(h + 1) * GT, :].rearrange("(u p) d -> p u d", p=P)
                             ).then_inc(x_in, 16)
                wait(sp, c_lo_set, g)
                sp.dma_start(ctx_in[:, :, :], ctx_t[b, :, h * GT:(h + 1) * GT].rearrange("(t p) n -> p t n", p=P)
                             ).then_inc(c_in, 16)
                wait(sp, mask_set, g)
                sp.dma_start(mask_i[:, :], mask[b, h * GT:(h + 1) * GT].unsqueeze(0).broadcast_to([P, GT])
                             ).then_inc(m_in, 16)

            def stores(b, h):
                g = b * GPB + h
                for u in range(8):
                    n, t = divmod(u, 4)
                    hi, lo = ((q_hi, q_lo), (k_hi, k_lo))[n]
                    sp.wait_ge(lo_set, 8 * g + u + 1)
                    if u == 0:
                        sp.sem_inc(wait_taken, 1)
                    for part, of in ((hi, qk_hi), (lo, qk_lo)):
                        sp.dma_start(part[b, t * P:(t + 1) * P, h * GT:(h + 1) * GT], of[:, u % 4, :].bitcast(F32)
                                     ).then_inc(qk_out[u % 4], 16)
                for u in range(TT):
                    sp.wait_ge(v_evac, 4 * g + u + 1)
                    sp.dma_start(v_out[b, h * GT + u * P:h * GT + (u + 1) * P, :], v_s[:, u, :]
                                 ).then_inc(v_outs[u], 16)

            load(0, 0)
            for n, w in enumerate((wq, wk, wv)):
                wait(sp, w_split, n)
                sp.dma_start(stage[:, :, :], w.rearrange("(t p) n -> p t n", p=P)).then_inc(w_in, 16)

            def group(b, h):
                if following(b, h):
                    load(*following(b, h))
                stores(b, h)

            over_groups(sp, group)
            for r in range(4):
                sp.wait_ge(qk_out[r], 32 * 2 * NG)
                sp.wait_ge(v_outs[r], 16 * NG)

        @block.gpsimd
        def _(pool):
            pool.memset(ident[:, :], 0.0).then_inc(consts_set, 1)
            pool.memset(neghalf[:, :], -0.5).then_inc(consts_set, 1)
            pool.wait_ge(consts_set, 2)
            pool.affine_select(out=ident[:, :], in_=ident[:, :], compare_op=ALU.not_equal, fill=1.0,
                               base=0, pattern=[[-1, P]], channel_multiplier=1).then_inc(consts_set, 1)

            def norm_scale(g):
                pool.wait_ge(ln_chain, 3 * g + 3)
                wait(pool, xn_set, g)
                pool.tensor_tensor(rstd[:, :], var_eps[:, :], neghalf[:, :], ALU.pow).then_inc(rstd_set, 1)

            def group(b, h):
                g = b * GPB + h
                if following(b, h):
                    norm_scale(g + 1)
                for u in range(8):
                    n = 8 * g + u
                    wait(pool, qk_out[u % 4], 32 * (2 * g + u // 4))
                    pool.wait_ge(hi_set, n + 1)
                    pool.tensor_tensor(qk_lo[:, u % 4, :], qk_f[:, u % 4, :], qk_hi[:, u % 4, :].bitcast(F32),
                                       ALU.subtract).then_inc(lo_set, 1)

            norm_scale(0)
            over_groups(pool, group)

        @block.vector
        def _(dve):
            def prepare(g, b, h, r):
                dve.wait_ge(x_in, 16 * g + 16)
                moments_of(dve, g, xin, TT, DIM, stats, moments, mean, var_eps, stats_set, ln_chain)
                dve.wait_ge(c_in, 16 * g + 16)
                wait(dve, out_mm, 12 * (g - 1))
                dve.tensor_copy(ctx_hi[:, r, :, :], ctx_in[:, :, :]).then_inc(c_hi_set, 1)
                dve.wait_ge(c_hi_set, g + 1)
                dve.tensor_tensor(ctx_lo[:, r, :, :], ctx_in[:, :, :], ctx_hi[:, r, :, :].bitcast(F32), ALU.subtract
                                  ).then_inc(c_lo_set, 1)
                dve.wait_ge(m_in, 16 * g + 16)
                dve.tensor_scalar(mask_f[:, r, :], mask_i[:, :], 0.0, None, ALU.not_equal).then_inc(mask_set, 1)
                dve.wait_ge(rstd_set, g + 1)
                wait(dve, xt_mm, 4 * g)
                for u in range(TT):
                    i = dve.tensor_scalar(xn[:, u, :], xin[:, u, :], mean[:, u:u + 1], rstd[:, u:u + 1],
                                          ALU.subtract, ALU.mult)
                i.then_inc(xn_set, 1)

            def transposed_lo(g, r):
                for u in range(TT):
                    dve.wait_ge(xt_hi_set, 4 * g + u + 1)
                    dve.tensor_tensor(xnt_lo[:, r, :, u * P:(u + 1) * P],
                                      bank[u % 2][:, :].rearrange("p (t n) -> p t n", t=KT),
                                      xnt_hi[:, r, :, u * P:(u + 1) * P].bitcast(F32), ALU.subtract
                                      ).then_inc(xt_lo_set, 1)

            prepare(0, 0, 0, 0)
            dve.wait_ge(consts_in, 48)
            for n in range(3):
                dve.wait_ge(w_in, 16 * n + 16)
                dve.tensor_copy(w_hi[n][:, :, :], stage[:, :, :]).then_inc(w_hi_set, 1)
                dve.wait_ge(w_hi_set, n + 1)
                dve.tensor_tensor(w_lo[n][:, :, :], stage[:, :, :], w_hi[n][:, :, :].bitcast(F32), ALU.subtract
                                  ).then_inc(w_split, 1)
                if n == 0:
                    transposed_lo(0, 0)

            def group(b, h):
                g, r = b * GPB + h, h % 2
                if following(b, h):
                    prepare(g + 1, *following(b, h), (h + 1) % 2)
                for t in range(4):
                    dve.wait_ge(out_mm, 12 * g + 5 + t)
                    dve.wait_ge(mask_set, g + 1)
                    wait(dve, lo_set, 8 * g + t + 1)
                    dve.scalar_tensor_tensor(out=qk_f[:, t, :], in0=bank[2 + (4 + t) % 6][:, :],
                                             scalar=bk_s[:, t:t + 1], in1=mask_f[:, r, :], op0=ALU.add,
                                             op1=ALU.mult).then_inc(k_evac, 1)
                if following(b, h):
                    transposed_lo(g + 1, (h + 1) % 2)
                for u in range(TT):
                    dve.wait_ge(out_mm, 12 * g + 9 + u)
                    wait(dve, v_outs[u], 16 * g)
                    dve.tensor_tensor(v_s[:, u, :], bank[2 + (8 + u) % 6][:, :], bv_s[:, :], ALU.add
                                      ).then_inc(v_evac, 1)

            over_groups(dve, group)

        @block.scalar
        def _(act):
            def transposed_hi(g, r):
                for u in range(TT):
                    act.wait_ge(xt_mm, 4 * g + u + 1)
                    wait(act, out_mm, 12 * (g - 1))
                    act.activation(xnt_hi[:, r, :, u * P:(u + 1) * P],
                                   bank[u % 2][:, :].rearrange("p (t n) -> p t n", t=KT), ACT.Copy
                                   ).then_inc(xt_hi_set, 1)

            def first_part(g, u):
                wait(act, qk_out[u % 4], 32 * (2 * g + u // 4))
                act.activation(qk_hi[:, u % 4, :], qk_f[:, u % 4, :], ACT.Copy).then_inc(hi_set, 1)

            transposed_hi(0, 0)
            act.wait_ge(consts_in, 48)

            def group(b, h):
                g = b * GPB + h
                for t in range(4):
                    act.wait_ge(out_mm, 12 * g + 1 + t)
                    wait(act, lo_set, 8 * g - 3 + t)
                    act.activation(qk_f[:, t, :], bank[2 + t][:, :], ACT.Identity, bias=bq_s[:, t:t + 1]
                                   ).then_inc(q_evac, 1)
                    act.wait_ge(q_evac, 4 * g + t + 1)
                    first_part(g, t)
                for t in range(4):
                    act.wait_ge(k_evac, 4 * g + t + 1)
                    first_part(g, 4 + t)
                if following(b, h):
                    transposed_hi(g + 1, (h + 1) % 2)

            over_groups(act, group)

        @block.tensor
        def _(pe):
            def transposes(g, tiles):
                for u in tiles:
                    pe.wait_ge(xn_set, g + 1)
                    wait(pe, xt_lo_set, 4 * g + u - 1)
                    for t in range(KT):
                        i = pe.transpose(bank[u % 2][:, t * P:(t + 1) * P], xn[:, u, t * P:(t + 1) * P], ident[:, :])
                    i.then_inc(xt_mm, 1)

            def product(out, left, right):
                for t in range(KT):
                    for n, (a, b) in enumerate(((0, 0), (0, 1), (1, 0))):
                        i = pe.matmul(out, left(a, t), right(b, t), start=t == 0 and n == 0, stop=t == KT - 1 and n == 2)
                return i

            def group(b, h):
                g, r = b * GPB + h, h % 2
                pe.wait_ge(xt_lo_set, 4 * g + 4)
                pe.wait_ge(c_lo_set, g + 1)
                for i in range(12):
                    if i in (8, 10) and following(b, h):
                        transposes(g + 1, range(i - 8, i - 6))
                    if i < 2:
                        wait(pe, k_evac, 4 * (g - 1) + i + 3)
                    elif i < 6:
                        wait(pe, v_evac, 4 * (g - 1) + i - 1)
                    elif i < 10:
                        pe.wait_ge(q_evac, 4 * g + i - 5)
                    else:
                        pe.wait_ge(k_evac, 4 * g + i - 9)
                    n, t = divmod(i, 4)
                    if t == 0:
                        pe.wait_ge(w_split, n + 1)
                    w = (w_hi[n], w_lo[n])
                    if n < 2:
                        act_ = ((xnt_hi, xnt_lo), (ctx_hi, ctx_lo))[n]
                        last = product(bank[2 + i % 6][:, :], lambda a, k: w[a][:, k, t * P:(t + 1) * P],
                                       lambda a, k: act_[a][:, r, k, :])
                    else:
                        last = product(bank[2 + i % 6][:, :],
                                       lambda a, k: (ctx_hi, ctx_lo)[a][:, r, k, t * P:(t + 1) * P],
                                       lambda a, k: w[a][:, k, :])
                    last.then_inc(out_mm, 1)

            pe.wait_ge(consts_set, 3)
            transposes(0, range(TT))
            over_groups(pe, group)


def scan_projection(nc, o_t, x, wo, x1):
    NB, L, DIM = x.shape
    NJ, _, NCH, TOK = o_t.shape
    CH = TOK // NB
    NT = TOK // P
    CG = 2
    NG = NCH // CG
    UT = CG * NT
    ex = ExitStack()
    with ex:
        sb = lambda name, shape, dt=F32: ex.enter_context(nc.sbuf_tensor("y_" + name, shape, dt))
        sem = semaphores(nc, ex, "y_")
        bank = [ex.enter_context(nc.psum_tensor(f"y_bank{i}", [P, 512], F32)) for i in range(8)]
        stage = sb("stage", [P, NJ, DIM])
        w_hi, w_lo = sb("w_hi", [P, NJ, DIM], F32R), sb("w_lo", [P, NJ, DIM], F32R)
        o_in = sb("o_in", [P, NJ, CG * TOK])
        o_hi, o_lo = sb("o_hi", [P, 2, NJ, CG * TOK], F32R), sb("o_lo", [P, 2, NJ, CG * TOK], F32R)
        xs = sb("xs", [P, 2, CG, NT, DIM])

        w_in = [sem(f"w_in{k}") for k in range(2)]
        w_hi_set, w_split = sem("w_hi_set"), sem("w_split")
        o_loaded = [sem(f"o_loaded{k}") for k in range(2)]
        hi_set, lo_set = sem("hi_set"), sem("lo_set")
        x_in = [sem(f"x_in{r}") for r in range(2)]
        y_mm, x1_set = sem("y_mm"), sem("x1_set")
        stored = [sem(f"stored{r}") for r in range(2)]
        wait_taken = sem("wait_taken")
        block = ex.enter_context(nc.Block())
        halves = [slice(k * NJ // 2, (k + 1) * NJ // 2) for k in range(2)]

        def over_groups(eng, group):
            for r in range(2):
                group(0, r)
            with eng.Fori(1, NG // 2 - 1) as t:
                for r in range(2):
                    group(t, r)
            for r in range(2):
                group(NG // 2 - 1, r)

        def following(t, r):
            if r == 0:
                return t, 1
            return (t + 1, 0) if not isinstance(t, int) or t + 1 < NG // 2 else None

        @block.sync
        def _(sp):
            def load_o(t, r, k):
                g = 2 * t + r
                wait(sp, lo_set, 2 * g - 1 + k)
                if not isinstance(t, int):
                    sp.sem_inc(wait_taken, 1)
                sp.dma_start(o_in[:, halves[k], :],
                             o_t[halves[k], :, bass.ds(g * CG, CG), :].rearrange("j p c n -> p j (c n)")
                             ).then_inc(o_loaded[k], 16)

            def load_x(t, r):
                g = 2 * t + r
                wait(sp, stored[r], 16 * NB * t)
                if not isinstance(t, int):
                    sp.sem_inc(wait_taken, 1)
                for b in range(NB):
                    sp.dma_start(xs[64 * (b % 2):64 * (b % 2) + 64, r, :, b // 2, :],
                                 x[b, bass.ds(g * CG * CH, CG * CH), :].rearrange("(c n) d -> n c d", c=CG)
                                 ).then_inc(x_in[r], 16)

            def store(t, r):
                g = 2 * t + r
                sp.wait_ge(x1_set, UT * g + UT)
                if not isinstance(t, int):
                    sp.sem_inc(wait_taken, 1)
                for b in range(NB):
                    sp.dma_start(x1[b, bass.ds(g * CG * CH, CG * CH), :].rearrange("(c n) d -> n c d", c=CG),
                                 xs[64 * (b % 2):64 * (b % 2) + 64, r, :, b // 2, :]).then_inc(stored[r], 16)

            for k in range(2):
                sp.dma_start(stage[:, halves[k], :], wo.rearrange("(t p) n -> p t n", p=P)[:, halves[k], :]
                             ).then_inc(w_in[k], 16)
                load_o(0, 0, k)
            load_x(0, 0)

            def group(t, r):
                if following(t, r):
                    for k in range(2):
                        load_o(*following(t, r), k)
                    load_x(*following(t, r))
                store(t, r)

            over_groups(sp, group)
            for r in range(2):
                sp.wait_ge(stored[r], 16 * NB * (NG // 2))

        @block.scalar
        def _(act):
            def group(t, r):
                g = 2 * t + r
                for k in range(2):
                    if isinstance(g, int) and g == 0:
                        act.wait_ge(w_in[k], 16)
                        act.activation(w_hi[:, halves[k], :], stage[:, halves[k], :], ACT.Copy).then_inc(w_hi_set, 1)
                    act.wait_ge(o_loaded[k], 16 * g + 16)
                    wait(act, y_mm, UT * (g - 1))
                    act.activation(o_hi[:, r, halves[k], :], o_in[:, halves[k], :], ACT.Copy).then_inc(hi_set, 1)

            over_groups(act, group)

        @block.vector
        def _(dve):
            def split(t, r):
                g = 2 * t + r
                for k in range(2):
                    if isinstance(g, int) and g == 0:
                        dve.wait_ge(w_hi_set, k + 1)
                        dve.tensor_tensor(w_lo[:, halves[k], :], stage[:, halves[k], :],
                                          w_hi[:, halves[k], :].bitcast(F32), ALU.subtract).then_inc(w_split, 1)
                    dve.wait_ge(hi_set, 2 * g + k + 1)
                    dve.tensor_tensor(o_lo[:, r, halves[k], :], o_in[:, halves[k], :],
                                      o_hi[:, r, halves[k], :].bitcast(F32), ALU.subtract).then_inc(lo_set, 1)

            split(0, 0)

            def group(t, r):
                if following(t, r):
                    split(*following(t, r))
                dve.wait_ge(x_in[r], 16 * NB * t + 16 * NB)
                for u in range(UT):
                    dve.wait_ge(y_mm, UT * (2 * t + r) + u + 1)
                    dve.tensor_tensor(xs[:, r, u // NT, u % NT, :], bank[UT * r + u][:, :],
                                      xs[:, r, u // NT, u % NT, :], ALU.add).then_inc(x1_set, 1)

            over_groups(dve, group)

        @block.tensor
        def _(pe):
            def group(t, r):
                g = 2 * t + r
                for u in range(UT):
                    wait(pe, x1_set, UT * (g - 2) + u + 1)
                    for j in range(NJ):
                        if u == 0 and j % (NJ // 2) == 0:
                            if isinstance(g, int) and g == 0:
                                pe.wait_ge(w_split, j // (NJ // 2) + 1)
                            pe.wait_ge(lo_set, 2 * g + j // (NJ // 2) + 1)
                        for n, (a, b) in enumerate(((0, 0), (0, 1), (1, 0))):
                            i = pe.matmul(bank[UT * r + u][:, :], (o_hi, o_lo)[a][:, r, j, u * P:(u + 1) * P],
                                          (w_hi, w_lo)[b][:, j, :], start=j == 0 and n == 0,
                                          stop=j == NJ - 1 and n == 2)
                    i.then_inc(y_mm, 1)

            over_groups(pe, group)


def cross_attention(nc, q_hi, q_lo, k_hi, k_lo, v, mask, m_rows, ctx_out):
    NB, DIM, S = q_hi.shape
    DK = 32
    HT = P // DK
    NTILE = DIM // P
    NSLOT = NB * NTILE
    KB = S // P
    NSTEP = 2 * KB
    SCALE = DK ** -0.5
    MASK_ROW, MAX_ROW, ROWS = 3 * DK, 3 * DK + 2, 3 * DK + 4
    PER_STEP = (2, 3, 2, 3, 2, 3, 2, 3, 2, 3, 2, 3, 2)
    MAX_STEP = len(PER_STEP)
    UNITS = HT * KB
    PARTS = 4
    assert sum(PER_STEP) == UNITS and NTILE % 2 == 0
    masked = -1e9 / SCALE
    unit = 2.0 ** (33 - 12)
    masked_hi = round(masked / unit) * unit
    masked_lo = round((masked - masked_hi) / 512.0) * 512.0
    ex = ExitStack()
    with ex:
        sb = lambda name, shape, dt=F32: ex.enter_context(nc.sbuf_tensor("c_" + name, shape, dt))
        sem = semaphores(nc, ex, "c_")
        psum = lambda name, shape: ex.enter_context(nc.psum_tensor("c_" + name, shape, F32))
        ps_s = [psum(f"ps_s{i}", [P, 512]) for i in range(2)]
        ps_max = [psum(f"ps_max{i}", [P, 2, 512]) for i in range(2)]
        ps_ctx, ps_sum = psum("ps_ctx", [P, 512]), psum("ps_sum", [P, 512])
        qs = [sb(f"qs{i}", [P, HT, S], F32R) for i in range(NTILE)]
        ks = [sb(f"ks{i}", [P, HT, S], F32R) for i in range(NTILE)]
        vs = sb("vs", [P, NTILE, KB, P])
        pt = sb("pt", [P, 2, HT, 512])
        inverse = sb("inverse", [P, 2, 512])
        ones = sb("ones", [P, DK])
        ident = sb("ident", [P, P])
        mask_i, mask_f = sb("mask_i", [P, S], I32), sb("mask_f", [P, S])
        mval, neg_mval = sb("mval", [P, 1]), sb("neg_mval", [P, 1])
        neg_max = sb("neg_max", [P, UNITS])
        max_parts = sb("max_parts", [P, P // UNITS, UNITS])
        max_t = sb("max_t", [2 * UNITS, P])
        sum_s, raw = sb("sum_s", [P, 2, 512]), sb("raw", [P, 2, 512])
        ctx_s = sb("ctx_s", [P, 2, 512])

        consts_set, rows_set = sem("consts_set"), sem("rows_set")
        stack_in = [sem(f"stack_in{i}") for i in range(2)]
        v_in = [sem(f"v_in{i}") for i in range(2)]
        m_in = sem("m_in")
        mask_set = sem("mask_set")
        mask_rows = sem("mask_rows")
        s_mm = sem("s_mm")
        exp_set = sem("exp_set")
        pv_mm = sem("pv_mm")
        c_mm, c_max = sem("c_mm"), sem("c_max")
        hi_set, parts_set = sem("hi_set"), sem("parts_set")
        mt_mm, mt_evac = sem("mt_mm"), sem("mt_evac")
        m_stored, m_rows_in = sem("m_stored"), sem("m_rows_in")
        sum_set, raw_set = sem("sum_set"), sem("raw_set")
        inverse_set = sem("inverse_set")
        norm_set = sem("norm_set")
        ctx_stored = [sem(f"ctx_stored{i}") for i in range(2)]
        parts_clear, wait_taken = sem("parts_clear"), sem("wait_taken")
        block = ex.enter_context(nc.Block())
        mrows = slice(MASK_ROW, MASK_ROW + 2)

        def over_slots(eng, slot):
            for t in range(NTILE):
                slot(0, t)
            with eng.Fori(1, NB - 1) as b:
                for t in range(NTILE):
                    slot(b, t)
            for t in range(NTILE):
                slot(NB - 1, t)

        def following(b, t):
            if t + 1 < NTILE:
                return b, t + 1
            return (b + 1, 0) if not isinstance(b, int) or b + 1 < NB else None

        def after_next(b, t):
            nxt = following(b, t)
            return following(*nxt) if nxt else None

        @block.sync
        def _(sp):
            def load_stack(b, t):
                T = NTILE * b + t
                wait(sp, s_mm, HT * NSTEP * (T - NTILE + 1))
                if not isinstance(T, int):
                    sp.sem_inc(wait_taken, 1)
                rows = lambda of: of[b, t * P:(t + 1) * P, :].rearrange("(h r) n -> r h n", h=HT)
                for i, (q, k) in enumerate(((q_hi, k_hi), (q_lo, k_hi), (q_hi, k_lo))):
                    sp.dma_start(qs[t][i * DK:(i + 1) * DK, :, :].bitcast(F32), rows(q)).then_inc(stack_in[t % 2], 16)
                    sp.dma_start(ks[t][i * DK:(i + 1) * DK, :, :].bitcast(F32), rows(k)).then_inc(stack_in[t % 2], 16)
                wait(sp, pv_mm, NSTEP * (T - NTILE + 1))
                if not isinstance(T, int):
                    sp.sem_inc(wait_taken, 1)
                sp.dma_start(vs[:, t, :, :], v[b, :, t * P:(t + 1) * P].rearrange("(i p) d -> p i d", p=P)
                             ).then_inc(v_in[t % 2], 16)

            def load_mask(b):
                sp.dma_start(mask_i[mrows, :], mask[b, :].unsqueeze(0).broadcast_to([2, S])).then_inc(m_in, 16)

            def maximum_rows(T, t):
                sp.wait_ge(mt_evac, T + 1)
                sp.dma_start(m_rows.rearrange("a h (t n) -> (a h t) n", n=P), max_t[:, :]).then_inc(m_stored, 16)
                sp.wait_ge(m_stored, 16 * T + 16)
                sp.dma_start(qs[t][MAX_ROW:ROWS, :, :].bitcast(F32), m_rows).then_inc(m_rows_in, 16)

            def store(b, t, half):
                sp.wait_ge(norm_set, 2 * (NTILE * b + t) + half + 1)
                if not isinstance(b, int):
                    sp.sem_inc(wait_taken, 1)
                sp.dma_start(ctx_out[b, t * P:(t + 1) * P, half * 512:(half + 1) * 512], ctx_s[:, half, :]
                             ).then_inc(ctx_stored[half], 16)

            load_mask(0)
            load_stack(0, 0)
            load_stack(0, 1)
            sp.wait_ge(rows_set, 2 * NTILE)
            maximum_rows(0, 0)

            def slot(b, t):
                T, nxt = NTILE * b + t, following(b, t)
                if nxt:
                    if t == 1 and (not isinstance(b, int) or b + 1 < NB):
                        sp.wait_ge(mask_set, b + 1)
                        load_mask(b + 1)
                    if after_next(b, t):
                        load_stack(*after_next(b, t))
                store(b, t, 0)
                if nxt:
                    maximum_rows(T + 1, (t + 1) % NTILE)
                store(b, t, 1)

            over_slots(sp, slot)
            for half in range(2):
                sp.wait_ge(ctx_stored[half], 16 * NSLOT)

        @block.gpsimd
        def _(pool):
            pool.memset(ident[:, :], 0.0).then_inc(consts_set, 1)
            pool.memset(ones[:, :], 1.0).then_inc(consts_set, 1)
            pool.memset(mval[:, :], masked_lo).then_inc(consts_set, 1)
            pool.memset(neg_mval[:, :], -masked_lo).then_inc(consts_set, 1)
            pool.wait_ge(consts_set, 4)
            pool.affine_select(out=ident[:, :], in_=ident[:, :], compare_op=ALU.not_equal, fill=1.0,
                               base=0, pattern=[[-1, P]], channel_multiplier=1).then_inc(consts_set, 1)
            for n, (of, value) in enumerate(((mval, masked_hi), (neg_mval, -masked_hi))):
                pool.wait_ge(consts_set, 5 + n)
                pool.affine_select(out=of[:, :], in_=of[:, :], compare_op=ALU.not_equal, fill=value,
                                   base=-MASK_ROW, pattern=[[0, 1]], channel_multiplier=1).then_inc(consts_set, 1)
            pool.wait_ge(consts_set, 7)
            for s_ in zip(qs, ks):
                for of in s_:
                    pool.memset(of[MASK_ROW:ROWS, :, :].bitcast(F32), 1.0).then_inc(rows_set, 1)

            def slot(b, t):
                T = NTILE * b + t
                for half in range(2):
                    pool.wait_ge(raw_set, 2 * T + half + 1)
                    pool.wait_ge(inverse_set, PARTS * (2 * T + half + 1))
                    wait(pool, ctx_stored[half], 16 * T)
                    pool.tensor_tensor(ctx_s[:, half, :], raw[:, half, :], inverse[:, half, :], ALU.mult
                                       ).then_inc(norm_set, 1)

            over_slots(pool, slot)

        @block.vector
        def _(dve):
            def set_mask(b):
                dve.wait_ge(m_in, 16 * b + 16)
                wait(dve, mask_rows, NTILE * HT * b)
                dve.tensor_scalar(mask_f[mrows, :], mask_i[mrows, :], 0.0, None, ALU.not_equal).then_inc(mask_set, 1)

            def set_mask_rows(b, t):
                T = NTILE * b + t
                dve.wait_ge(mask_set, b + 1)
                wait(dve, s_mm, HT * NSTEP * (T - NTILE + 1))
                for h in range(HT):
                    dve.tensor_scalar(ks[t][mrows, h, :], mask_f[mrows, :], neg_mval[mrows, :], mval[mrows, :],
                                      ALU.mult, ALU.add).then_inc(mask_rows, 1)

            def maxima(T, units):
                for u in units:
                    dve.wait_ge(c_mm, UNITS * T + u + 1)
                    if u == 0:
                        wait(dve, parts_set, T)
                    dve.tensor_reduce(neg_max[:, u:u + 1], ps_max[u % 2][:, :, :].rearrange("p t n -> p (t n)"),
                                      AX.X, ALU.max, negate=True).then_inc(c_max, 1)

            def parts_of_maxima(T):
                dve.wait_ge(c_max, UNITS * T + UNITS)
                wait(dve, mt_mm, T)
                dve.tensor_copy(max_parts[:, 0, :].bitcast(F32R), neg_max[:, :]).then_inc(hi_set, 1)
                dve.wait_ge(hi_set, T + 1)
                dve.tensor_tensor(max_parts[:, 1, :].bitcast(F32R), neg_max[:, :], max_parts[:, 0, :], ALU.subtract
                                  ).then_inc(parts_set, 1)

            def maxima_by_rows(T):
                dve.wait_ge(mt_mm, T + 1)
                wait(dve, m_stored, 16 * T)
                dve.tensor_copy(max_t[:, :], ps_max[0][0:2 * UNITS, 0, 0:P]).then_inc(mt_evac, 1)

            def summed(T, half):
                dve.wait_ge(pv_mm, NSTEP * T + KB * (half + 1))
                wait(dve, norm_set, 2 * T + half - 1)
                dve.tensor_copy(sum_s[:, half, :], ps_sum[:, :]).then_inc(sum_set, 1)

            def inverses(T, half, part):
                dve.wait_ge(sum_set, 2 * T + half + 1)
                wait(dve, norm_set, 2 * T + half - 1)
                n = 512 // PARTS
                dve.reciprocal(inverse[:, half, part * n:(part + 1) * n], sum_s[:, half, part * n:(part + 1) * n]
                               ).then_inc(inverse_set, 1)

            dve.memset(max_parts[:, 2:, :], 0.0).then_inc(parts_clear, 1)
            dve.wait_ge(rows_set, 2)
            set_mask(0)
            set_mask_rows(0, 0)
            maxima(0, range(UNITS))
            parts_of_maxima(0)
            maxima_by_rows(0)
            dve.wait_ge(rows_set, 2 * NTILE)
            set_mask_rows(0, 1)

            def slot(b, t):
                T, nxt = NTILE * b + t, following(b, t)
                later = after_next(b, t)
                u = 0
                for i in range(NSTEP):
                    if nxt and i < MAX_STEP:
                        n = PER_STEP[i]
                        maxima(T + 1, range(u, u + n))
                        u += n
                        if i == MAX_STEP - 1:
                            parts_of_maxima(T + 1)
                    if nxt and i == MAX_STEP:
                        maxima_by_rows(T + 1)
                    if i < PARTS and (not isinstance(T, int) or T):
                        inverses(T - 1, 1, i)
                    if KB <= i < KB + PARTS:
                        inverses(T, 0, i - KB)
                    if i % KB == KB - 1:
                        summed(T, i // KB)
                    if i == MAX_STEP and later:
                        if later[1] == 0:
                            set_mask(later[0])
                        set_mask_rows(*later)

            over_slots(dve, slot)
            for part in range(PARTS):
                inverses(NSLOT - 1, 1, part)

        @block.scalar
        def _(act):
            def weighted(T, half):
                act.wait_ge(pv_mm, NSTEP * T + KB * (half + 1))
                wait(act, norm_set, 2 * T + half - 1)
                act.activation(raw[:, half, :], ps_ctx[:, :], ACT.Copy).then_inc(raw_set, 1)

            def slot(b, t):
                T = NTILE * b + t
                for i in range(NSTEP):
                    for h in range(HT):
                        act.wait_ge(s_mm, HT * (NSTEP * T + i) + h + 1)
                        wait(act, pv_mm, NSTEP * T + i - 1)
                        act.activation(pt[:, i % 2, h, :], ps_s[h % 2][:, :], ACT.Exp, scale=SCALE).then_inc(exp_set, 1)
                        if h == HT - 1 and i % KB == 0 and (not isinstance(T, int) or T or i):
                            weighted(T if i else T - 1, (i // KB + 1) % 2)

            over_slots(act, slot)
            weighted(NSLOT - 1, 1)

        @block.tensor
        def _(pe):
            def scores(T, t, i, heads):
                half, kb = i // KB, i % KB
                if i == 0 and heads[0] == 0:
                    pe.wait_ge(m_rows_in, 16 * T + 16)
                for h in heads:
                    wait(pe, exp_set, HT * (NSTEP * T + i) + h - 1)
                    pe.matmul(ps_s[h % 2][:, :], ks[t][0:ROWS, h, kb * P:(kb + 1) * P],
                              qs[t][0:ROWS, h, half * 512:(half + 1) * 512], start=True, stop=True).then_inc(s_mm, 1)

            def score_rows(b, t, units):
                T = NTILE * b + t
                for u in units:
                    h, qb = divmod(u, KB)
                    if u == 0:
                        pe.wait_ge(stack_in[t % 2], 96 * (NTILE // 2 * b + t // 2) + 96)
                        wait(pe, mt_evac, T)
                    wait(pe, c_max, UNITS * T + u - 1)
                    for half in range(2):
                        i = pe.matmul(ps_max[u % 2][:, half, :], qs[t][0:MAX_ROW, h, qb * P:(qb + 1) * P],
                                      ks[t][0:MAX_ROW, h, half * 512:(half + 1) * 512], start=True, stop=True)
                    i.then_inc(c_mm, 1)

            def maxima_transposed(T):
                pe.wait_ge(parts_set, T + 1)
                pe.transpose(ps_max[0][:, 0, 0:P], max_parts[:, :, :].rearrange("p a u -> p (a u)"),
                             ident[:, :]).then_inc(mt_mm, 1)

            def values(b, T, t, i):
                kb = i % KB
                if i == 0:
                    pe.wait_ge(v_in[t % 2], 16 * (NTILE // 2 * b + t // 2) + 16)
                if kb == 0:
                    wait(pe, raw_set, 2 * T + i // KB)
                    wait(pe, sum_set, 2 * T + i // KB)
                for h in range(HT):
                    pe.wait_ge(exp_set, HT * (NSTEP * T + i) + h + 1)
                    pe.matmul(ps_ctx[h * DK:(h + 1) * DK, :], vs[:, t, kb, h * DK:(h + 1) * DK],
                              pt[:, i % 2, h, :], start=kb == 0, stop=kb == KB - 1)

            def sums(i):
                kb = i % KB
                for h in range(HT):
                    last = pe.matmul(ps_sum[h * DK:(h + 1) * DK, :], ones[:, :], pt[:, i % 2, h, :],
                                     start=kb == 0, stop=kb == KB - 1)
                last.then_inc(pv_mm, 1)

            pe.wait_ge(consts_set, 7)
            pe.wait_ge(rows_set, 2)
            pe.wait_ge(parts_clear, 1)
            pe.wait_ge(mask_rows, HT)
            score_rows(0, 0, range(UNITS))
            maxima_transposed(0)
            scores(0, 0, 0, range(HT // 2))
            scores(0, 0, 0, range(HT // 2, HT))

            def slot(b, t):
                T, nxt = NTILE * b + t, following(b, t)
                u = 0
                for i in range(NSTEP):
                    if i + 1 < NSTEP:
                        ahead = (T, t, i + 1)
                    else:
                        ahead = (T + 1, (t + 1) % NTILE, 0) if nxt else None
                    if ahead:
                        scores(*ahead, range(HT // 2))
                    if nxt and i == 0:
                        pe.wait_ge(mask_rows, HT * (T + 2))
                    units = range(u, u + PER_STEP[i]) if nxt and i < MAX_STEP else range(0)
                    u += len(units)
                    first = 2 if i % KB == 0 else 1
                    score_rows(*(nxt or (b, t)), units[:first])
                    values(b, T, t, i)
                    if nxt and i == MAX_STEP:
                        maxima_transposed(T + 1)
                    if ahead:
                        scores(*ahead, range(HT // 2, HT))
                    score_rows(*(nxt or (b, t)), units[first:])
                    sums(i)

            over_slots(pe, slot)


def output_projection_and_gate(nc, ctx, x1, wo, bo, gw1, gb1, x2, xn_hi, xn_lo, h_sums):
    NB, S, DIM = x1.shape
    GT = 512
    NG = NB * S // GT
    GPB = S // GT
    KT = DIM // P
    TT = GT // P
    ex = ExitStack()
    with ex:
        sb = lambda name, shape, dt=F32: ex.enter_context(nc.sbuf_tensor("o_" + name, shape, dt))
        sem = semaphores(nc, ex, "o_")
        bank = [ex.enter_context(nc.psum_tensor(f"o_bank{i}", [P, 512], F32)) for i in range(8)]
        stage = sb("stage", [P, KT, DIM])
        w_hi = [sb(f"w_hi{n}", [P, KT, DIM], F32R) for n in range(2)]
        w_lo = [sb(f"w_lo{n}", [P, KT, DIM], F32R) for n in range(2)]
        bo_s, gb1_s = sb("bo", [P, DIM]), sb("gb1", [P, KT])
        ident, neghalf = sb("ident", [P, P]), sb("neghalf", [P, TT])
        ctx_in = sb("ctx_in", [P, KT, GT])
        ctx_hi, ctx_lo = (sb(n, [P, KT, GT], F32R) for n in ("ctx_hi", "ctx_lo"))
        x1_in, x1_b = sb("x1_in", [P, TT, DIM]), sb("x1_b", [P, TT, DIM])
        x2_s, xn = sb("x2_s", [P, TT, DIM]), sb("xn", [P, TT, DIM])
        stats, moments = sb("stats", [P, TT, 6]), sb("moments", [P, 5, TT])
        mean, var_eps, rstd = sb("mean", [P, TT]), sb("var_eps", [P, TT]), sb("rstd", [P, TT])
        xnt_hi, xnt_lo = (sb(n, [P, 2, KT, GT], F32R) for n in ("xnt_hi", "xnt_lo"))
        relu = sb("relu", [P, 2, GT])
        hs = sb("hs", [P, NB, GPB, KT])

        consts_in, w_in, w_split, w_hi_set = sem("consts_in"), sem("w_in"), sem("w_split"), sem("w_hi_set")
        consts_set = sem("consts_set")
        c_in, x_in = sem("c_in"), sem("x_in")
        c_hi_set, c_lo_set = sem("c_hi_set"), sem("c_lo_set")
        biased = sem("biased")
        o_mm, x2_set = sem("o_mm"), sem("x2_set")
        x2_stored = sem("x2_stored")
        stats_set, ln_chain, rstd_set, xn_set = sem("stats_set"), sem("ln_chain"), sem("rstd_set"), sem("xn_set")
        xt_mm, xt_hi_set, xt_lo_set = sem("xt_mm"), sem("xt_hi_set"), sem("xt_lo_set")
        xn_stored = [sem(f"xn_stored{r}") for r in range(2)]
        gate_mm, relu_set = sem("gate_mm"), sem("relu_set")
        hs_stored = sem("hs_stored")
        wait_taken = sem("wait_taken")
        block = ex.enter_context(nc.Block())

        def over_groups(eng, group):
            for h in range(GPB):
                group(0, h)
            with eng.Fori(1, NB - 1) as b:
                for h in range(GPB):
                    group(b, h)
            for h in range(GPB):
                group(NB - 1, h)

        def following(b, h):
            if h + 1 < GPB:
                return b, h + 1
            return (b + 1, 0) if not isinstance(b, int) or b + 1 < NB else None

        def after_next(b, h):
            nxt = following(b, h)
            return following(*nxt) if nxt else None

        @block.sync
        def _(sp):
            sp.dma_start(bo_s[:, :], bo.unsqueeze(0).broadcast_to([P, DIM])).then_inc(consts_in, 16)
            sp.dma_start(gb1_s[:, :], gb1).then_inc(consts_in, 16)

            def load_context(b, h):
                g = b * GPB + h
                wait(sp, c_lo_set, g)
                if not isinstance(b, int):
                    sp.sem_inc(wait_taken, 1)
                sp.dma_start(ctx_in[:, :, :], ctx[b, :, h * GT:(h + 1) * GT].rearrange("(t p) n -> p t n", p=P)
                             ).then_inc(c_in, 16)

            def load_x1(b, h):
                g = b * GPB + h
                wait(sp, biased, g)
                if not isinstance(b, int):
                    sp.sem_inc(wait_taken, 1)
                sp.dma_start(x1_in[:, :, :], x1[b, h * GT:(h + 1) * GT, :].rearrange("(u p) d -> p u d", p=P)
                             ).then_inc(x_in, 16)

            def stores(b, h):
                g = b * GPB + h
                sp.wait_ge(x2_set, 4 * g + 4)
                if not isinstance(b, int):
                    sp.sem_inc(wait_taken, 1)
                sp.dma_start(x2[b, h * GT:(h + 1) * GT, :].rearrange("(u p) d -> p u d", p=P), x2_s[:, :, :]
                             ).then_inc(x2_stored, 16)
                sp.wait_ge(xt_lo_set, 4 * g + 4)
                if not isinstance(b, int):
                    sp.sem_inc(wait_taken, 1)
                for part, of in ((xn_hi, xnt_hi), (xn_lo, xnt_lo)):
                    sp.dma_start(part[b, :, h * GT:(h + 1) * GT].rearrange("(t p) n -> p t n", p=P),
                                 of[:, h, :, :].bitcast(F32)).then_inc(xn_stored[h], 16)

            load_context(0, 0)
            for n, w in enumerate((wo, gw1)):
                if n:
                    load_x1(0, 0)
                    sp.wait_ge(w_split, n)
                sp.dma_start(stage[:, :, :], w.rearrange("(t p) n -> p t n", p=P)).then_inc(w_in, 16)

            load_context(*following(0, 0))

            def group(b, h):
                if after_next(b, h):
                    load_context(*after_next(b, h))
                if following(b, h):
                    load_x1(*following(b, h))
                stores(b, h)

            over_groups(sp, group)
            sp.wait_ge(relu_set, 4 * NG)
            sp.dma_start(h_sums, hs[:, :, :, :]).then_inc(hs_stored, 16)
            sp.wait_ge(hs_stored, 16)
            sp.wait_ge(x2_stored, 16 * NG)
            for r in range(2):
                sp.wait_ge(xn_stored[r], 32 * NB)

        @block.gpsimd
        def _(pool):
            pool.memset(ident[:, :], 0.0).then_inc(consts_set, 1)
            pool.memset(neghalf[:, :], -0.5).then_inc(consts_set, 1)
            pool.wait_ge(consts_set, 2)
            pool.affine_select(out=ident[:, :], in_=ident[:, :], compare_op=ALU.not_equal, fill=1.0,
                               base=0, pattern=[[-1, P]], channel_multiplier=1).then_inc(consts_set, 1)
            pool.wait_ge(consts_in, 32)

            def add_bias(g):
                pool.wait_ge(x_in, 16 * g + 16)
                wait(pool, x2_set, 4 * g)
                pool.tensor_tensor(x1_b[:, :, :], x1_in[:, :, :],
                                   bo_s[:, :].unsqueeze(1).broadcast_to([P, TT, DIM]), ALU.add).then_inc(biased, 1)

            def norm_scale(g):
                pool.wait_ge(ln_chain, 3 * g + 3)
                wait(pool, xn_set, g)
                pool.tensor_tensor(rstd[:, :], var_eps[:, :], neghalf[:, :], ALU.pow).then_inc(rstd_set, 1)

            add_bias(0)
            norm_scale(0)

            def group(b, h):
                if following(b, h):
                    add_bias(b * GPB + h + 1)
                    norm_scale(b * GPB + h + 1)

            over_groups(pool, group)

        @block.vector
        def _(dve):
            def split_context(g):
                dve.wait_ge(c_hi_set, g + 1)
                wait(dve, o_mm, 4 * g)
                dve.tensor_tensor(ctx_lo[:, :, :], ctx_in[:, :, :], ctx_hi[:, :, :].bitcast(F32), ALU.subtract
                                  ).then_inc(c_lo_set, 1)

            def residual_and_norm(g):
                wait(dve, x2_stored, 16 * g)
                dve.wait_ge(biased, g + 1)
                for u in range(TT):
                    dve.wait_ge(o_mm, 4 * g + u + 1)
                    dve.tensor_tensor(x2_s[:, u, :], bank[u][:, :], x1_b[:, u, :], ALU.add).then_inc(x2_set, 1)
                dve.wait_ge(x2_set, 4 * g + 4)
                moments_of(dve, g, x2_s, TT, DIM, stats, moments, mean, var_eps, stats_set, ln_chain)
                dve.wait_ge(rstd_set, g + 1)
                wait(dve, xt_mm, 4 * g)
                for u in range(TT):
                    i = dve.tensor_scalar(xn[:, u, :], x2_s[:, u, :], mean[:, u:u + 1], rstd[:, u:u + 1],
                                          ALU.subtract, ALU.mult)
                i.then_inc(xn_set, 1)

            def transposed_lo(g, r):
                for u in range(TT):
                    dve.wait_ge(xt_hi_set, 4 * g + u + 1)
                    dve.tensor_tensor(xnt_lo[:, r, :, u * P:(u + 1) * P],
                                      bank[6 + u % 2][:, :].rearrange("p (t n) -> p t n", t=KT),
                                      xnt_hi[:, r, :, u * P:(u + 1) * P].bitcast(F32), ALU.subtract
                                      ).then_inc(xt_lo_set, 1)

            for n in range(2):
                if n:
                    split_context(0)
                dve.wait_ge(w_in, 16 * n + 16)
                dve.tensor_copy(w_hi[n][:, :, :], stage[:, :, :]).then_inc(w_hi_set, 1)
                dve.wait_ge(w_hi_set, n + 1)
                dve.tensor_tensor(w_lo[n][:, :, :], stage[:, :, :], w_hi[n][:, :, :].bitcast(F32), ALU.subtract
                                  ).then_inc(w_split, 1)
            residual_and_norm(0)
            split_context(1)
            transposed_lo(0, 0)

            def group(b, h):
                g = b * GPB + h
                if following(b, h):
                    residual_and_norm(g + 1)
                    if after_next(b, h):
                        split_context(g + 2)
                    transposed_lo(g + 1, (h + 1) % 2)

            over_groups(dve, group)

        @block.scalar
        def _(act):
            def context_hi(g):
                act.wait_ge(c_in, 16 * g + 16)
                wait(act, o_mm, 4 * g)
                act.activation(ctx_hi[:, :, :], ctx_in[:, :, :], ACT.Copy).then_inc(c_hi_set, 1)

            def transposed_hi(b, g, r, tiles):
                for u in tiles:
                    act.wait_ge(xt_mm, 4 * g + u + 1)
                    wait(act, xn_stored[r], 32 * b)
                    act.activation(xnt_hi[:, r, :, u * P:(u + 1) * P],
                                   bank[6 + u % 2][:, :].rearrange("p (t n) -> p t n", t=KT), ACT.Copy
                                   ).then_inc(xt_hi_set, 1)

            context_hi(0)
            context_hi(1)
            transposed_hi(0, 0, 0, range(TT))
            act.wait_ge(consts_in, 32)

            def group(b, h):
                g = b * GPB + h
                nxt = following(b, h)
                if after_next(b, h):
                    context_hi(g + 2)
                for t in range(KT):
                    if t == KT - 1 and nxt:
                        transposed_hi(nxt[0], g + 1, nxt[1], range(2))
                    act.wait_ge(gate_mm, 4 * g + t + 1)
                    wait(act, relu_set, 4 * g + t - 1)
                    act.activation(relu[:, t % 2, :], bank[4 + t % 2][:, :], ACT.Relu, bias=gb1_s[:, t:t + 1],
                                   accum_out=hs[:, b, h, t:t + 1]).then_inc(relu_set, 1)
                if nxt:
                    transposed_hi(nxt[0], g + 1, nxt[1], range(2, TT))

            over_groups(act, group)

        @block.tensor
        def _(pe):
            def product(out, left, right):
                for t in range(KT):
                    for n, (a, b) in enumerate(((0, 0), (0, 1), (1, 0))):
                        i = pe.matmul(out, left(a, t), right(b, t), start=t == 0 and n == 0, stop=t == KT - 1 and n == 2)
                return i

            def project(g):
                pe.wait_ge(c_lo_set, g + 1)
                for u in range(TT):
                    wait(pe, x2_set, 4 * (g - 1) + u + 1)
                    product(bank[u][:, :], lambda a, k: (ctx_hi, ctx_lo)[a][:, k, u * P:(u + 1) * P],
                            lambda a, k: (w_hi, w_lo)[a][0][:, k, :]).then_inc(o_mm, 1)

            def transposes(g, tiles):
                pe.wait_ge(xn_set, g + 1)
                for u in tiles:
                    wait(pe, xt_lo_set, 4 * g + u - 1)
                    for t in range(KT):
                        i = pe.transpose(bank[6 + u % 2][:, t * P:(t + 1) * P], xn[:, u, t * P:(t + 1) * P],
                                         ident[:, :])
                    i.then_inc(xt_mm, 1)

            def gate(g, r, more):
                pe.wait_ge(xt_lo_set, 4 * g + 4)
                for t in range(KT):
                    if t == KT - 1 and more:
                        transposes(g + 1, range(2))
                    wait(pe, relu_set, 4 * g + t - 1)
                    product(bank[4 + t % 2][:, :], lambda a, k: (w_hi, w_lo)[a][1][:, k, t * P:(t + 1) * P],
                            lambda a, k: (xnt_hi, xnt_lo)[a][:, r, k, :]).then_inc(gate_mm, 1)

            pe.wait_ge(consts_set, 3)
            pe.wait_ge(w_split, 1)
            project(0)
            pe.wait_ge(w_split, 2)
            transposes(0, range(TT))

            def group(b, h):
                g = b * GPB + h
                if following(b, h):
                    project(g + 1)
                gate(g, h, following(b, h))
                if following(b, h):
                    transposes(g + 1, range(2, TT))

            over_groups(pe, group)


def modulate_weights(nc, h_sums, gw2, gb2, tw, base, b1, tb1, b2, tb2, mw, mb1, mb2):
    NBLK, E, _, N = tw.shape
    NB, GPB, KT = h_sums.shape[1:]
    FT = b1.shape[1]
    R = P // E
    U = P // R
    PAIRS = U // 2
    RING = 4
    ex = ExitStack()
    with ex:
        sb = lambda name, shape, dt=F32: ex.enter_context(nc.sbuf_tensor("m_" + name, shape, dt))
        sem = semaphores(nc, ex, "m_")
        bank = [ex.enter_context(nc.psum_tensor(f"m_bank{i}", [P, 512], F32)) for i in range(8)]
        hs, hsum, hmean = sb("hs", [P, NB, GPB, KT]), sb("hsum", [P, KT, NB]), sb("hmean", [P, KT, NB])
        gw2_s, gb2_s = sb("gw2", [P, KT, E]), sb("gb2", [E, 1])
        b1_s, tb1_s, b2_s, tb2_s = sb("b1", [P, FT]), sb("tb1", [E, FT * P]), sb("b2", [P, N]), sb("tb2", [E, N])
        ident, expand = sb("ident", [P, P]), sb("expand", [E, P])
        same_row = sb("same_row", [P, R])
        g_s, g_wide, g_col = sb("g", [E, NB]), sb("g_wide", [E, NB, P]), sb("g_col", [P, NB])
        gates = sb("gates", [P, NB, R])
        pick = sb("pick", [P, PAIRS, 2, NB, R])
        mb1_s, mb2_s = sb("mb1", [P, NB, FT]), sb("mb2", [P, NB, N])
        tw_in = sb("tw_in", [P, RING, U, N])
        base_in = sb("base_in", [P, RING, N])
        made = sb("made", [P, 2, PAIRS, N])

        consts_in, consts_set = sem("consts_in"), sem("consts_set")
        g_mm, g_set = sem("g_mm"), sem("g_set")
        picks_set = sem("picks_set")
        bias_mm, bias_set, bias_stored = sem("bias_mm"), sem("bias_set"), sem("bias_stored")
        tw_loaded = [sem(f"tw_loaded{r}") for r in range(RING)]
        made_mm = sem("made_mm")
        act_copied, dve_copied = sem("act_copied"), sem("dve_copied")
        stored = [sem(f"stored{r}") for r in range(2)]
        wait_taken, wait_taken_act = sem("wait_taken"), sem("wait_taken_act")
        block = ex.enter_context(nc.Block())
        HALF = PAIRS // 2
        CONSTS = 7

        @block.sync
        def _(sp):
            sp.dma_start(hs[:, :, :, :], h_sums).then_inc(consts_in, 16)
            sp.dma_start(gw2_s[:, :, :], gw2.rearrange("(t p) e -> p t e", p=P)).then_inc(consts_in, 16)
            sp.dma_start(gb2_s[:, :], gb2).then_inc(consts_in, 16)
            sp.dma_start(b1_s[:, :], b1).then_inc(consts_in, 16)
            sp.dma_start(tb1_s[:, :], tb1).then_inc(consts_in, 16)
            sp.dma_start(b2_s[:, :], b2.unsqueeze(0).broadcast_to([P, N])).then_inc(consts_in, 16)
            sp.dma_start(tb2_s[:, :], tb2).then_inc(consts_in, 16)

            def load(c, r):
                wait(sp, made_mm, PAIRS * (c - RING + 1))
                if not isinstance(c, int):
                    sp.sem_inc(wait_taken, 1)
                sp.dma_start(tw_in[:, r, :, :], tw[c, :, :, :].rearrange("e (r u) n -> (e r) u n", u=U)
                             ).then_inc(tw_loaded[r], 16)
                sp.dma_start(base_in[:, r, :], base[c, :, :]).then_inc(tw_loaded[r], 16)

            for c in range(RING):
                load(c, c)
            with sp.Fori(1, NBLK // RING) as t:
                for r in range(RING):
                    load(t * RING + r, r)
            for c in range(NBLK // RING * RING, NBLK):
                load(c, c % RING)
            sp.wait_ge(bias_set, 1 + NB)
            sp.dma_start(mb1, mb1_s[:, :, :]).then_inc(bias_stored, 16)
            sp.dma_start(mb2.rearrange("b p n -> p b n"), mb2_s[:, :, :]).then_inc(bias_stored, 16)
            sp.wait_ge(bias_stored, 32)
            for r in range(2):
                sp.wait_ge(stored[r], 32 * (NBLK // 2))

        @block.gpsimd
        def _(pool):
            pool.memset(ident[:, :], 0.0).then_inc(consts_set, 1)
            pool.memset(expand[:, :], 1.0).then_inc(consts_set, 1)
            pool.wait_ge(consts_set, 2)
            pool.affine_select(out=ident[:, :], in_=ident[:, :], compare_op=ALU.not_equal, fill=1.0,
                               base=0, pattern=[[-1, P]], channel_multiplier=1).then_inc(consts_set, 1)
            pool.affine_select(out=expand[:, :], in_=expand[:, :], compare_op=ALU.is_ge, fill=0.0,
                               base=0, pattern=[[1, P]], channel_multiplier=-R).then_inc(consts_set, 1)
            pool.wait_ge(consts_set, 4)
            pool.affine_select(out=expand[:, :], in_=expand[:, :], compare_op=ALU.is_ge, fill=0.0,
                               base=R - 1, pattern=[[-1, P]], channel_multiplier=R).then_inc(consts_set, 1)

        @block.vector
        def _(dve):
            dve.wait_ge(consts_set, 5)
            dve.tensor_reduce(same_row[:, :], ident[:, :].rearrange("p (e r) -> p r e", r=R), AX.X, ALU.add
                              ).then_inc(g_set, 1)
            dve.wait_ge(consts_in, 16 * CONSTS)
            dve.tensor_reduce(hsum[:, :, :], hs[:, :, :, :].rearrange("p b h t -> p t b h"), AX.X, ALU.add
                              ).then_inc(g_set, 1)
            dve.wait_ge(g_set, 2)
            dve.tensor_scalar(hmean[:, :, :], hsum[:, :, :], 1.0 / (GPB * 512), None, ALU.mult).then_inc(g_set, 1)
            for j in range(PAIRS):
                for a in range(2):
                    i = dve.tensor_copy(pick[:, j, a, :, :],
                                        ident[:, :].rearrange("p (r u) -> p u r", u=U)[:, 2 * j + a, :]
                                        .unsqueeze(1).broadcast_to([P, NB, R]))
            i.then_inc(picks_set, 1)
            dve.wait_ge(g_mm, 1)
            dve.tensor_scalar(g_s[:, :], bank[0][:E, :NB], gb2_s[:, :], None, ALU.add).then_inc(g_set, 1)
            dve.wait_ge(g_set, 4)
            dve.tensor_copy(g_wide[:, :, :], g_s[:, :].unsqueeze(2).broadcast_to([E, NB, P])).then_inc(g_set, 1)
            dve.wait_ge(g_mm, 2)
            dve.tensor_copy(g_col[:, :], bank[1][:, :NB]).then_inc(g_set, 1)
            dve.wait_ge(g_set, 6)
            dve.tensor_tensor(gates[:, :, :], same_row[:, :].unsqueeze(1).broadcast_to([P, NB, R]),
                              g_col[:, :].unsqueeze(2).broadcast_to([P, NB, R]), ALU.mult).then_inc(g_set, 1)
            dve.wait_ge(bias_mm, 1)
            dve.tensor_tensor(mb1_s[:, :, :], bank[2][:, :NB * FT].rearrange("p (f b) -> p b f", b=NB),
                              b1_s[:, :].unsqueeze(1).broadcast_to([P, NB, FT]), ALU.add).then_inc(bias_set, 1)
            for b in range(NB):
                dve.wait_ge(bias_mm, 2 + b)
                dve.tensor_tensor(mb2_s[:, b, :], bank[3 + b][:, :], b2_s[:, :], ALU.add).then_inc(bias_set, 1)

            def copies(c, k, r):
                wait(dve, stored[r], 32 * k)
                for j in range(1, PAIRS, 2):
                    dve.wait_ge(made_mm, PAIRS * c + j + 1)
                    dve.tensor_copy(made[:, r, j, :], bank[PAIRS * r + j][:, :]).then_inc(dve_copied, 1)

            for r in range(2):
                copies(r, 0, r)
            with dve.Fori(1, NBLK // 2) as t:
                for r in range(2):
                    copies(t * 2 + r, t, r)

        @block.scalar
        def _(act):
            def copies(c, k, r):
                wait(act, stored[r], 32 * k)
                for j in range(0, PAIRS, 2):
                    act.wait_ge(made_mm, PAIRS * c + j + 1)
                    act.activation(made[:, r, j, :], bank[PAIRS * r + j][:, :], ACT.Copy).then_inc(act_copied, 1)
                act.wait_ge(dve_copied, HALF * c + HALF)
                if not isinstance(c, int):
                    act.sem_inc(wait_taken_act, 1)
                act.wait_ge(act_copied, HALF * c + HALF)
                if not isinstance(c, int):
                    act.sem_inc(wait_taken_act, 1)
                for a in range(2):
                    act.dma_start(mw[c, :, :, :].rearrange("b (r j a) n -> a (b r) j n", a=2, j=PAIRS)[a],
                                  made[a * NB * R:(a + 1) * NB * R, r, :, :]).then_inc(stored[r], 16)

            for r in range(2):
                copies(r, 0, r)
            with act.Fori(1, NBLK // 2) as t:
                for r in range(2):
                    copies(t * 2 + r, t, r)

        @block.tensor
        def _(pe):
            pe.wait_ge(g_set, 3)
            for t in range(KT):
                i = pe.matmul(bank[0][:E, :NB], gw2_s[:, t, :], hmean[:, t, :], start=t == 0, stop=t == KT - 1)
            i.then_inc(g_mm, 1)
            pe.wait_ge(g_set, 4)
            pe.matmul(bank[1][:, :NB], expand[:, :], g_s[:, :], start=True, stop=True).then_inc(g_mm, 1)
            for f in range(FT):
                i = pe.matmul(bank[2][:, f * NB:(f + 1) * NB], tb1_s[:, f * P:(f + 1) * P], g_s[:, :],
                              start=True, stop=True)
            i.then_inc(bias_mm, 1)
            pe.wait_ge(g_set, 5)
            for b in range(NB):
                pe.matmul(bank[3 + b][:, :], g_wide[:, b, :], tb2_s[:, :], start=True, stop=True).then_inc(bias_mm, 1)
            pe.wait_ge(g_set, 7)
            pe.wait_ge(bias_set, 1 + NB)
            pe.wait_ge(picks_set, 1)

            def products(c, k, rt, r):
                pe.wait_ge(tw_loaded[rt], 32 * k + 32)
                for j in range(PAIRS):
                    if j % 2:
                        wait(pe, dve_copied, HALF * (c - 2) + j // 2 + 1)
                    else:
                        wait(pe, act_copied, HALF * (c - 2) + j // 2 + 1)
                    out = bank[PAIRS * r + j]
                    pe.matmul(out[:, :], pick[:, j, :, :, :].rearrange("p a b r -> p (a b r)"), base_in[:, rt, :],
                              start=True, stop=False)
                    for a in range(2):
                        rows = slice(a * NB * R, (a + 1) * NB * R)
                        i = pe.matmul(out[rows, :], gates[:, :, :].rearrange("p b r -> p (b r)"),
                                      tw_in[:, rt, 2 * j + a, :], start=False, stop=True)
                    i.then_inc(made_mm, 1)

            BODY = 2 * RING
            for c in range(BODY):
                products(c, c // RING, c % RING, c % 2)
            with pe.Fori(1, NBLK // BODY) as t:
                for c in range(BODY):
                    products(t * BODY + c, t * 2 + c // RING, c % RING, c % 2)
            for c in range(NBLK // BODY * BODY, NBLK):
                products(c, c // RING, c % RING, c % 2)


def feed_forward(nc, xn_hi, xn_lo, x2, mw, mb1, mb2, out):
    NB, DIM, S = xn_hi.shape
    NBLK = mw.shape[0]
    GT = 512
    GPB = S // GT
    KT = DIM // P
    TT = GT // P
    FT = NBLK // 2
    FG = FT // KT
    STEPS = GPB * FT
    ex = ExitStack()
    with ex:
        sb = lambda name, shape, dt=F32: ex.enter_context(nc.sbuf_tensor("f_" + name, shape, dt))
        sem = semaphores(nc, ex, "f_")
        bank = [ex.enter_context(nc.psum_tensor(f"f_bank{i}", [P, 512], F32)) for i in range(8)]
        w_hi, w_lo = sb("w_hi", [P, NBLK, 512], F32R), sb("w_lo", [P, NBLK, 512], F32R)
        stage = sb("stage", [P, 2, 2, 512])
        x_hi, x_lo = sb("x_hi", [P, GPB, KT, GT], F32R), sb("x_lo", [P, GPB, KT, GT], F32R)
        mb1_s, mb2_s = sb("mb1", [P, NB, FT]), sb("mb2", [P, NB, DIM])
        u, u_hi, u_lo = sb("u", [P, 2, GT]), sb("u_hi", [P, 2, GT], F32R), sb("u_lo", [P, 2, GT], F32R)
        x2_s, out_s = sb("x2_s", [P, TT, DIM]), sb("out_s", [P, TT, DIM])

        mb1_in, mb2_in = sem("mb1_in"), sem("mb2_in")
        staged = [sem(f"staged{r}") for r in range(2)]
        w_hi_set, w_set = sem("w_hi_set"), sem("w_set")
        x_in = [sem(f"x_in{h}") for h in range(GPB)]
        x2_in = sem("x2_in")
        x2_biased = sem("x2_biased")
        u_mm, u_set, u_hi_set, u_lo_set = sem("u_mm"), sem("u_set"), sem("u_hi_set"), sem("u_lo_set")
        o_mm = sem("o_mm")
        out_set = sem("out_set")
        out_stored = sem("out_stored")
        wait_taken, wait_taken_act, wait_taken_pool = sem("wait_taken"), sem("wait_taken_act"), sem("wait_taken_pool")
        block = ex.enter_context(nc.Block())

        def over_batches(eng, batch):
            batch(0)
            with eng.Fori(1, NB - 1) as b:
                batch(b)
            batch(NB - 1)

        def more(b):
            return not isinstance(b, int) or b + 1 < NB

        @block.sync
        def _(sp):
            def taken(b):
                if not isinstance(b, int):
                    sp.sem_inc(wait_taken, 1)

            def load_unit(b, fg, k):
                wait(sp, w_set, FT * b + KT * fg + k - 1)
                taken(b)
                first = 2 * (KT * fg + k)
                sp.dma_start(stage[:, k % 2, :, :], mw[first:first + 2, b, :, :].rearrange("a p n -> p a n")
                             ).then_inc(staged[k % 2], 16)

            def load_x(b, h):
                wait(sp, u_mm, STEPS * (b - 1) + FT * (h + 1))
                taken(b)
                for part, to in ((xn_hi, x_hi), (xn_lo, x_lo)):
                    sp.dma_start(to[:, h, :, :].bitcast(F32),
                                 part[b, :, h * GT:(h + 1) * GT].rearrange("(t p) n -> p t n", p=P)
                                 ).then_inc(x_in[h], 16)

            def load_x2(b, h):
                wait(sp, out_set, TT * (GPB * b + h))
                taken(b)
                sp.dma_start(x2_s[:, :, :], x2[b, h * GT:(h + 1) * GT, :].rearrange("(u p) d -> p u d", p=P)
                             ).then_inc(x2_in, 16)

            def store(b, h):
                sp.wait_ge(out_set, TT * (GPB * b + h) + TT)
                taken(b)
                sp.dma_start(out[b, h * GT:(h + 1) * GT, :].rearrange("(u p) d -> p u d", p=P), out_s[:, :, :]
                             ).then_inc(out_stored, 16)

            for fg in range(FG - 1):
                for k in range(KT):
                    load_unit(0, fg, k)
                    if (fg, k) == (0, 1):
                        load_x(0, 0)
                        sp.dma_start(mb1_s[:, :, :], mb1).then_inc(mb1_in, 16)
                    if (fg, k) == (0, 3):
                        sp.dma_start(mb2_s[:, :, :], mb2.rearrange("b p n -> p b n")).then_inc(mb2_in, 16)
            for k in range(2):
                load_unit(0, FG - 1, k)

            def batch(b):
                for k in range(2, KT):
                    load_unit(b, FG - 1, k)
                for h in range(GPB):
                    if h + 1 < GPB:
                        load_x(b, h + 1)
                    load_x2(b, h)
                    if h + 1 == GPB and more(b):
                        load_x(b + 1, 0)
                        for fg in range(FG - 1):
                            for k in range(KT):
                                load_unit(b + 1, fg, k)
                        for k in range(2):
                            load_unit(b + 1, FG - 1, k)
                    store(b, h)

            over_batches(sp, batch)
            sp.wait_ge(out_stored, 16 * NB * GPB)

        @block.gpsimd
        def _(pool):
            pool.wait_ge(mb2_in, 16)

            def batch(b):
                for h in range(GPB):
                    pool.wait_ge(x2_in, 16 * (GPB * b + h) + 16)
                    pool.sem_inc(wait_taken_pool, 1)
                    pool.tensor_tensor(x2_s[:, :, :], x2_s[:, :, :],
                                       mb2_s[:, b, :].unsqueeze(1).broadcast_to([P, TT, DIM]), ALU.add
                                       ).then_inc(x2_biased, 1)

            over_batches(pool, batch)

        @block.vector
        def _(dve):
            def split_unit(b, fg, k):
                n = FT * b + KT * fg + k
                dve.wait_ge(staged[k % 2], 16 * (FT // 2 * b + KT // 2 * fg + k // 2) + 16)
                wait(dve, o_mm, TT * (STEPS * b - FT + KT * fg + KT))
                part = slice(2 * (KT * fg + k), 2 * (KT * fg + k) + 2)
                dve.tensor_copy(w_hi[:, part, :], stage[:, k % 2, :, :]).then_inc(w_hi_set, 1)
                dve.wait_ge(w_hi_set, n + 1)
                dve.tensor_tensor(w_lo[:, part, :], stage[:, k % 2, :, :], w_hi[:, part, :].bitcast(F32),
                                  ALU.subtract).then_inc(w_set, 1)

            def split_hidden(b, c):
                s = STEPS * b + c
                dve.wait_ge(u_hi_set, s + 1)
                dve.tensor_tensor(u_lo[:, c % 2, :], u[:, c % 2, :], u_hi[:, c % 2, :].bitcast(F32), ALU.subtract
                                  ).then_inc(u_lo_set, 1)

            def finish(b, h):
                g = GPB * b + h
                dve.wait_ge(x2_biased, g + 1)
                wait(dve, out_stored, 16 * g)
                for t in range(TT):
                    dve.wait_ge(o_mm, TT * (FT * g + FT - 1) + t + 1)
                    dve.tensor_tensor(out_s[:, t, :], bank[t][:, :], x2_s[:, t, :], ALU.add).then_inc(out_set, 1)

            for k in range(KT):
                split_unit(0, 0, k)

            def batch(b):
                for c in range(STEPS):
                    h, ft = divmod(c, FT)
                    split_hidden(b, c)
                    if ft == 0 and h:
                        finish(b, h - 1)
                    elif ft == 0 and (not isinstance(b, int) or b):
                        finish(b - 1, GPB - 1)
                    if h == 0 and isinstance(b, int) and b == 0:
                        if ft < FT - KT:
                            split_unit(0, 1 + ft // KT, ft % KT)
                    elif h == 0 and ft < KT:
                        split_unit(b, FG - 1, ft)
                    if h == GPB - 1 and ft >= KT and more(b):
                        split_unit(b + 1, ft // KT - 1, ft % KT)

            over_batches(dve, batch)
            finish(NB - 1, GPB - 1)

        @block.scalar
        def _(act):
            act.wait_ge(mb1_in, 16)

            def batch(b):
                for c in range(STEPS):
                    s, ft = STEPS * b + c, c % FT
                    act.wait_ge(u_mm, s + 1)
                    wait(act, u_lo_set, s - 1)
                    act.sem_inc(wait_taken_act, 1)
                    act.activation(u[:, c % 2, :], bank[4 + c % 4][:, :], ACT.Gelu_apprx_tanh,
                                   bias=mb1_s[:, b, ft:ft + 1]).then_inc(u_set, 1)
                    act.wait_ge(u_set, s + 1)
                    wait(act, o_mm, TT * (s - 1))
                    act.activation(u_hi[:, c % 2, :], u[:, c % 2, :], ACT.Copy).then_inc(u_hi_set, 1)

            over_batches(act, batch)

        @block.tensor
        def _(pe):
            PARTS = ((0, 0), (0, 1), (1, 0))

            def hidden(b, c):
                s = STEPS * b + c
                h, ft = divmod(c, FT)
                if ft == 0:
                    pe.wait_ge(x_in[h], 32 * b + 32)
                if h == 0 and ft % KT == 0:
                    pe.wait_ge(w_set, FT * b + ft + KT)
                wait(pe, u_set, s - 3)
                for k in range(KT):
                    for n, (wp, xp) in enumerate(PARTS):
                        i = pe.matmul(bank[4 + c % 4][:, :],
                                      (w_hi, w_lo)[wp][:, 2 * (ft // KT * KT + k), ft % KT * P:(ft % KT + 1) * P],
                                      (x_hi, x_lo)[xp][:, h, k, :], start=k == 0 and n == 0, stop=k == KT - 1 and n == 2)
                i.then_inc(u_mm, 1)

            def output(b, c):
                s = STEPS * b + c
                ft = c % FT
                pe.wait_ge(u_lo_set, s + 1)
                for t in range(TT):
                    if ft == 0:
                        wait(pe, out_set, TT * (GPB * b + c // FT - 1) + t + 1)
                    for n, (up, wp) in enumerate(PARTS):
                        i = pe.matmul(bank[t][:, :], (u_hi, u_lo)[up][:, c % 2, t * P:(t + 1) * P],
                                      (w_hi, w_lo)[wp][:, 2 * ft + 1, :], start=ft == 0 and n == 0,
                                      stop=ft == FT - 1 and n == 2)
                    i.then_inc(o_mm, 1)

            hidden(0, 0)

            def batch(b):
                for c in range(STEPS):
                    if c + 1 < STEPS:
                        hidden(b, c + 1)
                    elif more(b):
                        hidden(b + 1, 0)
                    output(b, c)

            over_batches(pe, batch)


def decoder_layer(nc, x, ctx_t, mask, wq, wk, wv, wlb, wo, w0, xwq, xwk, xwv, bq, bk, bv, xwo, bo, gw1, gb1, gw2, gb2,
                  tw, base, b1, tb1, b2, tb2, out):
    NB, S, DIM = x.shape
    dram = lambda name, *shape: nc.dram_tensor(name, shape, F32).ap()
    x1 = dram("x1", NB, S, DIM)
    o_t = dram("o_t", wo.shape[0] // P, P, S // CH, NB * CH)
    scan_attention(nc, x, wq, wk, wv, wlb, w0, o_t)
    scan_projection(nc, o_t, x, wo, x1)
    q_hi, q_lo, k_hi, k_lo = (dram(n, NB, DIM, S) for n in ("q_hi", "q_lo", "k_hi", "k_lo"))
    v = dram("v", NB, S, DIM)
    cross_projections(nc, x1, ctx_t, mask, xwq, xwk, xwv, bq, bk, bv, q_hi, q_lo, k_hi, k_lo, v)
    attended = dram("attended", NB, DIM, S)
    cross_attention(nc, q_hi, q_lo, k_hi, k_lo, v, mask, dram("m_rows", 2, 4, S), attended)
    x2 = dram("x2", NB, S, DIM)
    xn_hi, xn_lo, h_sums = dram("xn_hi", NB, DIM, S), dram("xn_lo", NB, DIM, S), dram("h_sums", P, NB, 2, DIM // P)
    output_projection_and_gate(nc, attended, x1, xwo, bo, gw1, gb1, x2, xn_hi, xn_lo, h_sums)
    mw, mb1, mb2 = dram("mw", tw.shape[0], NB, P, DIM), dram("mb1", P, NB, b1.shape[1]), dram("mb2", NB, P, DIM)
    modulate_weights(nc, h_sums, gw2, gb2, tw, base, b1, tb1, b2, tb2, mw, mb1, mb2)
    feed_forward(nc, xn_hi, xn_lo, x2, mw, mb1, mb2, out)


def _layouts(i):
    import numpy as np

    a = {k: np.asarray(v) for k, v in i.items()}
    t = lambda name: a[name].T
    columns = lambda name: a[name].reshape(-1, P).T

    def by_blocks(w1, w2):
        e, f, h = w1.shape
        parts, units = f // 512, h // P
        b1 = w1.reshape(e, parts, 512, units, P).transpose(1, 3, 0, 4, 2)
        b2 = w2.reshape(e, h, parts, units, P).transpose(2, 3, 0, 4, 1)
        return np.stack([b1, b2], 2).reshape(parts * units * 2, e, P, 512)

    w_in, w_out = a["L0_attn_W_in_init"][0], a["L0_attn_W_out_init"][0]
    heads, d = w_in.shape[1], w_in.shape[0]
    w0 = np.stack([w_in.transpose(1, 2, 0), w_out.transpose(1, 2, 0), w_out.transpose(1, 0, 2)])
    return {
        "x": a["x"], "ctx_t": a["ctx_1024"].transpose(0, 2, 1), "mask": a["mask_BxS2_if1"],
        "wq": t("L0_attn_Wq"), "wk": t("L0_attn_Wk"), "wv": t("L0_attn_Wv"),
        "wlb": np.concatenate([a["L0_attn_Wlr"], a["L0_attn_Wbeta"]], 0).T, "wo": t("L0_attn_Wo"),
        "w0": w0.reshape(3, heads // 2, 2, d, d).transpose(0, 2, 3, 1, 4).reshape(3, 2 * d, heads // 2, d),
        "xwq": t("L0_xattn_W_q"), "xwk": t("L0_xattn_W_k"), "xwv": t("L0_xattn_W_v"),
        "bq": columns("L0_xattn_b_q"), "bk": columns("L0_xattn_b_k"), "bv": a["L0_xattn_b_v"],
        "xwo": t("L0_xattn_W_o"), "bo": a["L0_xattn_b_o"],
        "gw1": t("L0_ffn_gate_w1"), "gb1": columns("L0_ffn_gate_b1"),
        "gw2": t("L0_ffn_gate_w2"), "gb2": a["L0_ffn_gate_b2"].reshape(-1, 1),
        "tw": by_blocks(a["L0_ffn_TW1"], a["L0_ffn_TW2"]),
        "base": by_blocks(a["L0_ffn_W1"][None], a["L0_ffn_W2"][None])[:, 0],
        "b1": columns("L0_ffn_b1"), "tb1": a["L0_ffn_Tb1"], "b2": a["L0_ffn_b2"], "tb2": a["L0_ffn_Tb2"],
    }


def kernel(**inputs):
    import numpy as _np
    import concourse.bacc as _bacc
    from concourse import mybir as _mybir
    from concourse.bass_utils import run_bass_kernel_spmd as _run

    nc = _bacc.Bacc("TRN2", target_bir_lowering=False, num_devices=1)
    arrays, args = {}, []
    for name, a in _layouts(inputs).items():
        a = _np.ascontiguousarray(a)
        arrays[f"in_{name}"] = a
        args.append(nc.dram_tensor(f"in_{name}", a.shape, _mybir.dt.from_np(a.dtype), kind="ExternalInput").ap())
    shape = inputs["x"].shape
    args.append(nc.dram_tensor("out", shape, F32, kind="ExternalOutput").ap())
    decoder_layer(nc, *args)
    r = _run(nc, [arrays], core_ids=[0])
    return r.results[0]["out"]
```
